# Optimizing a Trainium2 kernel written in Bass

```python
import numpy as np
import jax
import jax.numpy as jnp

def _softmax(x, axis=-1):
    return jax.nn.softmax(x, axis=axis)

def _gelu(x):
    return jax.nn.gelu(x, approximate=True)

def _silu(x):
    return jax.nn.silu(x)

def _sigmoid(x):
    return jax.nn.sigmoid(x)

def _layernorm(x, axis=-1, eps=1e-05):
    m = jnp.mean(x, axis=axis, keepdims=True)
    v = jnp.var(x, axis=axis, keepdims=True)
    return (x - m) / jnp.sqrt(v + eps)

def _scatter_add(tgt, idx, src, axis=0):
    return tgt.at[idx].add(src)

def _segment_sum(src, seg, n):
    return jax.ops.segment_sum(src, seg, n)
kernel_name = 'mk_audio_tower_d2_tok_audfeat512_r4_a16ca2'

def setup_inputs(seed: int=0):
    np.random.seed(seed)
    _w = jnp.asarray

    def _rec_inputs():
        import jax
        import jax.numpy as jnp
        _rk = jax.random.key(seed)
        x = -0.000125008 + 0.999885 * jax.random.normal(jax.random.fold_in(_rk, 1), (8, 64, 750), jnp.float32)
        return x
    x = _rec_inputs()

    def _L0_tok_setup():
        import jax, jax.numpy as jnp
        import numpy as np
        from jax import lax
        STRIDE = 1
        PADDING = 4
        key = jax.random.key(seed)
        k1, k2, k3 = jax.random.split(key, 3)
        B, C_IN, L = (32, 64, 1024)
        C_OUT, K = (128, 9)
        x = jax.random.normal(k1, (B, C_IN, L), dtype=jnp.float32)
        weight = jax.random.normal(k2, (C_OUT, C_IN, K), dtype=jnp.float32)
        bias = jax.random.normal(k3, (C_OUT,), dtype=jnp.float32)
        return {'x': x, 'weight': weight, 'bias': bias}
    _L0_tok_all = _L0_tok_setup()
    _L0_tok_in = {k: v for k, v in _L0_tok_all.items() if k in ('weight', 'bias')}
    del _L0_tok_all

    def _L0_attn_setup():
        import jax, jax.numpy as jnp
        import numpy as np
        EPS = 1.1920929e-07

        def _rmsnorm(x, g):
            inv = jax.lax.rsqrt(jnp.mean(x * x, axis=-1, keepdims=True) + EPS)
            return x * inv * g
        key = jax.random.key(seed)
        k1, k2, k3 = jax.random.split(key, 3)
        B, T, C, H = (4, 512, 128, 8)
        D = C // H
        x = jax.random.normal(k1, (B, T, C), dtype=jnp.float32)
        delta_w = jax.random.normal(k2, (C, C), dtype=jnp.float32) * 0.02
        qkv_w = jax.random.normal(k3, (C, C), dtype=jnp.float32) * 0.02
        g1 = jnp.ones((D,), dtype=jnp.float32)
        g2 = jnp.ones((D,), dtype=jnp.float32)
        g3 = jnp.ones((D,), dtype=jnp.float32)
        return {'x': x, 'delta_w': delta_w, 'qkv_w': qkv_w, 'g1': g1, 'g2': g2, 'g3': g3}
    _L0_attn_all = _L0_attn_setup()
    _L0_attn_in = {k: v for k, v in _L0_attn_all.items() if k in ('delta_w', 'qkv_w', 'g1', 'g2', 'g3')}
    del _L0_attn_all

    def _L0_ffn_setup():
        import jax, jax.numpy as jnp
        import numpy as np
        B, S, D, E, O = (256, 64, 128, 16, 128)
        key = jax.random.key(seed)
        k_x, k_wg, k_bg, k_we, k_be = jax.random.split(key, 5)
        scale_g = 1.0 / np.sqrt(D)
        scale_e = 1.0 / np.sqrt(D)
        return {'x': jax.random.normal(k_x, (B, S, D), dtype=jnp.float32), 'Wg': jax.random.uniform(k_wg, (D, E), jnp.float32, -scale_g, scale_g), 'bg': jax.random.uniform(k_bg, (E,), jnp.float32, -scale_g, scale_g), 'We': jax.random.uniform(k_we, (E, D, O), jnp.float32, -scale_e, scale_e), 'be': jax.random.uniform(k_be, (E, O), jnp.float32, -scale_e, scale_e)}
    _L0_ffn_all = _L0_ffn_setup()
    _L0_ffn_in = {k: v for k, v in _L0_ffn_all.items() if k in ('Wg', 'bg', 'We', 'be')}
    del _L0_ffn_all

    def _L1_attn_setup():
        import jax, jax.numpy as jnp
        import numpy as np
        H = 8
        EPS = 1e-05

        def _delta_net(x, Wq, Wk, Wv, Wb, Wo, ln_g, ln_b):
            B, L, D = x.shape
            dh = D // H

            def heads(W):
                return (x @ W).reshape(B, L, H, dh)
            q = heads(Wq)
            k = heads(Wk)
            v = heads(Wv)
            beta = jax.nn.sigmoid(heads(Wb))
            q = q / jnp.linalg.norm(q, axis=-1, keepdims=True)
            k = k / jnp.linalg.norm(k, axis=-1, keepdims=True)
            qs, ks_, vs, bs = (jnp.moveaxis(t, 1, 0) for t in (q, k, v, beta))
            S0 = jnp.zeros((B, H, dh, dh), x.dtype)

            def step(S, inp):
                qt, kt, vt, bt = inp
                pred = jnp.einsum('bhk,bhkv->bhv', kt, S)
                S = S + jnp.einsum('bhk,bhv->bhkv', kt, bt * (vt - pred))
                o = jnp.einsum('bhk,bhkv->bhv', qt, S)
                return (S, o)
            final_state, ys = jax.lax.scan(step, S0, (qs, ks_, vs, bs))
            y = jnp.moveaxis(ys, 0, 1).reshape(B, L, D)
            mu = jnp.mean(y, axis=-1, keepdims=True)
            var = jnp.var(y, axis=-1, keepdims=True)
            yn = (y - mu) * jax.lax.rsqrt(var + EPS) * ln_g + ln_b
            return (yn @ Wo, final_state)

        def _reference_tuple_inner(x, Wq, Wk, Wv, Wb, Wo, ln_g, ln_b):
            return _delta_net(x, Wq, Wk, Wv, Wb, Wo, ln_g, ln_b)
        key = jax.random.key(seed)
        ks = jax.random.split(key, 6)
        B, L, D = (2, 1024, 128)
        s = 1.0 / np.sqrt(D).astype(np.float32)
        x = jax.random.normal(ks[0], (B, L, D), jnp.float32)
        Wq = jax.random.normal(ks[1], (D, D), jnp.float32) * s
        Wk = jax.random.normal(ks[2], (D, D), jnp.float32) * s
        Wv = jax.random.normal(ks[3], (D, D), jnp.float32) * s
        Wb = jax.random.normal(ks[4], (D, D), jnp.float32) * s
        Wo = jax.random.normal(ks[5], (D, D), jnp.float32) * s
        ln_g = jnp.ones((D,), jnp.float32)
        ln_b = jnp.zeros((D,), jnp.float32)
        return dict(x=x, Wq=Wq, Wk=Wk, Wv=Wv, Wb=Wb, Wo=Wo, ln_g=ln_g, ln_b=ln_b)
    _L1_attn_all = _L1_attn_setup()
    _L1_attn_in = {k: v for k, v in _L1_attn_all.items() if k in ('Wq', 'Wk', 'Wv', 'Wb', 'Wo', 'ln_g', 'ln_b')}
    del _L1_attn_all

    def _L1_ffn_setup():
        import jax, jax.numpy as jnp
        import numpy as np
        D_MODEL = 128
        D_FF = 512
        N_EXPERTS = 64
        K_ACTIVE = 2
        N_HASHES = 4
        LAYER_ID = 0
        SALT = 0.0
        BUCKET_SCALE = 8.0
        CAPACITY_FACTOR = 1.25
        key = jax.random.key(seed)
        k0, k1, k2, k3 = jax.random.split(key, 4)
        B, S = (4, 512)
        hidden_states = jax.random.normal(k0, (B, S, D_MODEL), dtype=jnp.float32)
        W_hash = jax.random.normal(k1, (N_HASHES, D_MODEL), dtype=jnp.float32) / np.float32(np.sqrt(D_MODEL))
        W1 = jax.random.normal(k2, (N_EXPERTS, D_MODEL, D_FF), dtype=jnp.float32) * np.float32(1.0 / np.sqrt(D_MODEL))
        b1 = jnp.zeros((N_EXPERTS, D_FF), dtype=jnp.float32)
        W2 = jax.random.normal(k3, (N_EXPERTS, D_FF, D_MODEL), dtype=jnp.float32) * np.float32(1.0 / np.sqrt(D_FF))
        b2 = jnp.zeros((N_EXPERTS, D_MODEL), dtype=jnp.float32)
        return {'hidden_states': hidden_states, 'W_hash': W_hash, 'W1': W1, 'b1': b1, 'W2': W2, 'b2': b2}
    _L1_ffn_all = _L1_ffn_setup()
    _L1_ffn_in = {k: v for k, v in _L1_ffn_all.items() if k in ('W_hash', 'W1', 'b1', 'W2', 'b2')}
    del _L1_ffn_all
    return {'x': x, 'L0_tok_weight': _L0_tok_in['weight'], 'L0_tok_bias': _L0_tok_in['bias'], 'L0_attn_delta_w': _L0_attn_in['delta_w'], 'L0_attn_qkv_w': _L0_attn_in['qkv_w'], 'L0_attn_g1': _L0_attn_in['g1'], 'L0_attn_g2': _L0_attn_in['g2'], 'L0_attn_g3': _L0_attn_in['g3'], 'L0_ffn_Wg': _L0_ffn_in['Wg'], 'L0_ffn_bg': _L0_ffn_in['bg'], 'L0_ffn_We': _L0_ffn_in['We'], 'L0_ffn_be': _L0_ffn_in['be'], 'L1_attn_Wq': _L1_attn_in['Wq'], 'L1_attn_Wk': _L1_attn_in['Wk'], 'L1_attn_Wv': _L1_attn_in['Wv'], 'L1_attn_Wb': _L1_attn_in['Wb'], 'L1_attn_Wo': _L1_attn_in['Wo'], 'L1_attn_ln_g': _L1_attn_in['ln_g'], 'L1_attn_ln_b': _L1_attn_in['ln_b'], 'L1_ffn_W_hash': _L1_ffn_in['W_hash'], 'L1_ffn_W1': _L1_ffn_in['W1'], 'L1_ffn_b1': _L1_ffn_in['b1'], 'L1_ffn_W2': _L1_ffn_in['W2'], 'L1_ffn_b2': _L1_ffn_in['b2']}

def reference(x, L0_tok_weight, L0_tok_bias, L0_attn_delta_w, L0_attn_qkv_w, L0_attn_g1, L0_attn_g2, L0_attn_g3, L0_ffn_Wg, L0_ffn_bg, L0_ffn_We, L0_ffn_be, L1_attn_Wq, L1_attn_Wk, L1_attn_Wv, L1_attn_Wb, L1_attn_Wo, L1_attn_ln_g, L1_attn_ln_b, L1_ffn_W_hash, L1_ffn_W1, L1_ffn_b1, L1_ffn_W2, L1_ffn_b2):
    import jax
    import jax.numpy as jnp

    def _L0_tok_ref(x, weight, bias):
        import jax, jax.numpy as jnp
        import numpy as np
        from jax import lax
        STRIDE = 1
        PADDING = 4
        out = lax.conv_general_dilated(x, weight, window_strides=(STRIDE,), padding=[(PADDING, PADDING)], dimension_numbers=('NCH', 'OIH', 'NCH'))
        out = out + bias[None, :, None]
        return jnp.transpose(out, (0, 2, 1))

    def _L0_attn_ref(x, delta_w, qkv_w, g1, g2, g3):
        import jax, jax.numpy as jnp
        import numpy as np
        EPS = 1.1920929e-07

        def _rmsnorm(x, g):
            inv = jax.lax.rsqrt(jnp.mean(x * x, axis=-1, keepdims=True) + EPS)
            return x * inv * g
        B, T, C = x.shape
        H = 8
        D = C // H
        sqrt_d = jnp.float32(D) ** 0.5
        W = qkv_w + delta_w
        w = (x @ W.T).reshape(B, T, H, D).transpose(0, 2, 1, 3)
        att = jnp.einsum('bhif,bhjf->bhij', _rmsnorm(w, g1), _rmsnorm(w, g2)) / sqrt_d
        score = jax.nn.softmax(att, axis=-1) + jax.nn.softmax(att, axis=-2)
        y = jnp.einsum('bhij,bhjf->bihf', score, _rmsnorm(w, g3))
        return y.reshape(B, T, C) @ W

    def _L0_ffn_ref(x, Wg, bg, We, be):
        import jax, jax.numpy as jnp
        import numpy as np
        B, S, D, E, O = (256, 64, 128, 16, 128)
        scores = jax.nn.softmax(jnp.mean(x, axis=1) @ Wg + bg, axis=-1)
        idx = jnp.argmax(scores, axis=-1)
        gate = jnp.take_along_axis(scores, idx[:, None], axis=-1)
        W_sel = We[idx]
        b_sel = be[idx]
        y = jnp.einsum('bsd,bdo->bso', x, W_sel) + b_sel[:, None, :]
        return gate[:, :, None] * y

    def _L1_attn_ref(x, Wq, Wk, Wv, Wb, Wo, ln_g, ln_b):
        import jax, jax.numpy as jnp
        import numpy as np
        H = 8
        EPS = 1e-05

        def _delta_net(x, Wq, Wk, Wv, Wb, Wo, ln_g, ln_b):
            B, L, D = x.shape
            dh = D // H

            def heads(W):
                return (x @ W).reshape(B, L, H, dh)
            q = heads(Wq)
            k = heads(Wk)
            v = heads(Wv)
            beta = jax.nn.sigmoid(heads(Wb))
            q = q / jnp.linalg.norm(q, axis=-1, keepdims=True)
            k = k / jnp.linalg.norm(k, axis=-1, keepdims=True)
            qs, ks_, vs, bs = (jnp.moveaxis(t, 1, 0) for t in (q, k, v, beta))
            S0 = jnp.zeros((B, H, dh, dh), x.dtype)

            def step(S, inp):
                qt, kt, vt, bt = inp
                pred = jnp.einsum('bhk,bhkv->bhv', kt, S)
                S = S + jnp.einsum('bhk,bhv->bhkv', kt, bt * (vt - pred))
                o = jnp.einsum('bhk,bhkv->bhv', qt, S)
                return (S, o)
            final_state, ys = jax.lax.scan(step, S0, (qs, ks_, vs, bs))
            y = jnp.moveaxis(ys, 0, 1).reshape(B, L, D)
            mu = jnp.mean(y, axis=-1, keepdims=True)
            var = jnp.var(y, axis=-1, keepdims=True)
            yn = (y - mu) * jax.lax.rsqrt(var + EPS) * ln_g + ln_b
            return (yn @ Wo, final_state)

        def _reference_tuple_inner(x, Wq, Wk, Wv, Wb, Wo, ln_g, ln_b):
            return _delta_net(x, Wq, Wk, Wv, Wb, Wo, ln_g, ln_b)
        return _reference_tuple_inner(x, Wq, Wk, Wv, Wb, Wo, ln_g, ln_b)[0]

    def _L1_ffn_ref(hidden_states, W_hash, W1, b1, W2, b2):
        import jax, jax.numpy as jnp
        import numpy as np
        D_MODEL = 128
        D_FF = 512
        N_EXPERTS = 64
        K_ACTIVE = 2
        N_HASHES = 4
        LAYER_ID = 0
        SALT = 0.0
        BUCKET_SCALE = 8.0
        CAPACITY_FACTOR = 1.25
        B, S, D = hidden_states.shape
        T = B * S
        x = hidden_states.reshape(T, D)
        scores = x @ W_hash.T
        buckets = jnp.mod(jnp.floor(scores * BUCKET_SCALE + SALT).astype(jnp.int32) + LAYER_ID, N_EXPERTS)
        selected = buckets[:, :K_ACTIVE]
        flat_e = selected.reshape(-1)
        C = int(np.ceil(T * K_ACTIVE / N_EXPERTS * CAPACITY_FACTOR))
        oh = jax.nn.one_hot(flat_e, N_EXPERTS, dtype=jnp.int32)
        pos = jnp.sum((jnp.cumsum(oh, axis=0) - 1) * oh, axis=1)
        valid = pos < C
        pos_c = jnp.clip(pos, 0, C - 1)
        x_rep = jnp.repeat(x, K_ACTIVE, axis=0)
        buf = jnp.zeros((N_EXPERTS, C, D), dtype=x.dtype).at[flat_e, pos_c].add(jnp.where(valid[:, None], x_rep, 0.0))
        h = jax.nn.gelu(jnp.einsum('ecd,edf->ecf', buf, W1) + b1[:, None, :], approximate=False)
        y = jnp.einsum('ecf,efd->ecd', h, W2) + b2[:, None, :]
        out_pairs = jnp.where(valid[:, None], y[flat_e, pos_c], 0.0)
        out = out_pairs.reshape(T, K_ACTIVE, D).mean(axis=1)
        return out.reshape(B, S, D)
    h = _L0_tok_ref(x, L0_tok_weight, L0_tok_bias)
    h = h + _L0_attn_ref(_layernorm(h, axis=-1), L0_attn_delta_w, L0_attn_qkv_w, L0_attn_g1, L0_attn_g2, L0_attn_g3)
    h = h + _L0_ffn_ref(_layernorm(h, axis=-1), L0_ffn_Wg, L0_ffn_bg, L0_ffn_We, L0_ffn_be)
    h = h + _L1_attn_ref(_layernorm(h, axis=-1), L1_attn_Wq, L1_attn_Wk, L1_attn_Wv, L1_attn_Wb, L1_attn_Wo, L1_attn_ln_g, L1_attn_ln_b)
    h = h + _L1_ffn_ref(_layernorm(h, axis=-1), L1_ffn_W_hash, L1_ffn_W1, L1_ffn_b1, L1_ffn_W2, L1_ffn_b2)
    return h

_drawn_inputs = setup_inputs


def setup_inputs(seed=0):
    import zlib

    import numpy as np

    out = dict(_drawn_inputs(seed))
    spreads = {'L0_attn_g1': (1.0, 0.6),
     'L0_attn_g2': (1.0, 0.6),
     'L0_attn_g3': (1.0, 0.6),
     'L1_attn_ln_g': (1.0, 0.6),
     'L1_attn_ln_b': (0.0, 0.8),
     'L1_ffn_b1': (0.0, 0.8),
     'L1_ffn_b2': (0.0, 2.0)}
    factors = {'L0_attn_delta_w': 6.248,
     'L0_attn_qkv_w': 6.204,
     'L0_ffn_Wg': 8.0,
     'L0_ffn_bg': 8.0,
     'L0_ffn_We': 8.0,
     'L0_ffn_be': 8.0,
     'L1_attn_Wb': 3.402,
     'L1_ffn_W_hash': 3.759,
     'L1_ffn_W1': 4.189,
     'L1_ffn_W2': 3.753}
    for name, (base, spread) in spreads.items():
        noise = np.random.default_rng([zlib.crc32(name.encode()), seed]).standard_normal(out[name].shape)
        drawn = base * np.exp(spread * noise) if base else spread * noise
        out[name] = jnp.asarray(drawn.astype(out[name].dtype))
    for name, factor in factors.items():
        out[name] = (out[name] * factor).astype(out[name].dtype)
    return out
```

```python
import numpy as np
import concourse.bass as bass
from concourse import mybir
from contextlib import ExitStack

FP32 = mybir.dt.float32
BF16 = mybir.dt.bfloat16
I32 = mybir.dt.int32
ALU = mybir.AluOpType
ACT = mybir.ActivationFunctionType
AX = mybir.AxisListType

B, CIN, L = 8, 64, 750
D, H, F = 128, 8, 16
TT, NT = 125, 6
NTILES = B * NT
HALF = L // 2
TAPS, PAIRS = 9, 5
PAD = 4
XW = L + 2 * PAD
G = 2
LN_EPS = 1e-5
RMS_EPS = 1.1920929e-07
PIECES = 3
PIECES_A = [0, 0, 1, 1, 0, 2]
PIECES_B = [0, 1, 0, 1, 2, 0]
KROWS = len(PIECES_A) * F


class Memory:

    def __init__(self, nc, stage):
        self.nc, self.stage, self.stack, self.sems = nc, stage, ExitStack(), []

    def __enter__(self):
        return self

    def __exit__(self, *error):
        self.stack.close()
        if self.sems:
            self.nc.clear_and_free_semaphores(self.sems)
            self.nc.all_engine_barrier()

    def sbuf(self, name, shape, dt=FP32):
        return self.stack.enter_context(self.nc.sbuf_tensor(f"{self.stage}_{name}", shape, dt))

    def sem(self, name):
        self.sems.append(self.nc.alloc_semaphore(name=f"{self.stage}_{name}"))
        return self.sems[-1]


def convolution(nc, io, h, stats, psum, ident):
    with Memory(nc, "conv") as m:
        xpad = m.sbuf("xpad", [128, B, XW])
        wconv = m.sbuf("w", [128, PAIRS, D])
        cbias = m.sbuf("bias", [128, 1])
        hT = m.sbuf("hT", [128, 2, L])
        loaded = m.sem("loaded")
        padded = m.sem("padded")
        conv_ready, conv_free = m.sem("conv_ready"), m.sem("conv_free")
        hT_ready, hT_free = m.sem("hT_ready"), m.sem("hT_free")
        turned_ready, turned_free = m.sem("turned_ready"), m.sem("turned_free")
        h_written = m.sem("h_written")
        with nc.Block() as block:
            @block.sync
            def _(sp):
                sp.dma_start(wconv[0:64, :, :], io["conv_w_even"]).then_inc(loaded, 16)
                sp.dma_start(wconv[64:128, 0:PAIRS - 1, :], io["conv_w_odd"]).then_inc(loaded, 16)
                sp.dma_start(cbias[:], io["conv_b"]).then_inc(loaded, 16)
                x_cbl = io["x"].rearrange("b c l -> c b l")
                sp.dma_start(xpad[0:64, :, PAD:PAD + L], x_cbl).then_inc(loaded, 16)
                sp.dma_start(xpad[64:128, :, PAD - 1:PAD - 1 + L], x_cbl).then_inc(loaded, 16)

            @block.gpsimd
            def _(pool):
                nc.gpsimd.memset(xpad[0:64, :, 0:PAD], 0.0).then_inc(padded, 1)
                nc.gpsimd.memset(xpad[0:64, :, PAD + L:XW], 0.0).then_inc(padded, 1)
                nc.gpsimd.memset(xpad[64:128, :, 0:PAD - 1], 0.0).then_inc(padded, 1)
                nc.gpsimd.memset(xpad[64:128, :, PAD - 1 + L:XW], 0.0).then_inc(padded, 1)

            @block.tensor
            def _(pe):
                pe.wait_ge(loaded, 80)
                pe.wait_ge(padded, 4)
                with pe.Fori(0, B // 2) as i:
                    for u in range(2):
                        pe.wait_ge(conv_free, 2 * i + (u + 1))
                        for half in range(2):
                            for j in range(PAIRS):
                                rows = 128 if j < PAIRS - 1 else 64
                                mm = nc.tensor.matmul(
                                    psum[2 * u + half][:, 0:HALF], wconv[0:rows, j, :],
                                    xpad[0:rows, bass.ds(2 * i + u, 1), half * HALF + 2 * j:half * HALF + 2 * j + HALF],
                                    start=(j == 0), stop=(j == PAIRS - 1))
                        mm.then_inc(conv_ready, 1)
                    for u in range(2):
                        pe.wait_ge(hT_ready, 2 * (2 * i + u) + 2)
                        pe.wait_ge(turned_free, 2 * i + (u + 1))
                        for t in range(NT):
                            mm = nc.tensor.transpose(psum[4 + 2 * u + t // 3][0:TT, (t % 3) * D:(t % 3 + 1) * D],
                                                     hT[:, u, t * TT:(t + 1) * TT], ident[:])
                        mm.then_inc(turned_ready, 1)

            @block.scalar
            def _(act):
                act.sem_inc(conv_free, 2)
                with act.Fori(0, B // 2) as i:
                    for u in range(2):
                        act.wait_ge(conv_ready, 2 * i + (u + 1))
                        act.wait_ge(hT_free, 2 * i + (u + 1))
                        for half in range(2):
                            ins = nc.scalar.activation(hT[:, u, half * HALF:(half + 1) * HALF],
                                                       psum[2 * u + half][:, 0:HALF], ACT.Identity, bias=cbias[:])
                            ins.then_inc(hT_ready, 1)
                        act.wait_ge(hT_ready, 2 * (2 * i + u) + 2)
                        act.sem_inc(conv_free, 1)

            @block.vector
            def _(dve):
                dve.sem_inc(turned_free, 2)
                dve.sem_inc(hT_free, 2)
                with dve.Fori(0, B // 2) as i:
                    for u in range(2):
                        dve.wait_ge(turned_ready, 2 * i + (u + 1))
                        dve.sem_inc(hT_free, 1)
                        for k in range(2):
                            nc.vector.tensor_copy(
                                h[0:TT, bass.ds((2 * i + u) * NT + 3 * k, 3), :],
                                psum[4 + 2 * u + k][0:TT, 0:3 * D].rearrange("p (t d) -> p t d", d=D)).then_inc(h_written, 1)
                        for t in range(NT):
                            nc.vector.bn_stats(stats[0:TT, bass.ds((2 * i + u) * NT + t, 1), :],
                                               psum[4 + 2 * u + t // 3][0:TT, (t % 3) * D:(t % 3 + 1) * D]
                                               ).then_inc(h_written, 1)
                        dve.wait_ge(h_written, (2 + NT) * (2 * i + u + 1))
                        dve.sem_inc(turned_free, 1)


def pass_gate(eng, sem, value, gate):
    eng.wait_ge(sem, value)
    eng.sem_inc(gate, 1)


class Chain:

    def __init__(self, eng, sem, base=0, anchor=None):
        self.eng, self.sem, self.base, self.n, self.anchor = eng, sem, base, 0, anchor

    def add(self, ins):
        ins.then_inc(self.sem, 1)
        self.n += 1

    def settle(self):
        self.eng.wait_ge(self.sem, self.base + self.n)
        if self.anchor is not None:
            self.eng.sem_inc(self.anchor, 1)

    def link(self, ins):
        self.add(ins)
        self.settle()


def spread(scalars, n):
    rows, tiles = scalars.shape
    return scalars.unsqueeze(2).broadcast_to([rows, tiles, n])


def moments(nc, dve, chain, stats, mean, var, tmp):
    even_mean, even_m2 = stats[0:TT, :, 1], stats[0:TT, :, 2]
    odd_mean, odd_m2 = stats[0:TT, :, 4], stats[0:TT, :, 5]
    chain.link(nc.vector.tensor_tensor(mean, even_mean, odd_mean, ALU.add))
    chain.link(nc.vector.tensor_scalar(mean, mean, 0.5, None, ALU.mult))
    chain.link(nc.vector.tensor_tensor(tmp, even_mean, odd_mean, ALU.subtract))
    chain.link(nc.vector.tensor_tensor(tmp, tmp, tmp, ALU.mult))
    chain.link(nc.vector.tensor_tensor(var, even_m2, odd_m2, ALU.add))
    chain.link(nc.vector.tensor_scalar(var, var, 1.0 / D, None, ALU.mult))
    chain.link(nc.vector.scalar_tensor_tensor(out=var, in0=tmp, scalar=0.25, in1=var, op0=ALU.mult, op1=ALU.add))
    chain.link(nc.vector.tensor_scalar(var, var, LN_EPS, None, ALU.add))


def refine_rsqrt(nc, chain, rstd, var, tmp):
    chain.link(nc.vector.tensor_tensor(tmp, rstd, rstd, ALU.mult))
    chain.link(nc.vector.tensor_tensor(tmp, tmp, var, ALU.mult))
    chain.link(nc.vector.tensor_scalar(tmp, tmp, -0.5, 1.5, ALU.mult, ALU.add))
    chain.link(nc.vector.tensor_tensor(rstd, rstd, tmp, ALU.mult))


def layernorm_scalars(nc, stage, stats, mean, rstd):
    with Memory(nc, stage) as m:
        var = m.sbuf("var", [128, NTILES])
        tmp = m.sbuf("tmp", [128, NTILES])
        var_ready, root_ready, done = m.sem("var_ready"), m.sem("root_ready"), m.sem("done")
        with nc.Block() as block:
            @block.vector
            def _(dve):
                chain = Chain(dve, done)
                moments(nc, dve, chain, stats, mean[0:TT, :], var[0:TT, :], tmp[0:TT, :])
                dve.sem_inc(var_ready, 1)
                dve.wait_ge(root_ready, 1)
                chain.link(nc.vector.reciprocal(rstd[0:TT, :], tmp[0:TT, :]))
                refine_rsqrt(nc, chain, rstd[0:TT, :], var[0:TT, :], tmp[0:TT, :])

            @block.scalar
            def _(act):
                act.wait_ge(var_ready, 1)
                nc.scalar.activation(tmp[0:TT, :], var[0:TT, :], ACT.Sqrt).then_inc(root_ready, 1)


def head_vectors(nc, io, h, mean, rstd, n3, dmax, pieces_dram, psum, ident, block_ones):
    with Memory(nc, "heads") as m:
        wT = m.sbuf("wT", [128, D])
        wTd = m.sbuf("wTd", [128, D])
        gcols = m.sbuf("gcols", [128, 2])
        pcol = m.sbuf("pcol", [128, 1])
        pabs = m.sbuf("pabs", [128, 1])
        eps = m.sbuf("eps", [128, 1])
        bound_w = m.sbuf("bound_w", [128, D])
        g3row = m.sbuf("g3row", [128, D])
        xn = m.sbuf("xn", [128, 2, NT, D])
        xnT = m.sbuf("xnT", [128, 2, L])
        sq = m.sbuf("sq", [128, 2, L])
        rms = m.sbuf("rms", [128, 2, L])
        nT = m.sbuf("nT", [128, 2, L])
        pnT = m.sbuf("pnT", [128, 2, L])
        rest = m.sbuf("rest", [128, 2, 2, L])
        pieces = m.sbuf("pieces", [128, 2, 2 * PIECES, L], BF16)
        loaded = m.sem("loaded")
        setup = m.sem("setup")
        xn_ready, xnT_psum, xnT_ready, w_psum, sq_ready, ms_psum, rms_ready = (
            m.sem(s) for s in ("xn_ready", "xnT_psum", "xnT_ready", "w_psum", "sq_ready", "ms_psum", "rms_ready"))
        n_ready, n2_ready, n3_psum, bound_psum, dmax_ready, n3_ready = (
            m.sem(s) for s in ("n_ready", "n2_ready", "n3_psum", "bound_psum", "dmax_ready", "n3_ready"))
        a_split, b_split, stored, dve_chain, pool_chain = (
            m.sem(s) for s in ("a_split", "b_split", "stored", "dve_chain", "pool_chain"))
        gate = m.sem("gate")
        pieces_free, nT_free = m.sem("pieces_free"), m.sem("nT_free")
        dmax2 = m.sbuf("dmax2", [128, 2 * B])

        def two_banks(bank):
            return [psum[bank][:, 0:HALF], psum[bank + 1][:, 0:HALF]]

        def split(eng, chain, source, rest, out, first):
            high, middle, low = (out[:, first + k, :] for k in range(PIECES))
            chain.link(eng.tensor_copy(high, source))
            chain.link(eng.tensor_tensor(rest, source, high, ALU.subtract))
            chain.link(eng.tensor_copy(middle, rest))
            return eng.tensor_tensor(low, rest, middle, ALU.subtract)

        with nc.Block() as block:
            @block.sync
            def _(sp):
                sp.dma_start(wT[:], io["w_qkv_T"]).then_inc(loaded, 16)
                sp.dma_start(wTd[:], io["w_delta_T"]).then_inc(loaded, 16)
                sp.dma_start(gcols[:], io["g12_cols"]).then_inc(loaded, 16)
                sp.dma_start(g3row[:], io["g3_row"].partition_broadcast(128)).then_inc(loaded, 16)
                sp.sem_inc(pieces_free, 2)
                with sp.Fori(0, B // 2) as i:
                    for u in range(2):
                        sp.wait_ge(a_split, 2 * i + (u + 1))
                        sp.wait_ge(b_split, 2 * i + (u + 1))
                        sp.dma_start(pieces_dram[bass.ds(2 * i + u, 1), :, :, :].rearrange("o k p t -> p (o k) t"),
                                     pieces[:, u, :, :]).then_inc(stored, 16)
                        sp.wait_ge(stored, 16 * (2 * i + u) + 16)
                        sp.sem_inc(pieces_free, 1)

            @block.tensor
            def _(pe):
                pe.wait_ge(setup, 1)
                with pe.Fori(0, B // 2) as i:
                    for u in range(2):
                        pe.wait_ge(xn_ready, 2 * i + (u + 1))
                        pe.wait_ge(dmax_ready, 2 * i + (u + 1))
                        for t in range(NT):
                            mm = nc.tensor.transpose(psum[4 * u + t // 3][:, (t % 3) * TT:(t % 3 + 1) * TT],
                                                     xn[0:TT, u, t, :], ident[0:TT, 0:TT])
                        mm.then_inc(xnT_psum, 1)
                    for u in range(2):
                        pe.wait_ge(xnT_ready, 2 * (2 * i + u) + 2)
                        pe.wait_ge(n3_ready, 2 * i + (u + 1))
                        for half in range(2):
                            mm = nc.tensor.matmul(psum[4 * u + 2 + half][:, 0:HALF], wT[:],
                                                  xnT[:, u, half * HALF:(half + 1) * HALF], start=True, stop=True)
                        mm.then_inc(w_psum, 1)
                    for u in range(2):
                        pe.wait_ge(sq_ready, 2 * (2 * i + u) + 2)
                        for half in range(2):
                            mm = nc.tensor.matmul(psum[4 * u + half][:, 0:HALF], block_ones[:],
                                                  sq[:, u, half * HALF:(half + 1) * HALF], start=True, stop=True)
                        mm.then_inc(ms_psum, 1)
                    for u in range(2):
                        pe.wait_ge(n_ready, 2 * i + (u + 1))
                        for t in range(NT):
                            mm = nc.tensor.transpose(psum[4 * u + 2 + t // 3][0:TT, (t % 3) * D:(t % 3 + 1) * D],
                                                     nT[:, u, t * TT:(t + 1) * TT], ident[:])
                        mm.then_inc(n3_psum, 1)
                        pe.wait_ge(n2_ready, 2 * i + (u + 1))
                        for half in range(2):
                            mm = nc.tensor.matmul(psum[4 * u + half][:, 0:HALF], bound_w[:],
                                                  sq[:, u, half * HALF:(half + 1) * HALF], start=True, stop=True)
                        mm.then_inc(bound_psum, 1)

            @block.scalar
            def _(act):
                act.wait_ge(setup, 1)
                with act.Fori(0, B // 2) as i:
                    for u in range(2):
                        act.wait_ge(xnT_psum, 2 * i + (u + 1))
                        for half in range(2):
                            nc.scalar.activation(xnT[:, u, half * HALF:(half + 1) * HALF],
                                                 psum[4 * u + half][:, 0:HALF], ACT.Identity).then_inc(xnT_ready, 1)
                    for u in range(2):
                        act.wait_ge(w_psum, 2 * i + (u + 1))
                        for half in range(2):
                            nc.scalar.activation(sq[:, u, half * HALF:(half + 1) * HALF],
                                                 psum[4 * u + 2 + half][:, 0:HALF], ACT.Square).then_inc(sq_ready, 1)
                    for u in range(2):
                        act.wait_ge(ms_psum, 2 * i + (u + 1))
                        for half in range(2):
                            nc.scalar.activation(rms[:, u, half * HALF:(half + 1) * HALF],
                                                 psum[4 * u + half][:, 0:HALF], ACT.Sqrt, bias=eps[:]).then_inc(rms_ready, 1)

            @block.gpsimd
            def _(pool):
                pool.wait_ge(setup, 1)
                pool.sem_inc(nT_free, 2)
                with pool.Fori(0, B // 2) as i:
                    chain = Chain(pool, pool_chain, 8 * i, gate)
                    for u in range(2):
                        pool.wait_ge(n_ready, 2 * i + (u + 1))
                        pass_gate(pool, pieces_free, 2 * i + (u + 1), gate)
                        chain.link(nc.gpsimd.tensor_scalar(pnT[:, u, :], nT[:, u, :], pcol[:], None, ALU.mult))
                        split(nc.gpsimd, chain, pnT[:, u, :], rest[:, 1, u, :], pieces[:, u], PIECES).then_inc(b_split, 1)
                        pool.wait_ge(b_split, 2 * i + (u + 1))
                        pool.sem_inc(nT_free, 1)

            @block.vector
            def _(dve):
                setup_chain = Chain(dve, dve_chain)
                dve.wait_ge(loaded, 64)
                dve.sem_inc(dmax_ready, 2)
                dve.sem_inc(n3_ready, 2)
                setup_chain.link(nc.vector.memset(eps[:], RMS_EPS))
                setup_chain.link(nc.vector.tensor_tensor(wT[:], wT[:], wTd[:], ALU.add))
                setup_chain.link(nc.vector.tensor_tensor(pcol[:], gcols[:, 0:1], gcols[:, 1:2], ALU.mult))
                setup_chain.link(nc.vector.tensor_scalar(pcol[:], pcol[:], F ** -0.5, None, ALU.mult))
                setup_chain.link(nc.vector.tensor_scalar(pabs[:], pcol[:], -1.0, None, ALU.mult))
                setup_chain.link(nc.vector.tensor_tensor(pabs[:], pabs[:], pcol[:], ALU.max))
                setup_chain.link(nc.vector.tensor_scalar(bound_w[:], block_ones[:], pabs[:], float(F), ALU.mult, ALU.mult))
                dve.sem_inc(setup, 1)
                with dve.Fori(0, B // 2) as i:
                    chain = Chain(dve, dve_chain, setup_chain.n + i * 24)
                    for u in range(2):
                        for t in range(NT):
                            col = (2 * i + u) * NT + t
                            chain.add(nc.vector.tensor_scalar(
                                xn[0:TT, u, t, :], h[0:TT, bass.ds(col, 1), :], mean[0:TT, bass.ds(col, 1)],
                                rstd[0:TT, bass.ds(col, 1)], ALU.subtract, ALU.mult))
                        chain.settle()
                        dve.sem_inc(xn_ready, 1)
                    for u in range(2):
                        dve.wait_ge(rms_ready, 2 * (2 * i + u) + 2)
                        chain.link(nc.vector.reciprocal(rms[:, u, :], rms[:, u, :]))
                        dve.wait_ge(nT_free, 2 * i + (u + 1))
                        for half in range(2):
                            cols = slice(half * HALF, (half + 1) * HALF)
                            ins = nc.vector.tensor_tensor(nT[:, u, cols], psum[4 * u + 2 + half][:, 0:HALF],
                                                          rms[:, u, cols], ALU.mult)
                            chain.add(ins)
                        chain.settle()
                        dve.sem_inc(n_ready, 1)
                        nc.vector.tensor_tensor(sq[:, u, :], nT[:, u, :], nT[:, u, :], ALU.mult).then_inc(n2_ready, 1)
                    for u in range(2):
                        dve.wait_ge(pieces_free, 2 * i + (u + 1))
                        split(nc.vector, chain, nT[:, u, :], rest[:, 0, u, :], pieces[:, u], 0).then_inc(a_split, 1)
                        dve.wait_ge(n3_psum, 2 * i + (u + 1))
                        for k in range(2):
                            ins = nc.vector.tensor_tensor(
                                n3[0:TT, bass.ds((2 * i + u) * NT + 3 * k, 3), :],
                                psum[4 * u + 2 + k][0:TT, 0:3 * D].rearrange("p (t d) -> p t d", d=D),
                                g3row[0:TT, :].unsqueeze(1).broadcast_to([TT, 3, D]), ALU.mult)
                        ins.then_inc(n3_ready, 1)
                        dve.wait_ge(bound_psum, 2 * i + (u + 1))
                        for half in range(2):
                            ins = nc.vector.tensor_reduce(dmax2[:, bass.ds(2 * (2 * i + u) + half, 1)],
                                                          psum[4 * u + half][:, 0:HALF], AX.X, ALU.max)
                        ins.then_inc(dmax_ready, 1)
                        dve.wait_ge(a_split, 2 * i + (u + 1))
                    assert chain.n == 24
                dve.wait_ge(dmax_ready, B + 2)
                nc.vector.tensor_reduce(dmax[:], dmax2[:].rearrange("p (b k) -> p b k", k=2), AX.X, ALU.max).then_inc(setup, 1)


def attention(nc, io, h, stats, n3, dmax, pieces_dram, psum_banks, psum, ident, ones):
    EBUFS = 3
    with Memory(nc, "att") as m:
        piece_a = m.sbuf("piece_a", [KROWS, G, 4, L], BF16)
        piece_b = m.sbuf("piece_b", [KROWS, G, 4, L], BF16)
        w2 = m.sbuf("w2", [128, G, D])
        w2d = m.sbuf("w2d", [128, G, D])
        head_start = m.sbuf("head_start", [128, H])
        dsel = m.sbuf("dsel", [128, B, H])
        guard = m.sbuf("guard", [128, B * H])
        e = m.sbuf("e", [128, EBUFS, 4, L])
        z = m.sbuf("z", [128, EBUFS, 4])
        rz = m.sbuf("rz", [128, EBUFS, 4])
        values = m.sbuf("values", [128, EBUFS, 4, 2, F])
        scales = m.sbuf("scales", [128, G, NT, 4, 2, F])
        scaleT = m.sbuf("scaleT", [128, L])
        ys = m.sbuf("ys", [128, G, L])
        loaded, setup = m.sem("loaded"), m.sem("setup")
        guard_psum = m.sem("guard_psum")
        ab_ready = [m.sem(f"ab_ready{g}") for g in range(G)]
        ab_free = [m.sem(f"ab_free{g}") for g in range(G)]
        att_ready, att_free, e_ready, e_free = (m.sem(s) for s in ("att_ready", "att_free", "e_ready", "e_free"))
        values_ready, scales_ready, scaleT_psum, scaleT_free = (
            m.sem(s) for s in ("values_ready", "scales_ready", "scaleT_psum", "scaleT_free"))
        y_psum, y_free, ys_ready, out_psum, out_free = (
            m.sem(s) for s in ("y_psum", "y_free", "ys_ready", "out_psum", "out_free"))
        dve_chain, dve_done = m.sem("dve_chain"), m.sem("dve_done")
        gate = m.sem("gate")
        SETS = G * NT
        assert SETS % EBUFS == 0
        CUTS = [(0, 0, 188), (0, 188, HALF), (1, 0, 188), (1, 188, HALF)]

        def batches(eng, body):
            body(0, True)
            with eng.Fori(1, B) as b:
                body(b, False)

        with nc.Block() as block:
            @block.sync
            def _(sp):
                sp.dma_start(w2[:], io["w_qkv_rows"]).then_inc(loaded, 16)
                sp.dma_start(w2d[:], io["w_delta_rows"]).then_inc(loaded, 16)
                sp.dma_start(head_start[:], io["head_start"]).then_inc(loaded, 16)
                with sp.Fori(0, B) as b:
                    for g in range(G):
                        sp.wait_ge(ab_free[g], b + 1)
                        for dst, which in ((piece_a, [0, 0, 1, 1, 0, 2]), (piece_b, [3, 4, 3, 4, 5, 3])):
                            for k, piece in enumerate(which):
                                src = pieces_dram[bass.ds(b, 1), piece, g * 64:(g + 1) * 64, :]
                                sp.dma_start(dst[k * F:(k + 1) * F, g, :, :],
                                             src.rearrange("o (q f) t -> f (o q) t", f=F)).then_inc(ab_ready[g], 16)

            @block.tensor
            def _(pe):
                pe.wait_ge(setup, 1)
                nc.tensor.matmul(psum[6][:, 0:B * H], ones[:], dsel[:].rearrange("p b h -> p (b h)"),
                                 start=True, stop=True).then_inc(guard_psum, 1)
                pe.sem_inc(ab_free[0], 1)
                pe.sem_inc(ab_free[1], 1)
                pe.wait_ge(setup, 2)

                def scores(b, s, q):
                    g, j = divmod(s, NT)
                    if j == 0 and q == 0:
                        pe.wait_ge(ab_ready[g], 192 * b + 192)
                    pe.wait_ge(att_free, 4 * SETS * b + (4 * s + q + 1))
                    for half in range(2):
                        mm = nc.tensor.matmul(psum[2 * (q % 2) + half][0:TT, 0:HALF],
                                              piece_a[:, g, q, j * TT:(j + 1) * TT],
                                              piece_b[:, g, q, half * HALF:(half + 1) * HALF], start=True, stop=True)
                    mm.then_inc(att_ready, 1)
                    if j == NT - 1 and q == 3:
                        pe.wait_ge(att_ready, 4 * SETS * b + (4 * s + q + 1))
                        pe.sem_inc(ab_free[g], 1)

                def weigh(b, s, k):
                    j = s % NT
                    half, lo, hi = CUTS[k]
                    if j == 0:
                        if k % 2 == 1:
                            lo = hi
                        else:
                            hi = HALF
                    if k == 0:
                        pe.wait_ge(values_ready, SETS * b + (s + 1))
                        if j == 0:
                            pe.wait_ge(y_free, G * b + (s // NT + 1))
                    for q in range(4 if hi > lo else 0):
                        mm = nc.tensor.matmul(psum[4 + half][32 * q:32 * q + 32, lo:hi],
                                              values[0:TT, s % EBUFS, q, :, :].rearrange("p a f -> p (a f)"),
                                              e[0:TT, s % EBUFS, q, half * HALF + lo:half * HALF + hi],
                                              start=(j == 0), stop=(j == NT - 1), skip_group_check=True)
                    if k == (3 if j > 0 else 2):
                        mm.then_inc(e_free, 1)
                        if j == NT - 1:
                            pe.wait_ge(e_free, SETS * b + (s + 1 + EBUFS))
                            pe.sem_inc(y_psum, 1)

                def turn_scales(b, g, tiles):
                    if tiles[0] == 0:
                        pe.wait_ge(scales_ready, SETS * b + (g + 1) * NT)
                        pe.wait_ge(out_free, (G + 1) * b + (g + 1))
                    for t in tiles:
                        mm = nc.tensor.transpose(psum[6 + t // 3][:, (t % 3) * TT:(t % 3 + 1) * TT],
                                                 scales[0:TT, g, t, :, :, :].rearrange("p q a f -> p (q a f)"),
                                                 ident[0:TT, 0:TT])
                    if tiles[-1] == NT - 1:
                        mm.then_inc(scaleT_psum, 1)

                def project(b, t):
                    if t == 0:
                        pe.wait_ge(ys_ready, G * b + G)
                        pe.wait_ge(out_free, (G + 1) * b + (G + 1))
                    for g in range(G):
                        mm = nc.tensor.matmul(psum[6 + t // 3][0:TT, (t % 3) * D:(t % 3 + 1) * D],
                                              ys[:, g, t * TT:(t + 1) * TT], w2[:, g, :],
                                              start=(g == 0), stop=(g == G - 1))
                    if t == NT - 1:
                        mm.then_inc(out_psum, 1)

                def body(b, first):
                    for s in range(SETS):
                        for q in range(4):
                            scores(b, s, q)
                            n = 4 * s + q - 5
                            if n >= 0:
                                weigh(b, n // 4, n % 4)
                            elif not first:
                                weigh(b - 1, SETS + n // 4, n % 4)
                            if s % NT == 0 and q > 0:
                                if s == NT:
                                    turn_scales(b, 0, [2 * q - 2, 2 * q - 1])
                                elif not first:
                                    turn_scales(b - 1, 1, [2 * q - 2, 2 * q - 1])
                            at = 4 * s + q - 9
                            if 0 <= at < NT and not first:
                                project(b - 1, at)
                batches(pe, body)
                for n in range(4 * SETS - 5, 4 * SETS):
                    weigh(B - 1, n // 4, n % 4)
                turn_scales(B - 1, 1, list(range(NT)))
                for t in range(NT):
                    project(B - 1, t)

            @block.scalar
            def _(act):
                act.wait_ge(setup, 2)
                act.sem_inc(att_free, 2)
                act.sem_inc(e_free, EBUFS)
                act.wait_ge(loaded, 48)
                with act.Fori(0, B) as b:
                    for s in range(SETS):
                        g = s // NT
                        act.wait_ge(e_free, SETS * b + (s + 1))
                        for q in range(4):
                            pass_gate(act, att_ready, 4 * SETS * b + (4 * s + q + 1), gate)
                            nc.scalar.activation(
                                e[0:TT, s % EBUFS, q, :].rearrange("p (a t) -> p a t", a=2),
                                psum_banks[0:TT, 2 * (q % 2):2 * (q % 2) + 2, 0:HALF], ACT.Exp,
                                bias=guard[0:TT, bass.ds(H * b + 4 * g + q, 1)],
                                accum_out=z[0:TT, s % EBUFS, q:q + 1]).then_inc(att_free, 1)

            @block.vector
            def _(dve):
                chain = Chain(dve, dve_chain)
                dve.wait_ge(loaded, 48)
                chain.link(nc.vector.memset(scales[:], 1.0))
                chain.link(nc.vector.tensor_tensor(w2[:], w2[:], w2d[:], ALU.add))
                chain.link(nc.vector.tensor_tensor(dsel[:], dmax[:].unsqueeze(2).broadcast_to([128, B, H]),
                                                   head_start[:].unsqueeze(1).broadcast_to([128, B, H]), ALU.mult))
                dve.sem_inc(setup, 1)
                dve.wait_ge(guard_psum, 1)
                chain.link(nc.vector.tensor_scalar(guard[:], psum[6][:, 0:B * H], -1.0, None, ALU.mult))
                dve.sem_inc(y_free, 1)
                dve.sem_inc(out_free, 1)
                dve.sem_inc(setup, 1)

                def turned_scales(b, g, chain):
                    dve.wait_ge(scaleT_psum, G * b + (g + 1))
                    for half in range(2):
                        chain.add(nc.vector.tensor_copy(scaleT[:, half * HALF:(half + 1) * HALF],
                                                        psum[6 + half][:, 0:HALF]))
                    chain.settle()
                    dve.sem_inc(out_free, 1)

                def scaled(b, g, chain):
                    dve.wait_ge(y_psum, G * b + (g + 1))
                    for half in range(2):
                        cols = slice(half * HALF, (half + 1) * HALF)
                        chain.add(nc.vector.tensor_tensor(ys[:, g, cols], psum[4 + half][:, 0:HALF],
                                                          scaleT[:, cols], ALU.mult))
                    chain.settle()
                    dve.sem_inc(y_free, 1)
                    dve.sem_inc(ys_ready, 1)

                def residual(b, chain):
                    dve.wait_ge(out_psum, b + 1)
                    for k in range(2):
                        rows = h[0:TT, bass.ds(b * NT + 3 * k, 3), :]
                        chain.add(nc.vector.tensor_tensor(rows, rows, psum[6 + k][0:TT, 0:3 * D].rearrange(
                            "p (t d) -> p t d", d=D), ALU.add))
                    chain.settle()
                    dve.sem_inc(out_free, 1)

                def statistics(b, chain):
                    for t in range(NT):
                        chain.add(nc.vector.bn_stats(stats[0:TT, bass.ds(b * NT + t, 1), :],
                                                     h[0:TT, bass.ds(b * NT + t, 1), :]))
                    chain.settle()

                def weights(b, s, chain):
                    g, j = divmod(s, NT)
                    dve.wait_ge(att_free, 4 * SETS * b + (4 * s + 4 + 2))
                    v = n3[0:TT, bass.ds(b * NT + j, 1), g * 64:(g + 1) * 64].rearrange("p o (q f) -> p (o q) f", f=F)
                    dve.wait_ge(e_free, SETS * b + (s + 1))
                    slot = s % EBUFS
                    chain.add(nc.vector.tensor_copy(values[0:TT, slot, :, 0, :], v))
                    chain.link(nc.vector.reciprocal(rz[0:TT, slot, :], z[0:TT, slot, :]))
                    z_inv = rz[0:TT, slot, :].unsqueeze(2).broadcast_to([TT, 4, F])
                    chain.link(nc.vector.tensor_tensor(values[0:TT, slot, :, 1, :], v, z_inv, ALU.mult))
                    dve.sem_inc(values_ready, 1)
                    chain.link(nc.vector.tensor_copy(scales[0:TT, g, j, :, 0, :], z_inv))
                    dve.sem_inc(scales_ready, 1)

                counted = []

                def body(b, first):
                    chain = Chain(dve, dve_done) if first else Chain(dve, dve_done, counted[0] + per_batch * (b - 1))
                    for s in range(SETS):
                        if s == NT:
                            turned_scales(b, 0, chain)
                        if s == 0 and not first:
                            turned_scales(b - 1, 1, chain)
                        weights(b, s, chain)
                        if s == NT:
                            scaled(b, 0, chain)
                        if s == 0 and not first:
                            scaled(b - 1, 1, chain)
                        if s == 3 and not first:
                            residual(b - 1, chain)
                        if s == 4 and not first:
                            statistics(b - 1, chain)
                    if first:
                        counted.append(chain.n)
                    else:
                        assert chain.n == per_batch
                end_of_batch = 2 + 2 + 2 + NT
                per_batch = 4 * SETS + 4 + end_of_batch
                batches(dve, body)
                assert counted[0] == per_batch - end_of_batch
                chain = Chain(dve, dve_done, counted[0] + per_batch * (B - 1))
                turned_scales(B - 1, 1, chain)
                scaled(B - 1, 1, chain)
                residual(B - 1, chain)
                statistics(B - 1, chain)


def normalized_tiles(nc, dve, chain, xn, h, mean, rstd, batch):
    for t in range(NT):
        col = batch * NT + t
        chain.add(nc.vector.tensor_scalar(
            xn[0:TT, t, :], h[0:TT, bass.ds(col, 1), :], mean[0:TT, bass.ds(col, 1)],
            rstd[0:TT, bass.ds(col, 1)], ALU.subtract, ALU.mult))
    chain.settle()


def expert_of_batch(nc, io, h, stats, mean, rstd, psum, ident, ones):
    NE = 16
    with Memory(nc, "expert_of_batch") as m:
        xn = m.sbuf("xn", [128, 2, NT, D])
        xnT = m.sbuf("xnT", [128, B, L])
        sums = m.sbuf("sums", [128, B, 2])
        wg = m.sbuf("wg", [128, NE])
        bg = m.sbuf("bg", [1, NE])
        scores = m.sbuf("scores", [1, B, NE])
        best = m.sbuf("best", [1, B])
        picks = m.sbuf("picks", [1, B, NE])
        countdown = m.sbuf("countdown", [1, NE])
        gate = m.sbuf("gate", [1, B])
        index = m.sbuf("index", [1, B], I32)
        gates = m.sbuf("gates", [128, B])
        w_sel = m.sbuf("w_sel", [128, B, D])
        b_sel = m.sbuf("b_sel", [1, B, D])
        w_gated = m.sbuf("w_gated", [128, 2, D])
        b_gated = m.sbuf("b_gated", [1, 2, D])
        xT = m.sbuf("xT", [128, 2, L])
        loaded, xn_ready, xnT_psum, xnT_ready, scores_psum = (
            m.sem(s) for s in ("loaded", "xn_ready", "xnT_psum", "xnT_ready", "scores_psum"))
        dve_chain, exp_in, exp_out, index_ready, picked, gates_psum = (
            m.sem(s) for s in ("dve_chain", "exp_in", "exp_out", "index_ready", "picked", "gates_psum"))
        gates_ready, gated_ready, xT_ready, xT_free, y_psum, y_free = (
            m.sem(s) for s in ("gates_ready", "gated_ready", "xT_ready", "xT_free", "y_psum", "y_free"))
        with nc.Block() as block:
            @block.sync
            def _(sp):
                sp.dma_start(wg[:], io["moe0_wg"]).then_inc(loaded, 16)
                sp.dma_start(bg[:], io["moe0_bg"]).then_inc(loaded, 16)
                sp.dma_start(countdown[:], io["countdown"]).then_inc(loaded, 16)
                sp.wait_ge(index_ready, 1)
                for b in range(B):
                    e = sp.value_load(index[0:1, b:b + 1], min_val=0, max_val=NE - 1)
                    sp.dma_start(w_sel[:, b, :], io["moe0_we"][bass.ds(e, 1), :, :].rearrange("o p n -> p (o n)")
                                 ).then_inc(picked, 16)
                    sp.dma_start(b_sel[:, b, :], io["moe0_be"][bass.ds(e, 1), :]).then_inc(picked, 16)

            @block.tensor
            def _(pe):
                with pe.Fori(0, B // 2) as i:
                    for u in range(2):
                        pe.wait_ge(xn_ready, 2 * i + (u + 1))
                        pe.wait_ge(xT_free, 2 * i + (u + 1))
                        for t in range(NT):
                            mm = nc.tensor.transpose(psum[2 * u + t // 3][:, (t % 3) * TT:(t % 3 + 1) * TT],
                                                     xn[0:TT, u, t, :], ident[0:TT, 0:TT])
                        mm.then_inc(xnT_psum, 1)
                pe.wait_ge(xnT_ready, 2 * B)
                pe.wait_ge(loaded, 48)
                for b in range(B):
                    for half in range(2):
                        mm = nc.tensor.matmul(psum[4][0:1, b * NE:(b + 1) * NE], sums[:, b, half:half + 1], wg[:],
                                              start=(half == 0), stop=(half == 1))
                mm.then_inc(scores_psum, 1)
                pe.wait_ge(gates_ready, 1)
                nc.tensor.matmul(psum[5][:, 0:B], ones[0:1, :], gate[:], start=True, stop=True).then_inc(gates_psum, 1)
                with pe.Fori(0, B // 2) as i:
                    for u in range(2):
                        pe.wait_ge(gated_ready, 2 * i + (u + 1))
                        pe.wait_ge(xT_ready, 2 * i + (u + 1))
                        pe.wait_ge(y_free, 2 * i + (u + 1))
                        for t in range(NT):
                            out = psum[2 * u + t // 3][0:TT, (t % 3) * D:(t % 3 + 1) * D]
                            nc.tensor.matmul(out, ones[0:1, 0:TT], b_gated[:, u, :], start=True, stop=False)
                            mm = nc.tensor.matmul(out, xT[:, u, t * TT:(t + 1) * TT], w_gated[:, u, :],
                                                  start=False, stop=True)
                        mm.then_inc(y_psum, 1)

            @block.scalar
            def _(act):
                act.sem_inc(xT_free, 2)
                with act.Fori(0, B // 2) as i:
                    for u in range(2):
                        act.wait_ge(xnT_psum, 2 * i + (u + 1))
                        for half in range(2):
                            nc.scalar.activation(
                                xnT[:, bass.ds(2 * i + u, 1), half * HALF:(half + 1) * HALF],
                                psum[2 * u + half][:, 0:HALF], ACT.Identity,
                                accum_out=sums[:, bass.ds(2 * i + u, 1), half:half + 1].rearrange("p a b -> p (a b)")
                            ).then_inc(xnT_ready, 1)
                        act.wait_ge(xnT_ready, 2 * (2 * i + u) + 2)
                        act.sem_inc(xT_free, 1)
                act.wait_ge(exp_in, 1)
                nc.scalar.activation(picks[:], scores[:], ACT.Exp).then_inc(exp_out, 1)
                with act.Fori(0, B // 2) as i:
                    for u in range(2):
                        act.wait_ge(y_free, 2 * i + (u + 1))
                        act.sem_inc(xT_free, 1)
                        nc.scalar.activation(xT[:, u, :], xnT[:, bass.ds(2 * i + u, 1), :],
                                             ACT.Identity).then_inc(xT_ready, 1)

            @block.vector
            def _(dve):
                with dve.Fori(0, B // 2) as i:
                    chain = Chain(dve, dve_chain, 2 * NT * i)
                    for u in range(2):
                        dve.wait_ge(xT_free, 2 * i + (u + 1))
                        normalized_tiles(nc, dve, chain, xn[:, u], h, mean, rstd, 2 * i + u)
                        dve.sem_inc(xn_ready, 1)
                chain = Chain(dve, dve_chain, NTILES)
                dve.wait_ge(scores_psum, 1)
                wide = best[:].unsqueeze(2).broadcast_to([1, B, NE])
                chain.link(nc.vector.scalar_tensor_tensor(
                    out=scores[:], in0=psum[4][0:1, 0:B * NE].rearrange("p (b e) -> p b e", e=NE), scalar=1.0 / L,
                    in1=bg[:].unsqueeze(1).broadcast_to([1, B, NE]), op0=ALU.mult, op1=ALU.add))
                chain.link(nc.vector.tensor_reduce(best[:], scores[:], AX.X, ALU.max))
                chain.link(nc.vector.tensor_tensor(scores[:], scores[:], wide, ALU.subtract))
                dve.sem_inc(exp_in, 1)
                dve.wait_ge(exp_out, 1)
                chain.link(nc.vector.tensor_reduce(gate[:], picks[:], AX.X, ALU.add))
                chain.link(nc.vector.reciprocal(gate[:], gate[:]))
                dve.sem_inc(gates_ready, 1)
                chain.link(nc.vector.tensor_scalar(picks[:], scores[:], 0.0, None, ALU.is_ge))
                chain.link(nc.vector.tensor_tensor(picks[:], picks[:], countdown[:].unsqueeze(1).broadcast_to([1, B, NE]), ALU.mult))
                chain.link(nc.vector.tensor_reduce(best[:], picks[:], AX.X, ALU.max))
                chain.link(nc.vector.tensor_scalar(index[:], best[:], -1.0, float(NE), ALU.mult, ALU.add))
                dve.sem_inc(index_ready, 1)
                dve.wait_ge(gates_psum, 1)
                chain.link(nc.vector.tensor_copy(gates[:], psum[5][:, 0:B]))
                dve.wait_ge(picked, 32 * B)
                dve.sem_inc(y_free, 2)
                after = NTILES + chain.n
                with dve.Fori(0, B // 2) as i:
                    chain = Chain(dve, dve_chain, after + 2 * (4 + NT) * i)
                    for u in range(2):
                        b = 2 * i + u
                        chain.add(nc.vector.tensor_scalar(w_gated[:, u, :], w_sel[:, bass.ds(b, 1), :],
                                                          gates[:, bass.ds(b, 1)], None, ALU.mult))
                        chain.add(nc.vector.tensor_scalar(b_gated[:, u, :], b_sel[:, bass.ds(b, 1), :],
                                                          gates[0:1, bass.ds(b, 1)], None, ALU.mult))
                        chain.settle()
                        dve.sem_inc(gated_ready, 1)
                    for u in range(2):
                        dve.wait_ge(y_psum, 2 * i + (u + 1))
                        for k in range(2):
                            rows = h[0:TT, bass.ds((2 * i + u) * NT + 3 * k, 3), :]
                            chain.add(nc.vector.tensor_tensor(rows, rows, psum[2 * u + k][0:TT, 0:3 * D].rearrange(
                                "p (t d) -> p t d", d=D), ALU.add))
                        chain.settle()
                        dve.sem_inc(y_free, 1)
                        for t in range(NT):
                            chain.add(nc.vector.bn_stats(stats[0:TT, bass.ds((2 * i + u) * NT + t, 1), :],
                                                         h[0:TT, bass.ds((2 * i + u) * NT + t, 1), :]))
                        chain.settle()
                    assert chain.n == 2 * (4 + NT)


C = 10
SUB = C // 2
NCH = L // C
HALVES = [(0, 38 * C), (38 * C, L)]
NCOEF = 3 * SUB * SUB


def delta_projections(nc, io, h, mean, rstd, kq_all, v_all, beta, k_rows_dram, psum, ident):
    with Memory(nc, "proj") as m:
        w_kq = m.sbuf("w_kq", [128, 2 * D])
        w_v = m.sbuf("w_v", [128, D])
        w_b = m.sbuf("w_b", [128, D])
        xn = m.sbuf("xn", [128, NT, D])
        xnT = m.sbuf("xnT", [128, L])
        sq = m.sbuf("sq", [128, NT, 2 * D])
        norm = m.sbuf("norm", [128, NT * 2 * H])
        kqn = m.sbuf("kqn", [128, NT, 2 * D])
        turned = m.sbuf("turned", [128, 2, L])
        names = ("loaded xn_ready xnT_psum xnT_ready v_psum v_taken kq_psum sq_ready norm_sq norm_ready kqn_ready "
                 "b_psum b_taken kT_psum kT_ready kT_taken k_stored k_free dve_chain act_chain batch_done")
        s = {n: m.sem(n) for n in names.split()}
        with nc.Block() as block:
            @block.sync
            def _(sp):
                sp.dma_start(w_kq[:, 0:D], io["wk"]).then_inc(s["loaded"], 16)
                sp.dma_start(w_kq[:, D:2 * D], io["wq"]).then_inc(s["loaded"], 16)
                sp.dma_start(w_v[:], io["wv"]).then_inc(s["loaded"], 16)
                sp.dma_start(w_b[:], io["wb"]).then_inc(s["loaded"], 16)
                sp.sem_inc(s["k_free"], 1)
                with sp.Fori(0, B) as b:
                    sp.wait_ge(s["kqn_ready"], b + 1)
                    sp.dma_start(k_rows_dram[bass.ds(b, 1), :, :].rearrange("o (t p) d -> p (o t) d", p=TT),
                                 kqn[0:TT, :, 0:D]).then_inc(s["k_stored"], 16)
                    sp.wait_ge(s["k_stored"], 16 * b + 16)
                    sp.sem_inc(s["k_free"], 1)

            @block.tensor
            def _(pe):
                pe.wait_ge(s["loaded"], 64)
                with pe.Fori(0, B) as b:
                    pe.wait_ge(s["xn_ready"], b + 1)
                    pe.wait_ge(s["kT_taken"], 2 * b + 2)
                    for t in range(NT):
                        mm = nc.tensor.transpose(psum[t // 3][:, (t % 3) * TT:(t % 3 + 1) * TT],
                                                 xn[0:TT, t, :], ident[0:TT, 0:TT])
                    mm.then_inc(s["xnT_psum"], 1)
                    pe.wait_ge(s["xnT_ready"], 2 * b + 2)
                    for t in range(NT):
                        mm = nc.tensor.matmul(psum[2 + t // 2][0:TT, (t % 2) * 2 * D:(t % 2 + 1) * 2 * D],
                                              xnT[:, t * TT:(t + 1) * TT], w_kq[:], start=True, stop=True)
                    mm.then_inc(s["kq_psum"], 1)
                    for half, (lo, hi) in enumerate(HALVES):
                        mm = nc.tensor.matmul(psum[5 + half][:, 0:hi - lo], w_v[:], xnT[:, lo:hi], start=True, stop=True)
                    mm.then_inc(s["v_psum"], 1)
                    for half, (lo, hi) in enumerate(HALVES):
                        mm = nc.tensor.matmul(psum[half][:, 0:hi - lo], w_b[:], xnT[:, lo:hi], start=True, stop=True)
                    mm.then_inc(s["b_psum"], 1)
                    pe.wait_ge(s["kqn_ready"], b + 1)
                    for which in range(2):
                        pe.wait_ge(s["v_taken" if which == 0 else "b_taken"], b + 1)
                        base = 5 if which == 0 else 0
                        for t in range(NT):
                            mm = nc.tensor.transpose(psum[base + t // 3][:, (t % 3) * TT:(t % 3 + 1) * TT],
                                                     kqn[0:TT, t, which * D:(which + 1) * D], ident[0:TT, 0:TT])
                        mm.then_inc(s["kT_psum"], 1)

            @block.scalar
            def _(act):
                act.sem_inc(s["kT_taken"], 2)
                with act.Fori(0, B) as b:
                    act.wait_ge(s["xnT_psum"], b + 1)
                    for half in range(2):
                        nc.scalar.activation(xnT[:, half * HALF:(half + 1) * HALF], psum[half][:, 0:HALF],
                                             ACT.Identity).then_inc(s["xnT_ready"], 1)
                    act.wait_ge(s["kq_psum"], b + 1)
                    for k in range(3):
                        ins = nc.scalar.activation(sq[0:TT, 2 * k:2 * k + 2, :], psum[2 + k][0:TT, :], ACT.Square)
                    ins.then_inc(s["sq_ready"], 1)
                    act.wait_ge(s["b_psum"], b + 1)
                    for half, (lo, hi) in enumerate(HALVES):
                        ins = nc.scalar.activation(beta[:, bass.ds(b, 1), lo:hi], psum[half][:, 0:hi - lo], ACT.Identity)
                    ins.then_inc(s["b_taken"], 1)
                    act.wait_ge(s["norm_sq"], b + 1)
                    nc.scalar.activation(norm[0:TT, :], norm[0:TT, :], ACT.Sqrt).then_inc(s["norm_ready"], 1)
                    for which in range(2):
                        act.wait_ge(s["kT_psum"], 2 * b + which + 1)
                        base = 5 if which == 0 else 0
                        for half in range(2):
                            nc.scalar.activation(turned[:, which, half * HALF:(half + 1) * HALF],
                                                 psum[base + half][:, 0:HALF], ACT.Identity).then_inc(s["kT_ready"], 1)
                        act.wait_ge(s["kT_ready"], 4 * b + 2 * which + 2)
                        act.sem_inc(s["kT_taken"], 1)
                act.wait_ge(s["b_taken"], B)
                nc.scalar.activation(beta[:], beta[:], ACT.Sigmoid).then_inc(s["act_chain"], 1)

            @block.vector
            def _(dve):
                with dve.Fori(0, B) as b:
                    chain = Chain(dve, s["dve_chain"], 15 * b)
                    if True:
                        normalized_tiles(nc, dve, chain, xn, h, mean, rstd, b)
                        dve.sem_inc(s["xn_ready"], 1)
                    dve.wait_ge(s["sq_ready"], b + 1)
                    chain.link(nc.vector.tensor_reduce(norm[0:TT, :], sq[0:TT, :, :].rearrange("p t (g f) -> p (t g) f", f=F),
                                                       AX.X, ALU.add))
                    dve.sem_inc(s["norm_sq"], 1)
                    dve.wait_ge(s["v_psum"], b + 1)
                    for half, (lo, hi) in enumerate(HALVES):
                        chain.add(nc.vector.tensor_copy(
                            v_all[:, lo // C:hi // C, bass.ds(b, 1), :].rearrange("p c o t -> p c (o t)"),
                            psum[5 + half][:, 0:hi - lo].rearrange("p (c t) -> p c t", t=C)))
                    chain.settle()
                    dve.sem_inc(s["v_taken"], 1)
                    dve.wait_ge(s["norm_ready"], b + 1)
                    chain.link(nc.vector.reciprocal(norm[0:TT, :], norm[0:TT, :]))
                    dve.wait_ge(s["k_free"], b + 1)
                    for k in range(3):
                        chain.add(nc.vector.tensor_tensor(
                            kqn[0:TT, 2 * k:2 * k + 2, :].rearrange("p t (g f) -> p (t g) f", f=F),
                            psum[2 + k][0:TT, :].rearrange("p (g f) -> p g f", f=F),
                            spread(norm[0:TT, 32 * k:32 * k + 32], F), ALU.mult))
                    chain.settle()
                    dve.sem_inc(s["kqn_ready"], 1)
                    for which in range(2):
                        dve.wait_ge(s["kT_ready"], 4 * b + 2 * which + 2)
                        chain.add(nc.vector.tensor_copy(
                            kq_all[:, :, bass.ds(b, 1), which, :].rearrange("p c o t -> p c (o t)"),
                            turned[:, which, :].rearrange("p (c t) -> p c t", t=C)))
                    chain.settle()
                    assert chain.n == 15


def triangular_coefficients(nc, kq_all, beta, coef_dram, psum, block_sum):
    with Memory(nc, "coef") as m:
        products = m.sbuf("products", [128, 2, L])
        inv = m.sbuf("inv", [128, NCH, 2, SUB, SUB])
        neg = m.sbuf("neg", [128, NCH, 2, SUB, SUB])
        cross = m.sbuf("cross", [128, NCH, SUB * SUB])
        out = m.sbuf("out", [128, NCH, NCOEF])
        term = m.sbuf("term", [128, NCH, 2, SUB])
        names = "products_ready products_free dots_psum dots_free dve_chain pool_chain cross_ready cross_free out_ready out_free stored gate"
        s = {n: m.sem(n) for n in names.split()}
        groups = []
        for d in range(1, C):
            width = C - d
            per = 512 // width
            for lo in range(0, NCH, per):
                groups.append((d, width, lo, min(NCH, lo + per)))
        ND = C - 1
        RING = 6
        assert len(groups) % RING == 0

        with nc.Block() as block:
            @block.sync
            def _(sp):
                sp.sem_inc(s["out_free"], 1)
                with sp.Fori(0, B) as b:
                    sp.wait_ge(s["out_ready"], b + 1)
                    sp.dma_start(coef_dram[bass.ds(b, 1), :, :, :].rearrange("o p c k -> p (o c) k"),
                                 out[:]).then_inc(s["stored"], 16)
                    sp.wait_ge(s["stored"], 16 * b + 16)
                    sp.sem_inc(s["out_free"], 1)

            @block.gpsimd
            def _(pool):
                with pool.Fori(0, B) as b:
                    for d in range(1, C):
                        pass_gate(pool, s["products_free"], ND * b + d + (d == 1), s["gate"])
                        width = C - d
                        nc.gpsimd.tensor_tensor(
                            products[:, d % 2, 0:NCH * width].rearrange("p (c t) -> p c t", t=width),
                            kq_all[:, :, bass.ds(b, 1), 0, d:C].rearrange("p c o t -> p c (o t)"),
                            kq_all[:, :, bass.ds(b, 1), 0, 0:width].rearrange("p c o t -> p c (o t)"),
                            ALU.mult).then_inc(s["products_ready"], 1)

            @block.tensor
            def _(pe):
                pe.sem_inc(s["products_free"], 2)
                with pe.Fori(0, B) as b:
                    for n, (d, width, lo, hi) in enumerate(groups):
                        if lo == 0:
                            pe.wait_ge(s["products_ready"], ND * b + d)
                        pe.wait_ge(s["dots_free"], len(groups) * b + n + 1)
                        nc.tensor.matmul(psum[n % RING][:, 0:(hi - lo) * width], block_sum[:],
                                         products[:, d % 2, lo * width:hi * width], start=True, stop=True
                                         ).then_inc(s["dots_psum"], 1)
                        if hi == NCH:
                            pe.wait_ge(s["dots_psum"], len(groups) * b + n + 1)
                            pe.sem_inc(s["products_free"], 1)

            @block.scalar
            def _(act):
                act.sem_inc(s["cross_free"], 1)
                with act.Fori(0, B) as b:
                    act.wait_ge(s["cross_ready"], b + 1)
                    act.wait_ge(s["out_free"], b + 1)
                    nc.scalar.activation(out[:, :, SUB * SUB:2 * SUB * SUB], cross[:], ACT.Identity
                                         ).then_inc(s["cross_free"], 1)

            @block.vector
            def _(dve):
                first = Chain(dve, s["dve_chain"])
                first.add(nc.vector.memset(inv[:], 0.0))
                first.add(nc.vector.memset(neg[:], 0.0))
                first.settle()
                for t in range(SUB):
                    first.add(nc.vector.memset(inv[:, :, :, t, t], 1.0))
                first.settle()
                dve.sem_inc(s["dots_free"], RING)

                def batch(b, base):
                    chain = Chain(dve, s["dve_chain"], base)
                    dve.wait_ge(s["cross_free"], b + 1)
                    for n, (d, width, lo, hi) in enumerate(groups):
                        dve.wait_ge(s["dots_psum"], len(groups) * b + n + 1)
                        dots = psum[n % RING][:, 0:(hi - lo) * width].rearrange("p (c t) -> p c t", t=width)
                        before = chain.n
                        for part in range(2):
                            k = SUB - d
                            if k <= 0:
                                continue
                            dst = neg[:, lo:hi, part, :, :].rearrange("p c t s -> p c (t s)")[:, :, d * SUB:d * SUB + (k - 1) * (SUB + 1) + 1:SUB + 1]
                            times = beta[:, bass.ds(b, 1), :].rearrange("p o (c t) -> p (o c) t", t=C)[:, lo:hi, part * SUB + d:part * SUB + SUB]
                            chain.add(nc.vector.scalar_tensor_tensor(
                                out=dst, in0=dots[:, :, part * SUB:part * SUB + k], scalar=-1.0, in1=times,
                                op0=ALU.mult, op1=ALU.mult))
                        s0, s1 = max(0, SUB - d), min(SUB, C - d)
                        t0 = s0 + d - SUB
                        at = t0 * SUB + s0
                        dst = cross[:, lo:hi, at:at + (s1 - s0 - 1) * (SUB + 1) + 1:SUB + 1]
                        chain.add(nc.vector.tensor_scalar(dst, dots[:, :, s0:s1], -1.0, None, ALU.mult))
                        if n > 0:
                            dve.wait_ge(s["dve_chain"], base + before)
                            dve.sem_inc(s["dots_free"], 1)
                    chain.settle()
                    dve.sem_inc(s["dots_free"], 1)
                    dve.sem_inc(s["cross_ready"], 1)
                    flat_inv = inv[:].rearrange("p c a t s -> p (c a) t s")
                    flat_neg = neg[:].rearrange("p c a t s -> p (c a) t s")
                    flat_term = term[:].rearrange("p c a s -> p (c a) s")
                    NB = 2 * NCH
                    for t in range(1, SUB):
                        chain.add(nc.vector.tensor_copy(flat_inv[:, :, t, 0:t], flat_neg[:, :, t, 0:t]))
                    chain.settle()
                    for t in range(1, SUB):
                        for r in range(1, t):
                            chain.link(nc.vector.tensor_tensor(
                                flat_term[:, :, 0:r], flat_inv[:, :, r, 0:r],
                                flat_neg[:, :, t, r:r + 1].broadcast_to([128, NB, r]), ALU.mult))
                            chain.link(nc.vector.tensor_tensor(
                                flat_inv[:, :, t, 0:r], flat_inv[:, :, t, 0:r], flat_term[:, :, 0:r], ALU.add))
                    dve.wait_ge(s["out_free"], b + 1)
                    for part in range(2):
                        beta_s = beta[:, bass.ds(b, 1), :].rearrange("p o (c t) -> p (o c) t", t=C)[:, :, part * SUB:(part + 1) * SUB]
                        at = 2 * SUB * SUB * part
                        chain.add(nc.vector.tensor_tensor(
                            out[:, :, at:at + SUB * SUB].rearrange("p c (t s) -> p c t s", s=SUB), inv[:, :, part],
                            beta_s.unsqueeze(2).broadcast_to([128, NCH, SUB, SUB]), ALU.mult))
                    chain.settle()
                    dve.wait_ge(s["cross_free"], b + 2)
                    dve.sem_inc(s["out_ready"], 1)
                    return chain.n

                per = sum(1 + 2 * (SUB - d > 0) for d, _, _, _ in groups) + (SUB - 1) + 2 * sum(t - 1 for t in range(1, SUB)) + 2
                with dve.Fori(0, B) as b:
                    assert batch(b, first.n + per * b) == per


RING = 3
STREAMS = 2
BS = B // STREAMS


def delta_rule(nc, io, kq_all, v_all, u_all, o_all, k_rows_dram, coef_dram, psum_banks, psum):
    with Memory(nc, "delta") as m:
        masks = m.sbuf("masks", [128, 2])
        kq = m.sbuf("kq", [128, RING, B, 2 * C])
        k_rows = m.sbuf("k_rows", [128, RING, B, 32])
        coef = m.sbuf("coef", [128, 2, B, RING, NCOEF])
        state = m.sbuf("state", [128, B, 32])
        r = m.sbuf("r", [128, STREAMS, BS, SUB])
        prod = m.sbuf("prod", [128, STREAMS, BS, SUB, SUB])
        coupling = m.sbuf("coupling", [128, STREAMS, BS, SUB, SUB + 1])
        coupled = m.sbuf("coupled", [128, STREAMS, BS, SUB])
        u_pad = m.sbuf("u_pad", [128, RING, B, 32])
        u_rows = m.sbuf("u_rows", [128, RING, B, 32])
        loaded, gate, pool_gate, zeroed = m.sem("loaded"), m.sem("gate"), m.sem("pool_gate"), m.sem("zeroed")
        kq_ready, kq_free = m.sem("kq_ready"), m.sem("kq_free")
        rows_free = m.sem("rows_free")
        rows_ready = [m.sem(f"rows_ready{u}") for u in range(RING)]
        coef_ready = [m.sem(f"coef_ready{k}") for k in range(2)]
        coef_free = m.sem("coef_free")
        r_psum = [m.sem(f"r_psum{x}") for x in range(STREAMS)]
        u_ready = [m.sem(f"u_ready{x}") for x in range(STREAMS)]
        s_psum = [m.sem(f"s_psum{x}") for x in range(STREAMS)]
        s_ready = [m.sem(f"s_ready{x}") for x in range(STREAMS)]
        q_taken = [m.sem(f"q_taken{x}") for x in range(STREAMS)]
        r_taken = [m.sem(f"r_taken{x}") for x in range(STREAMS)]
        act_gate = m.sem("act_gate")
        u_kept = m.sem("u_kept")
        dve_chain = m.sem("dve_chain")
        SOLVE = 9

        def own(x):
            return slice(x * BS, (x + 1) * BS)

        def chunks(eng, body):
            for u in range(RING):
                body(u, u, u == 0, 0, 0, 1)
            with eng.Fori(0, (NCH - RING) // (2 * RING)) as i:
                for k in range(2):
                    for u in range(RING):
                        body(2 * RING * i + (RING * (k + 1) + u), u, False, 2 * i + (k + 1), 1 - k, i + (k + 1))

        with nc.Block() as block:
            @block.sync
            def _(sp):
                sp.dma_start(masks[:], io["pair_masks"]).then_inc(loaded, 16)

                def body(c, u, first, turn, half, uses):
                    sp.wait_ge(rows_free, c + 1)
                    for w in range(4):
                        src = k_rows_dram[:, bass.ds(c * C, C), 32 * w:32 * w + 32].rearrange("b t k -> t b k")
                        sp.dma_start(k_rows[32 * w:32 * w + C, u, :, :], src).then_inc(rows_ready[u], 16)
                    if u == 0:
                        sp.wait_ge(coef_free, turn + 1)
                        sp.dma_start(coef[:, half].rearrange("p b c k -> p b (c k)"),
                                     coef_dram[:, :, bass.ds(c, RING), :].rearrange("b p c k -> p b (c k)")
                                     ).then_inc(coef_ready[half], 16)
                chunks(sp, body)

            @block.gpsimd
            def _(pool):
                def body(c, u, first, turn, half, uses):
                    pass_gate(pool, kq_free, c + 1, pool_gate)
                    nc.gpsimd.tensor_copy(kq[:, u, :, :], kq_all[:, bass.ds(c, 1), :, :, :].rearrange(
                        "p o b a t -> p (o b) (a t)")).then_inc(kq_ready, 1)
                    if not first:
                        keep_u(c - 1, (u - 1) % RING)

                def keep_u(c, u):
                    pool.wait_ge(u_ready[0], c + 1)
                    pass_gate(pool, u_ready[1], c + 1, pool_gate)
                    nc.gpsimd.tensor_copy(u_all[:, bass.ds(c, 1), :, :].rearrange("p o b t -> p (o b) t"),
                                          u_pad[:, u, :, 0:C]).then_inc(u_kept, 1)
                pool.sem_inc(u_kept, RING)
                chunks(pool, body)
                keep_u(NCH - 1, RING - 1)

            @block.tensor
            def _(pe):
                pe.sem_inc(rows_free, RING)
                pe.sem_inc(kq_free, RING)
                pe.wait_ge(zeroed, 1)
                for w in range(4):
                    nc.tensor.matmul(psum[6][32 * w:32 * w + 32, 0:32 * B], state[32 * w:32 * w + 32, 0, :],
                                     state[32 * w:32 * w + 32, :, :].rearrange("p b k -> p (b k)"),
                                     start=True, stop=False, skip_group_check=True)
                for w in range(4):
                    nc.tensor.matmul(psum[7][32 * w:32 * w + 32, 0:32 * B], state[32 * w:32 * w + 32, 0, :],
                                     state[32 * w:32 * w + 32, :, :].rearrange("p b k -> p (b k)"),
                                     start=True, stop=False, skip_group_check=True)

                def residuals(c, u, x):
                    if x == 0:
                        pe.wait_ge(kq_ready, c + 1)
                    pe.wait_ge(q_taken[x], c + 1)
                    pass_gate(pe, s_ready[x], c + 1, gate)
                    for b in range(x * BS, (x + 1) * BS):
                        for w in range(4):
                            rows = slice(32 * w, 32 * w + 32)
                            mm = nc.tensor.matmul(psum[RING * x + u][rows, 2 * C * b:2 * C * (b + 1)], state[rows, b, :],
                                                  kq[rows, u, b, :], start=True, stop=True)
                    mm.then_inc(r_psum[x], 1)

                def add_updates(c, u, x, turn):
                    if x == 0:
                        pe.wait_ge(rows_ready[u], 64 * turn + 64)
                    pass_gate(pe, u_ready[x], c + 1, gate)
                    for b in range(x * BS, (x + 1) * BS):
                        for w in range(4):
                            rows = slice(32 * w, 32 * w + C)
                            mm = nc.tensor.matmul(psum[6 + x][32 * w:32 * w + 32, 32 * b:32 * b + 32], k_rows[rows, u, b, :],
                                                  u_rows[rows, u, b, :], start=False, stop=False, skip_group_check=True)
                    mm.then_inc(s_psum[x], 1)
                    if x == 1:
                        pass_gate(pe, s_psum[x], c + 1, gate)
                        pe.sem_inc(rows_free, 1)
                        pe.sem_inc(kq_free, 1)

                def body(c, u, first, turn, half, uses):
                    residuals(c, u, 0)
                    if not first:
                        add_updates(c - 1, (u - 1) % RING, 1, None)
                    residuals(c, u, 1)
                    add_updates(c, u, 0, turn)
                chunks(pe, body)
                add_updates(NCH - 1, RING - 1, 1, None)

            @block.scalar
            def _(act):
                act.wait_ge(loaded, 16)
                act.wait_ge(zeroed, 1)
                for x in range(STREAMS):
                    act.sem_inc(s_ready[x], 1)
                    act.sem_inc(q_taken[x], RING)

                def keep_q(c, u, x):
                    pass_gate(act, r_taken[x], c + 1, act_gate)
                    nc.scalar.activation(
                        o_all[:, bass.ds(c, 1), own(x), :].rearrange("p o b t -> p (o b) t"),
                        psum[RING * x + u][:, 2 * C * BS * x:2 * C * BS * (x + 1)].rearrange(
                            "p (b a) -> p b a", a=2 * C)[:, :, C:2 * C], ACT.Identity).then_inc(q_taken[x], 1)

                def new_state(c, x):
                    act.wait_ge(s_psum[x], c + 1)
                    for head in range(2):
                        ins = nc.scalar.activation(
                            state[:, own(x), F * head:F * head + F],
                            psum[6 + x][:, 32 * BS * x:32 * BS * (x + 1)].rearrange("p (b k) -> p b k", k=32)[:, :, F * head:F * head + F],
                            ACT.Identity, scale=masks[:, head:head + 1])
                    ins.then_inc(s_ready[x], 1)

                def body(c, u, first, turn, half, uses):
                    if not first:
                        new_state(c - 1, 1)
                    keep_q(c, u, 0)
                    new_state(c, 0)
                    keep_q(c, u, 1)
                chunks(act, body)

            @block.vector
            def _(dve):
                zero = Chain(dve, zeroed)
                zero.add(nc.vector.memset(state[:], 0.0))
                nc.vector.memset(u_pad[:], 0.0).then_inc(dve_chain, 1)
                dve.sem_inc(coef_free, 2)

                def body(c, u, first, turn, half, uses):
                    chain = Chain(dve, dve_chain, STREAMS * SOLVE * c + 1)
                    for x in range(STREAMS):
                        dve.wait_ge(r_psum[x], c + 1)
                        if x == 0:
                            dve.wait_ge(coef_ready[half], 16 * uses)
                            dve.wait_ge(u_kept, c + 1)
                        b = own(x)
                        r_x, p_x, w_x, terms = r[:, x], prod[:, x], coupled[:, x], coupling[:, x]
                        inv1, cross, inv2 = (coef[:, half, b, u, k * SUB * SUB:(k + 1) * SUB * SUB].rearrange(
                            "p b (t s) -> p b t s", s=SUB) for k in range(3))

                        def along(values):
                            return values.unsqueeze(2).broadcast_to([128, BS, SUB, SUB])

                        def residual(out, lo, hi):
                            return nc.vector.tensor_tensor(
                                out, v_all[:, bass.ds(c, 1), b, lo:hi].rearrange("p o b t -> p (o b) t"),
                                psum[RING * x + u][:, 2 * C * BS * x:2 * C * BS * (x + 1)].rearrange(
                                    "p (b a) -> p b a", a=2 * C)[:, :, lo:hi], ALU.subtract)
                        chain.add(residual(r_x, 0, SUB))
                        chain.link(residual(terms[:, :, :, SUB], SUB, C))
                        dve.sem_inc(r_taken[x], 1)
                        chain.link(nc.vector.tensor_tensor(p_x, inv1, along(r_x), ALU.mult))
                        chain.link(nc.vector.tensor_reduce(u_pad[:, u, b, 0:SUB], p_x, AX.X, ALU.add))
                        chain.link(nc.vector.tensor_tensor(terms[:, :, :, 0:SUB], cross, along(u_pad[:, u, b, 0:SUB]), ALU.mult))
                        chain.link(nc.vector.tensor_reduce(w_x, terms, AX.X, ALU.add))
                        chain.link(nc.vector.tensor_tensor(p_x, inv2, along(w_x), ALU.mult))
                        chain.link(nc.vector.tensor_reduce(u_pad[:, u, b, SUB:C], p_x, AX.X, ALU.add))
                        chain.link(nc.vector.transpose(u_rows[:, u, b, :].rearrange("p b k -> p (b k)"),
                                                       u_pad[:, u, b, :].rearrange("p b k -> p (b k)")))
                        dve.sem_inc(u_ready[x], 1)
                    if u == RING - 1:
                        dve.sem_inc(coef_free, 1)
                chunks(dve, body)


def within_chunks(nc, kq_all, u_all, o_all, psum, block_sum):
    BUFS = C // 2
    with Memory(nc, "within") as m:
        products = m.sbuf("products", [128, BUFS, L])
        terms = m.sbuf("terms", [128, 3, 512])
        names = "products_ready products_free dots_psum dots_free dve_chain gate"
        s = {n: m.sem(n) for n in names.split()}
        groups = []
        for d in range(C):
            width = C - d
            per = 512 // width
            for lo in range(0, NCH, per):
                groups.append((d, width, lo, min(NCH, lo + per)))
        BANKS = 7
        assert len(groups) % BANKS == 0 and C % 2 == 0

        with nc.Block() as block:
            @block.gpsimd
            def _(pool):
                with pool.Fori(0, B) as b:
                    for d in range(C):
                        pass_gate(pool, s["products_free"], C * b + d + 1, s["gate"])
                        width = C - d
                        nc.gpsimd.tensor_tensor(
                            products[:, d % BUFS, 0:NCH * width].rearrange("p (c t) -> p c t", t=width),
                            kq_all[:, :, bass.ds(b, 1), 1, d:C].rearrange("p c o t -> p c (o t)"),
                            kq_all[:, :, bass.ds(b, 1), 0, 0:width].rearrange("p c o t -> p c (o t)"),
                            ALU.mult).then_inc(s["products_ready"], 1)

            @block.tensor
            def _(pe):
                pe.sem_inc(s["products_free"], BUFS)
                with pe.Fori(0, B) as b:
                    for n, (d, width, lo, hi) in enumerate(groups):
                        if lo == 0:
                            pe.wait_ge(s["products_ready"], C * b + d + 1)
                        pe.wait_ge(s["dots_free"], len(groups) * b + n + 1)
                        nc.tensor.matmul(psum[n % BANKS][:, 0:(hi - lo) * width], block_sum[:],
                                         products[:, d % BUFS, lo * width:hi * width], start=True, stop=True
                                         ).then_inc(s["dots_psum"], 1)
                        if n > 0 and groups[n - 1][3] == NCH:
                            pe.wait_ge(s["dots_psum"], len(groups) * b + n)
                            pe.sem_inc(s["products_free"], 1)
                    pe.wait_ge(s["dots_psum"], len(groups) * b + len(groups))
                    pe.sem_inc(s["products_free"], 1)

            @block.vector
            def _(dve):
                dve.sem_inc(s["dots_free"], BANKS)
                with dve.Fori(0, B) as b:
                    chain = Chain(dve, s["dve_chain"], 2 * len(groups) * b)
                    for n in range(len(groups) + 1):
                        issued = chain.n
                        if n < len(groups):
                            d, width, lo, hi = groups[n]
                            dve.wait_ge(s["dots_psum"], len(groups) * b + n + 1)
                            dots = psum[n % BANKS][:, 0:(hi - lo) * width].rearrange("p (c t) -> p c t", t=width)
                            term = terms[:, n % 3, 0:(hi - lo) * width].rearrange("p (c t) -> p c t", t=width)
                            chain.add(nc.vector.tensor_tensor(term, dots, u_all[:, lo:hi, bass.ds(b, 1), 0:width].rearrange(
                                "p c o t -> p c (o t)"), ALU.mult))
                        if n > 0:
                            dve.wait_ge(s["dve_chain"], chain.base + issued)
                            dve.sem_inc(s["dots_free"], 1)
                            d, width, lo, hi = groups[n - 1]
                            term = terms[:, (n - 1) % 3, 0:(hi - lo) * width].rearrange("p (c t) -> p c t", t=width)
                            o = o_all[:, lo:hi, bass.ds(b, 1), d:C].rearrange("p c o t -> p c (o t)")
                            chain.add(nc.vector.tensor_tensor(o, o, term, ALU.add))
                    chain.settle()
                    assert chain.n == 2 * len(groups)


def delta_output(nc, io, h, stats, mean, rstd, o_all, psum, ident, ones):
    with Memory(nc, "output") as m:
        wo = m.sbuf("wo", [128, D])
        ln_cols = m.sbuf("ln_cols", [128, 2])
        wc = m.sbuf("wc", [128, D])
        b_wide = m.sbuf("b_wide", [128, TT])
        bwo = m.sbuf("bwo", [128, D])
        oT = m.sbuf("oT", [128, 2, L])
        yvar = m.sbuf("yvar", [128, NTILES])
        ytmp = m.sbuf("ytmp", [128, NTILES])
        names = "loaded oT_ready oT_free o_psum o_free wg_ready w_psum b_ready w_ready dve_chain var_ready root_ready o2_ready o2_free z_psum z_free"
        s = {n: m.sem(n) for n in names.split()}

        def batch_of_o(b):
            return o_all[:, :, bass.ds(b, 1), :].rearrange("p c o t -> p c (o t)")

        def turned(u):
            return oT[:, u, :].rearrange("p (c t) -> p c t", t=C)

        with nc.Block() as block:
            @block.sync
            def _(sp):
                sp.dma_start(wo[:], io["wo"]).then_inc(s["loaded"], 16)
                sp.dma_start(ln_cols[:], io["ln_cols"]).then_inc(s["loaded"], 16)

            @block.tensor
            def _(pe):
                pe.wait_ge(s["wg_ready"], 1)
                nc.tensor.matmul(psum[4][:, 0:D], ones[:], wc[:], start=True, stop=True)
                nc.tensor.matmul(psum[5][0:TT, 0:D], b_wide[:], wo[:], start=True, stop=True).then_inc(s["w_psum"], 1)
                with pe.Fori(0, B // 2) as i:
                    for u in range(2):
                        pe.wait_ge(s["oT_ready"], 2 * i + (u + 1))
                        pe.wait_ge(s["o_free"], 2 * i + (u + 1))
                        for t in range(NT):
                            mm = nc.tensor.transpose(psum[2 * u + t // 3][0:TT, (t % 3) * D:(t % 3 + 1) * D],
                                                     oT[:, u, t * TT:(t + 1) * TT], ident[:])
                        mm.then_inc(s["o_psum"], 1)
                pe.wait_ge(s["w_ready"], 1)
                with pe.Fori(0, B // 2) as i:
                    for u in range(2):
                        pe.wait_ge(s["o2_ready"], 2 * i + (u + 1))
                        pe.wait_ge(s["z_free"], 2 * i + (u + 1))
                        for t in range(NT):
                            mm = nc.tensor.matmul(psum[2 * u + t // 3][0:TT, (t % 3) * D:(t % 3 + 1) * D],
                                                  oT[:, u, t * TT:(t + 1) * TT], wc[:], start=True, stop=True)
                        mm.then_inc(s["z_psum"], 1)

            @block.scalar
            def _(act):
                act.sem_inc(s["oT_free"], 2)
                with act.Fori(0, B // 2) as i:
                    for u in range(2):
                        act.wait_ge(s["oT_free"], 2 * i + (u + 1))
                        nc.scalar.activation(turned(u), batch_of_o(2 * i + u), ACT.Identity).then_inc(s["oT_ready"], 1)
                        act.wait_ge(s["o_psum"], 2 * i + (u + 1))
                        act.sem_inc(s["oT_free"], 1)
                act.wait_ge(s["var_ready"], 1)
                nc.scalar.activation(ytmp[0:TT, :], yvar[0:TT, :], ACT.Sqrt).then_inc(s["root_ready"], 1)
                act.sem_inc(s["o2_free"], 2)
                with act.Fori(0, B // 2) as i:
                    for u in range(2):
                        act.wait_ge(s["o2_free"], 2 * i + (u + 1))
                        nc.scalar.activation(turned(u), batch_of_o(2 * i + u), ACT.Identity).then_inc(s["o2_ready"], 1)
                        act.wait_ge(s["z_psum"], 2 * i + (u + 1))
                        act.sem_inc(s["o2_free"], 1)

            @block.vector
            def _(dve):
                chain = Chain(dve, s["dve_chain"])
                dve.wait_ge(s["loaded"], 32)
                chain.link(nc.vector.tensor_scalar(wc[:], wo[:], ln_cols[:, 0:1], None, ALU.mult))
                chain.link(nc.vector.tensor_copy(b_wide[:], ln_cols[:, 1:2].broadcast_to([128, TT])))
                dve.sem_inc(s["wg_ready"], 1)
                dve.wait_ge(s["w_psum"], 1)
                chain.link(nc.vector.scalar_tensor_tensor(out=wc[:], in0=psum[4][:, 0:D], scalar=-1.0 / D, in1=wc[:],
                                                          op0=ALU.mult, op1=ALU.add))
                chain.link(nc.vector.tensor_copy(bwo[0:TT, :], psum[5][0:TT, 0:D]))
                dve.sem_inc(s["w_ready"], 1)
                dve.sem_inc(s["o_free"], 2)
                before = chain.n
                with dve.Fori(0, B // 2) as i:
                    chain = Chain(dve, s["dve_chain"], before + 2 * NT * i)
                    for u in range(2):
                        dve.wait_ge(s["o_psum"], 2 * i + (u + 1))
                        for t in range(NT):
                            chain.add(nc.vector.bn_stats(stats[0:TT, bass.ds((2 * i + u) * NT + t, 1), :],
                                                         psum[2 * u + t // 3][0:TT, (t % 3) * D:(t % 3 + 1) * D]))
                        chain.settle()
                        dve.sem_inc(s["o_free"], 1)
                chain = Chain(dve, s["dve_chain"], before + NTILES)
                moments(nc, dve, chain, stats, mean[0:TT, :], yvar[0:TT, :], ytmp[0:TT, :])
                dve.sem_inc(s["var_ready"], 1)
                dve.wait_ge(s["root_ready"], 1)
                chain.link(nc.vector.reciprocal(rstd[0:TT, :], ytmp[0:TT, :]))
                refine_rsqrt(nc, chain, rstd[0:TT, :], yvar[0:TT, :], ytmp[0:TT, :])
                dve.sem_inc(s["z_free"], 2)
                before += NTILES + chain.n
                with dve.Fori(0, B // 2) as i:
                    chain = Chain(dve, s["dve_chain"], before + 2 * (1 + 2 * NT) * i)
                    for u in range(2):
                        rows = h[0:TT, bass.ds((2 * i + u) * NT, NT), :]
                        chain.link(nc.vector.tensor_tensor(rows, rows, bwo[0:TT, :].unsqueeze(1).broadcast_to([TT, NT, D]), ALU.add))
                        dve.wait_ge(s["z_psum"], 2 * i + (u + 1))
                        for t in range(NT):
                            col = (2 * i + u) * NT + t
                            row = h[0:TT, bass.ds(col, 1), :].rearrange("p o d -> p (o d)")
                            chain.add(nc.vector.scalar_tensor_tensor(
                                out=row, in0=psum[2 * u + t // 3][0:TT, (t % 3) * D:(t % 3 + 1) * D],
                                scalar=rstd[0:TT, bass.ds(col, 1)], in1=row, op0=ALU.mult, op1=ALU.add))
                        chain.settle()
                        dve.sem_inc(s["z_free"], 1)
                        for t in range(NT):
                            chain.add(nc.vector.bn_stats(stats[0:TT, bass.ds((2 * i + u) * NT + t, 1), :],
                                                         h[0:TT, bass.ds((2 * i + u) * NT + t, 1), :]))
                        chain.settle()
                    assert chain.n == 2 * (1 + 2 * NT)


NEXP, DFF = 64, 512
ACTIVE = 2
CAP = 235
HP = (CAP + 1) // 2
SLOTS = 2 * HP
FCH = DFF // D
BUCKET_SCALE = 8.0


def zero_slots(nc, slots_dram):
    with Memory(nc, "zero") as m:
        zeros = m.sbuf("zeros", [128, NEXP * SLOTS * D // 128 // 8])
        made, stored = m.sem("made"), m.sem("stored")
        flat = slots_dram.rearrange("r d -> (r d)").rearrange("(k p n) -> k p n", k=8, p=128)
        with nc.Block() as block:
            @block.gpsimd
            def _(pool):
                nc.gpsimd.memset(zeros[:], 0.0).then_inc(made, 1)

            @block.sync
            def _(sp):
                sp.wait_ge(made, 1)
                for k in range(8):
                    sp.dma_start(flat[k], zeros[:]).then_inc(stored, 16)
                sp.wait_ge(stored, 128)


def route(nc, io, h, mean, rstd, xn, weight, slot_in, slot_out, psum, ident, ones):
    with Memory(nc, "route") as m:
        w_hash = m.sbuf("w_hash", [128, ACTIVE])
        buckets = m.sbuf("buckets", [128, NEXP])
        earlier = m.sbuf("earlier", [128, 128])
        earlier16 = m.sbuf("earlier16", [128, 128], BF16)
        ones16 = m.sbuf("ones16", [128, 128], BF16)
        xT = m.sbuf("xT", [128, 2, 3, TT])
        score = m.sbuf("score", [128, NTILES, ACTIVE])
        whole = m.sbuf("whole", [128, NTILES, ACTIVE], I32)
        floor = m.sbuf("floor", [128, NTILES, ACTIVE])
        above = m.sbuf("above", [128, NTILES, ACTIVE])
        expert = m.sbuf("expert", [128, NTILES, ACTIVE])
        hot = m.sbuf("hot", [128, ACTIVE, NTILES, NEXP], BF16)
        both = m.sbuf("both", [128, NTILES, NEXP], BF16)
        prior = m.sbuf("prior", [128, NTILES, NEXP], BF16)
        product = m.sbuf("product", [128, NTILES, NEXP])
        place = m.sbuf("place", [128, ACTIVE, NTILES])
        same = m.sbuf("same", [128, NTILES])
        full = m.sbuf("full", [128, ACTIVE, NTILES])
        slot = m.sbuf("slot", [128, ACTIVE, NTILES])
        names = "loaded chain x_ready xT_psum xT_ready xT_bank_free score_psum hot_ready prior_ready rank_psum"
        s = {n: m.sem(n) for n in names.split()}
        per_bank = 512 // NEXP
        BIG = float(2 * NEXP * SLOTS)

        with nc.Block() as block:
            @block.sync
            def _(sp):
                sp.dma_start(w_hash[:], io["w_hash_T"]).then_inc(s["loaded"], 16)
                sp.dma_start(buckets[:], io["buckets"].partition_broadcast(128)).then_inc(s["loaded"], 16)
                sp.dma_start(earlier[:], io["earlier"]).then_inc(s["loaded"], 16)

            @block.tensor
            def _(pe):
                pe.wait_ge(s["loaded"], 48)
                for g in range(NTILES // 3):
                    pe.wait_ge(s["x_ready"], g // 2 + 1)
                    if g >= 2:
                        pe.wait_ge(s["xT_ready"], g - 1)
                    for t in range(3):
                        mm = nc.tensor.transpose(psum[g % 2][:, t * TT:(t + 1) * TT], xn[0:TT, 3 * g + t, :],
                                                 ident[0:TT, 0:TT])
                    mm.then_inc(s["xT_psum"], 1)
                    if g >= 1:
                        pe.wait_ge(s["xT_ready"], g)
                        for t in range(3):
                            tile = 3 * (g - 1) + t
                            mm = nc.tensor.matmul(psum[2][0:TT, ACTIVE * tile:ACTIVE * (tile + 1)],
                                                  xT[:, (g - 1) % 2, t, :], w_hash[:], start=True, stop=True)
                        mm.then_inc(s["score_psum"], 1)
                g = NTILES // 3
                pe.wait_ge(s["xT_ready"], g)
                for t in range(3):
                    tile = 3 * (g - 1) + t
                    mm = nc.tensor.matmul(psum[2][0:TT, ACTIVE * tile:ACTIVE * (tile + 1)],
                                          xT[:, (g - 1) % 2, t, :], w_hash[:], start=True, stop=True)
                mm.then_inc(s["score_psum"], 1)
                pe.wait_ge(s["hot_ready"], 1)
                for k in range(NTILES // per_bank):
                    out = psum[k][0:TT, :].rearrange("p (t e) -> p t e", e=NEXP)
                    tiles = slice(k * per_bank, (k + 1) * per_bank)
                    nc.tensor.matmul(out, earlier16[0:TT, 0:TT], both[0:TT, tiles, :], start=True, stop=False)
                    pe.wait_ge(s["prior_ready"], 1)
                    mm = nc.tensor.matmul(out, ones16[0:TT, 0:TT], prior[0:TT, tiles, :], start=False, stop=True)
                    mm.then_inc(s["rank_psum"], 1)

            @block.scalar
            def _(act):
                for g in range(NTILES // 3):
                    act.wait_ge(s["xT_psum"], g + 1)
                    if g >= 2:
                        act.wait_ge(s["score_psum"], g - 1)
                    nc.scalar.activation(xT[:, g % 2, :, :].rearrange("p t k -> p (t k)"),
                                         psum[g % 2][:, 0:3 * TT], ACT.Identity).then_inc(s["xT_ready"], 1)

            @block.vector
            def _(dve):
                chain = Chain(dve, s["chain"])
                for b in range(B):
                    normalized_tiles(nc, dve, chain, xn[:, b * NT:(b + 1) * NT, :], h, mean, rstd, b)
                    dve.sem_inc(s["x_ready"], 1)
                dve.wait_ge(s["loaded"], 48)
                chain.add(nc.vector.tensor_copy(earlier16[:], earlier[:]))
                chain.add(nc.vector.tensor_copy(ones16[:], ones[:]))
                dve.wait_ge(s["score_psum"], NTILES // 3)
                chain.link(nc.vector.tensor_scalar(
                    score[0:TT], psum[2][0:TT, 0:NTILES * ACTIVE].rearrange("p (t a) -> p t a", a=ACTIVE),
                    BUCKET_SCALE, None, ALU.mult))
                chain.link(nc.vector.tensor_copy(whole[0:TT], score[0:TT]))
                chain.link(nc.vector.tensor_copy(floor[0:TT], whole[0:TT]))
                chain.link(nc.vector.tensor_tensor(above[0:TT], floor[0:TT], score[0:TT], ALU.is_gt))
                chain.link(nc.vector.tensor_tensor(floor[0:TT], floor[0:TT], above[0:TT], ALU.subtract))
                chain.link(nc.vector.tensor_copy(whole[0:TT], floor[0:TT]))
                chain.link(nc.vector.tensor_single_scalar(whole[0:TT], whole[0:TT], NEXP - 1, ALU.bitwise_and))
                chain.link(nc.vector.tensor_copy(expert[0:TT], whole[0:TT]))
                for a in range(ACTIVE):
                    chain.add(nc.vector.tensor_tensor(
                        hot[0:TT, a], expert[0:TT, :, a:a + 1].broadcast_to([TT, NTILES, NEXP]),
                        buckets[0:TT, :].unsqueeze(1).broadcast_to([TT, NTILES, NEXP]), ALU.is_equal))
                chain.settle()
                chain.link(nc.vector.tensor_tensor(both[0:TT], hot[0:TT, 0], hot[0:TT, 1], ALU.add))
                dve.sem_inc(s["hot_ready"], 1)
                chain.link(nc.vector.memset(prior[0:TT, 0, :], 0.0))
                for t in range(NTILES - 1):
                    chain.link(nc.vector.tensor_tensor(prior[0:TT, t + 1, :], prior[0:TT, t, :], both[0:TT, t, :], ALU.add))
                dve.sem_inc(s["prior_ready"], 1)
                chain.link(nc.vector.tensor_tensor(same[0:TT], expert[0:TT, :, 0], expert[0:TT, :, 1], ALU.is_equal))
                dve.wait_ge(s["rank_psum"], NTILES // per_bank)
                for a in range(ACTIVE):
                    for k in range(NTILES // per_bank):
                        tiles = slice(k * per_bank, (k + 1) * per_bank)
                        chain.add(nc.vector.tensor_tensor(
                            product[0:TT, tiles, :], psum[k][0:TT, :].rearrange("p (t e) -> p t e", e=NEXP),
                            hot[0:TT, a, tiles, :], ALU.mult))
                    chain.settle()
                    chain.link(nc.vector.tensor_reduce(place[0:TT, a], product[0:TT], AX.X, ALU.add))
                chain.link(nc.vector.tensor_tensor(place[0:TT, 1], place[0:TT, 1], same[0:TT], ALU.add))
                chain.link(nc.vector.tensor_scalar(full[0:TT], place[0:TT], float(CAP), None, ALU.is_ge))
                for a in range(ACTIVE):
                    chain.add(nc.vector.scalar_tensor_tensor(
                        out=slot[0:TT, a], in0=expert[0:TT, :, a], scalar=float(SLOTS), in1=place[0:TT, a],
                        op0=ALU.mult, op1=ALU.add))
                chain.settle()
                chain.link(nc.vector.scalar_tensor_tensor(
                    out=place[0:TT], in0=full[0:TT], scalar=BIG, in1=slot[0:TT], op0=ALU.mult, op1=ALU.add))
                chain.add(nc.vector.tensor_copy(slot_in[0:TT], place[0:TT]))
                chain.link(nc.vector.tensor_scalar(weight[0:TT], full[0:TT], -0.5, 0.5, ALU.mult, ALU.add))
                chain.link(nc.vector.tensor_scalar(same[0:TT], weight[0:TT, 0], 2.0, None, ALU.mult))
                chain.link(nc.vector.tensor_tensor(slot[0:TT, 0], slot[0:TT, 0], same[0:TT], ALU.mult))
                chain.link(nc.vector.tensor_scalar(same[0:TT], weight[0:TT, 1], 2.0, None, ALU.mult))
                chain.link(nc.vector.tensor_tensor(slot[0:TT, 1], slot[0:TT, 1], same[0:TT], ALU.mult))
                chain.link(nc.vector.tensor_copy(slot_out[0:TT], slot[0:TT]))


def dispatch(nc, xn, slot_in, slots_dram):
    with Memory(nc, "dispatch") as m:
        sent = m.sem("sent")
        with nc.Block() as block:
            @block.gpsimd
            def _(pool):
                for t in range(NTILES):
                    for a in range(ACTIVE):
                        nc.gpsimd.indirect_dma_start(
                            slots_dram, bass.IndirectOffsetOnAxis(slot_in[0:TT, a, t:t + 1], 0), xn[0:TT, t, :], None,
                            bounds_check=NEXP * SLOTS - 1, oob_is_err=False).then_inc(sent, 16)
                pool.wait_ge(sent, 16 * NTILES * ACTIVE)


def experts(nc, io, slots_dram, y_dram, psum, ident):
    U = 4
    with Memory(nc, "experts") as m:
        w1 = m.sbuf("w1", [128, U, DFF])
        w2 = m.sbuf("w2", [128, U, FCH, D])
        b1 = m.sbuf("b1", [128, NEXP, FCH])
        b2 = m.sbuf("b2", [128, NEXP, D])
        x = m.sbuf("x", [128, U, 2, D])
        xT = m.sbuf("xT", [128, 2, SLOTS])
        inner = m.sbuf("inner", [128, 2, FCH, SLOTS])
        y = m.sbuf("y", [128, U, 2, D])
        biases = m.sem("biases")
        got = [m.sem(f"got_{u}") for u in range(U)]
        put = [m.sem(f"put_{u}") for u in range(U)]
        names = "turned_psum xT_ready inner_psum inner_ready y_psum y_ready y_free"
        s = {n: m.sem(n) for n in names.split()}
        ROUNDS = NEXP // U
        rows = lambda dram, e: dram[bass.ds(e * SLOTS, SLOTS), :].rearrange("(s p) d -> p s d", p=HP)
        w1_of = lambda e: io["moe1_w1"][bass.ds(e, 1), :, :].rearrange("o p f -> p (o f)")
        w2_of = lambda e: io["moe1_w2"][bass.ds(e, 1), :, :].rearrange("o (p j) d -> p (o j) d", j=FCH)

        with nc.Block() as block:
            @block.sync
            def _(sp):
                sp.dma_start(b1[:], io["moe1_b1"]).then_inc(biases, 16)
                sp.dma_start(b2[:], io["moe1_b2"].partition_broadcast(128)).then_inc(biases, 16)

                def load(e, u):
                    sp.dma_start(x[0:HP, u], rows(slots_dram, e)).then_inc(got[u], 16)
                    sp.dma_start(w1[:, u, :], w1_of(e)).then_inc(got[u], 16)
                    sp.dma_start(w2[:, u], w2_of(e)).then_inc(got[u], 16)

                for u in range(U):
                    load(u, u)
                with sp.Fori(0, ROUNDS - 1) as i:
                    for u in range(U):
                        sp.wait_ge(s["y_psum"], U * i + (u + 1) + 2)
                        load(U * (i + 1) + u, u)

            @block.gpsimd
            def _(pool):
                with pool.Fori(0, ROUNDS) as i:
                    for u in range(U):
                        pool.wait_ge(s["y_ready"], U * i + (u + 1) + 2)
                        pool.dma_start(rows(y_dram, U * i + u), y[0:HP, u]).then_inc(put[u], 16)
                        pool.wait_ge(put[u], 16 * i + 16)
                        pool.sem_inc(s["y_free"], 1)

            @block.tensor
            def _(pe):
                def first(i, u):
                    e = U * i + u
                    pe.wait_ge(got[u], 48 * i + 48)
                    pe.wait_ge(s["xT_ready"], e + 1)
                    for k in range(2):
                        mm = nc.tensor.transpose(psum[4 + u % 2][:, k * HP:(k + 1) * HP], x[0:HP, u, k, :],
                                                 ident[0:HP, 0:HP])
                    mm.then_inc(s["turned_psum"], 1)
                    pe.wait_ge(s["xT_ready"], e + 1 + 2)
                    for j in range(FCH):
                        pe.wait_ge(s["inner_ready"], FCH * e + (j + 1))
                        nc.tensor.matmul(psum[j][:, 0:SLOTS], w1[:, u, :].rearrange("p (k j) -> p k j", j=FCH)[:, :, j],
                                         xT[:, u % 2, :], start=True, stop=True).then_inc(s["inner_psum"], 1)

                def second(i, u):
                    e = U * i + u
                    pe.wait_ge(s["y_ready"], e + 1)
                    for k in range(2):
                        for j in range(FCH):
                            pe.wait_ge(s["inner_ready"], FCH * e + (j + 1) + FCH)
                            mm = nc.tensor.matmul(psum[6 + u % 2][0:HP, k * D:(k + 1) * D],
                                                  inner[:, u % 2, j, k * HP:(k + 1) * HP], w2[:, u, j, :],
                                                  start=(j == 0), stop=(j == FCH - 1))
                    mm.then_inc(s["y_psum"], 1)

                first(0, 0)
                with pe.Fori(0, ROUNDS - 1) as i:
                    for u in range(U):
                        if u < U - 1:
                            first(i, u + 1)
                        else:
                            first(i + 1, 0)
                        second(i, u)
                for u in range(U):
                    if u < U - 1:
                        first(ROUNDS - 1, u + 1)
                    second(ROUNDS - 1, u)

            @block.scalar
            def _(act):
                act.sem_inc(s["inner_ready"], FCH)
                act.wait_ge(biases, 32)
                with act.Fori(0, ROUNDS) as i:
                    for u in range(U):
                        e = U * i + u
                        act.wait_ge(s["y_psum"], e + 1)
                        for j in range(FCH):
                            act.wait_ge(s["inner_psum"], FCH * e + (j + 1) + 2 * FCH)
                            nc.scalar.activation(inner[:, u % 2, j, :], psum[j][:, 0:SLOTS], ACT.Gelu,
                                                 bias=b1[:, bass.ds(e, 1), j:j + 1].rearrange("p o j -> p (o j)")
                                                 ).then_inc(s["inner_ready"], 1)

            @block.vector
            def _(dve):
                dve.sem_inc(s["xT_ready"], 2)
                dve.sem_inc(s["y_ready"], 2)
                dve.sem_inc(s["inner_psum"], 2 * FCH)
                dve.sem_inc(s["y_psum"], 2)
                dve.sem_inc(s["y_free"], U)

                def turned(i, u):
                    e = U * i + u
                    dve.wait_ge(s["turned_psum"], e + 1)
                    dve.wait_ge(s["inner_psum"], FCH * (e + 1))
                    nc.vector.tensor_copy(xT[:, u % 2, :], psum[4 + u % 2][:, 0:SLOTS]).then_inc(s["xT_ready"], 1)

                def biased(i, u):
                    e = U * i + u
                    dve.wait_ge(s["y_psum"], e + 1 + 2)
                    dve.wait_ge(s["y_free"], e + 1)
                    nc.vector.tensor_tensor(
                        y[0:HP, u], psum[6 + u % 2][0:HP, 0:2 * D].rearrange("p (k d) -> p k d", d=D),
                        b2[0:HP, bass.ds(e, 1), :].broadcast_to([HP, 2, D]), ALU.add).then_inc(s["y_ready"], 1)

                dve.wait_ge(biases, 32)
                turned(0, 0)
                with dve.Fori(0, ROUNDS - 1) as i:
                    for u in range(U):
                        if u < U - 1:
                            turned(i, u + 1)
                        else:
                            turned(i + 1, 0)
                        biased(i, u)
                for u in range(U):
                    if u < U - 1:
                        turned(ROUNDS - 1, u + 1)
                    biased(ROUNDS - 1, u)


def combine(nc, h, weight, slot_out, y_dram, out):
    R = 4
    with Memory(nc, "combine") as m:
        y = m.sbuf("y", [128, R, ACTIVE, D])
        got = [m.sem(f"got_{r}") for r in range(R)]
        used, done, chain_sem, stored = m.sem("used"), m.sem("done"), m.sem("chain"), m.sem("stored")
        out_tiles = out.rearrange("b (t p) d -> p (b t) d", p=TT)
        with nc.Block() as block:
            @block.gpsimd
            def _(pool):
                for t in range(NTILES):
                    if t >= R:
                        pool.wait_ge(used, t - R + 1)
                    for a in range(ACTIVE):
                        nc.gpsimd.indirect_dma_start(
                            y[0:TT, t % R, a, :], None, y_dram,
                            bass.IndirectOffsetOnAxis(slot_out[0:TT, a, t:t + 1], 0),
                            bounds_check=NEXP * SLOTS - 1, oob_is_err=False).then_inc(got[t % R], 16)

            @block.vector
            def _(dve):
                chain = Chain(dve, chain_sem)
                for t in range(NTILES):
                    dve.wait_ge(got[t % R], 16 * ACTIVE * (t // R + 1))
                    for a in range(ACTIVE):
                        chain.link(nc.vector.scalar_tensor_tensor(
                            out=h[0:TT, t, :], in0=y[0:TT, t % R, a, :], scalar=weight[0:TT, a, t:t + 1],
                            in1=h[0:TT, t, :], op0=ALU.mult, op1=ALU.add))
                    dve.sem_inc(used, 1)

            @block.sync
            def _(sp):
                for g in range(NTILES // NT):
                    sp.wait_ge(used, NT * (g + 1))
                    tiles = slice(g * NT, (g + 1) * NT)
                    sp.dma_start(out_tiles[:, tiles, :], h[0:TT, tiles, :]).then_inc(stored, 16)
                sp.wait_ge(stored, 16 * (NTILES // NT))


def tower(nc, io, out):
    pieces_dram = nc.dram_tensor("head_pieces", (B, 2 * PIECES, D, L), BF16).ap()
    k_rows_dram = nc.dram_tensor("key_rows", (B, L, D), FP32).ap()
    coef_dram = nc.dram_tensor("chunk_coefficients", (B, 128, NCH, NCOEF), FP32).ap()
    slots_dram = nc.dram_tensor("slot_rows", (NEXP * SLOTS, D), FP32).ap()
    y_dram = nc.dram_tensor("result_rows", (NEXP * SLOTS, D), FP32).ap()
    with Memory(nc, "tower") as m:
        h = m.sbuf("h", [128, NTILES, D])
        stats = m.sbuf("stats", [128, NTILES, 6])
        mean = m.sbuf("mean", [128, NTILES])
        rstd = m.sbuf("rstd", [128, NTILES])
        ident = m.sbuf("ident", [128, 128])
        ones = m.sbuf("ones", [128, 128])
        banks = m.stack.enter_context(nc.psum_tensor("tower_banks", [128, 8, 512], FP32))
        psum = [banks[:, i, :] for i in range(8)]
        load_constants(nc, "constants", [(ident, io["ident"]), (ones, io["ones"])])

        zero_slots(nc, slots_dram)
        convolution(nc, io, h, stats, psum, ident)

        layernorm_scalars(nc, "ln1", stats, mean, rstd)
        with Memory(nc, "attention_values") as a:
            n3 = a.sbuf("n3", [128, NTILES, D])
            dmax = a.sbuf("dmax", [128, B])
            block_ones = a.sbuf("block_ones", [128, 128])
            load_constants(nc, "block_constants", [(block_ones, io["block_ones"])])
            head_vectors(nc, io, h, mean, rstd, n3, dmax, pieces_dram, psum, ident, block_ones)
            attention(nc, io, h, stats, n3, dmax, pieces_dram, banks, psum, ident, ones)
        layernorm_scalars(nc, "ln2", stats, mean, rstd)
        expert_of_batch(nc, io, h, stats, mean, rstd, psum, ident, ones)

        layernorm_scalars(nc, "ln3", stats, mean, rstd)
        with Memory(nc, "delta_values") as a:
            kq_all = a.sbuf("kq_all", [128, NCH, B, 2, C])
            v_all = a.sbuf("v_all", [128, NCH, B, C])
            block_sum = a.sbuf("block_sum", [128, 128])
            load_constants(nc, "sum_constants", [(block_sum, io["block_sum"])])
            with Memory(nc, "delta_rates") as r:
                beta = r.sbuf("beta", [128, B, L])
                delta_projections(nc, io, h, mean, rstd, kq_all, v_all, beta, k_rows_dram, psum, ident)
                triangular_coefficients(nc, kq_all, beta, coef_dram, psum, block_sum)
            u_all = a.sbuf("u_all", [128, NCH, B, C])
            o_all = a.sbuf("o_all", [128, NCH, B, C])
            delta_rule(nc, io, kq_all, v_all, u_all, o_all, k_rows_dram, coef_dram, banks, psum)
            within_chunks(nc, kq_all, u_all, o_all, psum, block_sum)
            delta_output(nc, io, h, stats, mean, rstd, o_all, psum, ident, ones)

        layernorm_scalars(nc, "ln4", stats, mean, rstd)
        with Memory(nc, "routing") as a:
            xn = a.sbuf("xn", [128, NTILES, D])
            weight = a.sbuf("weight", [128, ACTIVE, NTILES])
            slot_in = a.sbuf("slot_in", [128, ACTIVE, NTILES], I32)
            slot_out = a.sbuf("slot_out", [128, ACTIVE, NTILES], I32)
            route(nc, io, h, mean, rstd, xn, weight, slot_in, slot_out, psum, ident, ones)
            dispatch(nc, xn, slot_in, slots_dram)
            experts(nc, io, slots_dram, y_dram, psum, ident)
            combine(nc, h, weight, slot_out, y_dram, out)


def load_constants(nc, stage, pairs):
    with Memory(nc, stage) as m:
        loaded = m.sem("loaded")
        with nc.Block() as block:
            @block.sync
            def _(sp):
                for buffer, source in pairs:
                    sp.dma_start(buffer[:], source).then_inc(loaded, 16)
                sp.wait_ge(loaded, 16 * len(pairs))


def kernel(**inputs):
    import concourse.bacc as bacc
    from concourse.bass_utils import run_bass_kernel_spmd

    given = {name: np.asarray(a) for name, a in inputs.items()}
    f32 = np.float32

    def head_rows(w):
        return np.repeat(w.reshape(G, 4, 1, F, D), 2, axis=2).reshape(G, 128, D).transpose(1, 0, 2)

    taps = given["L0_tok_weight"].transpose(1, 2, 0)
    partition = np.arange(128)
    arrays = {
        "x": given["x"], "conv_w_even": taps[:, 0::2], "conv_w_odd": taps[:, 1::2],
        "conv_b": given["L0_tok_bias"].reshape(D, 1),
        "w_qkv_T": given["L0_attn_qkv_w"].T, "w_delta_T": given["L0_attn_delta_w"].T,
        "g12_cols": np.stack([np.tile(given["L0_attn_g1"], H), np.tile(given["L0_attn_g2"], H)], 1),
        "g3_row": np.tile(given["L0_attn_g3"], H),
        "w_qkv_rows": head_rows(given["L0_attn_qkv_w"]), "w_delta_rows": head_rows(given["L0_attn_delta_w"]),
        "moe0_wg": given["L0_ffn_Wg"], "moe0_bg": given["L0_ffn_bg"].reshape(1, -1),
        "moe0_we": given["L0_ffn_We"], "moe0_be": given["L0_ffn_be"],
        "wq": given["L1_attn_Wq"], "wk": given["L1_attn_Wk"], "wv": given["L1_attn_Wv"],
        "wb": given["L1_attn_Wb"], "wo": given["L1_attn_Wo"],
        "ln_cols": np.stack([given["L1_attn_ln_g"], given["L1_attn_ln_b"]], 1),
        "w_hash_T": given["L1_ffn_W_hash"][:ACTIVE].T,
        "moe1_w1": given["L1_ffn_W1"], "moe1_w2": given["L1_ffn_W2"],
        "moe1_b1": given["L1_ffn_b1"].reshape(NEXP, D, FCH).transpose(1, 0, 2), "moe1_b2": given["L1_ffn_b2"],
        "ident": np.eye(128, dtype=f32), "ones": np.ones((128, 128), f32),
        "block_ones": np.kron(np.eye(H), np.full((F, F), 1.0 / F)).astype(f32),
        "block_sum": np.kron(np.eye(H), np.ones((F, F))).astype(f32),
        "head_start": (partition[:, None] == F * np.arange(H)).astype(f32),
        "countdown": (16 - np.arange(16)).astype(f32).reshape(1, 16),
        "pair_masks": np.stack([partition // F % 2 == 0, partition // F % 2 == 1], 1).astype(f32),
        "buckets": np.arange(NEXP).astype(f32),
        "earlier": np.triu(np.ones((128, 128), f32), 1),
    }
    arrays = {name: np.ascontiguousarray(a) for name, a in arrays.items()}
    nc = bacc.Bacc("TRN2", target_bir_lowering=False, num_devices=1)
    io = {name: nc.dram_tensor(name, a.shape, mybir.dt.from_np(a.dtype), kind="ExternalInput").ap()
          for name, a in arrays.items()}
    out = nc.dram_tensor("out", (B, L, D), FP32, kind="ExternalOutput").ap()
    tower(nc, io, out)
    return run_bass_kernel_spmd(nc, [arrays], core_ids=[0]).results[0]["out"]
```

```python
import numpy as np
import concourse.bass as bass
from concourse import mybir
from contextlib import ExitStack

FP32 = mybir.dt.float32
BF16 = mybir.dt.bfloat16
I32 = mybir.dt.int32
ALU = mybir.AluOpType
ACT = mybir.ActivationFunctionType
AX = mybir.AxisListType

B, CIN, L = 8, 64, 750
D, H, F = 128, 8, 16
TT, NT = 125, 6
NTILES = B * NT
HALF = L // 2
TAPS, PAIRS = 9, 5
PAD = 4
XW = L + 2 * PAD
G = 2
NEXP, DFF = 64, 512
ACTIVE = 2
CAP = 235
HP = (CAP + 1) // 2
SLOTS = 2 * HP
FCH = DFF // D
BUCKET_SCALE = 8.0
ZERO_PARTS = 8
LN_EPS = 1e-5
RMS_EPS = 1.1920929e-07
PIECES = 3
PIECES_A = [0, 0, 1, 1, 0, 2]
PIECES_B = [0, 1, 0, 1, 2, 0]
KROWS = len(PIECES_A) * F


class Memory:

    def __init__(self, nc, stage):
        self.nc, self.stage, self.stack, self.sems = nc, stage, ExitStack(), []

    def __enter__(self):
        return self

    def __exit__(self, *error):
        self.stack.close()
        if self.sems:
            self.nc.clear_and_free_semaphores(self.sems)
            self.nc.all_engine_barrier()

    def sbuf(self, name, shape, dt=FP32):
        return self.stack.enter_context(self.nc.sbuf_tensor(f"{self.stage}_{name}", shape, dt))

    def sem(self, name):
        self.sems.append(self.nc.alloc_semaphore(name=f"{self.stage}_{name}"))
        return self.sems[-1]


def convolution(nc, io, h, stats, psum, ident):
    with Memory(nc, "conv") as m:
        xpad = m.sbuf("xpad", [128, B, XW])
        wconv = m.sbuf("w", [128, PAIRS, D])
        cbias = m.sbuf("bias", [128, 1])
        hT = m.sbuf("hT", [128, 2, L])
        loaded = m.sem("loaded")
        padded = m.sem("padded")
        conv_ready, conv_free = m.sem("conv_ready"), m.sem("conv_free")
        hT_ready, hT_free = m.sem("hT_ready"), m.sem("hT_free")
        turned_ready, turned_free = m.sem("turned_ready"), m.sem("turned_free")
        h_written = m.sem("h_written")
        with nc.Block() as block:
            @block.sync
            def _(sp):
                sp.dma_start(wconv[0:64, :, :], io["conv_w_even"]).then_inc(loaded, 16)
                sp.dma_start(wconv[64:128, 0:PAIRS - 1, :], io["conv_w_odd"]).then_inc(loaded, 16)
                sp.dma_start(cbias[:], io["conv_b"]).then_inc(loaded, 16)
                x_cbl = io["x"].rearrange("b c l -> c b l")
                sp.dma_start(xpad[0:64, :, PAD:PAD + L], x_cbl).then_inc(loaded, 16)
                sp.dma_start(xpad[64:128, :, PAD - 1:PAD - 1 + L], x_cbl).then_inc(loaded, 16)

            @block.gpsimd
            def _(pool):
                nc.gpsimd.memset(xpad[0:64, :, 0:PAD], 0.0).then_inc(padded, 1)
                nc.gpsimd.memset(xpad[0:64, :, PAD + L:XW], 0.0).then_inc(padded, 1)
                nc.gpsimd.memset(xpad[64:128, :, 0:PAD - 1], 0.0).then_inc(padded, 1)
                nc.gpsimd.memset(xpad[64:128, :, PAD - 1 + L:XW], 0.0).then_inc(padded, 1)

            @block.tensor
            def _(pe):
                pe.wait_ge(loaded, 80)
                pe.wait_ge(padded, 4)
                with pe.Fori(0, B // 2) as i:
                    for u in range(2):
                        pe.wait_ge(conv_free, 2 * i + (u + 1))
                        for half in range(2):
                            for j in range(PAIRS):
                                rows = 128 if j < PAIRS - 1 else 64
                                mm = nc.tensor.matmul(
                                    psum[2 * u + half][:, 0:HALF], wconv[0:rows, j, :],
                                    xpad[0:rows, bass.ds(2 * i + u, 1), half * HALF + 2 * j:half * HALF + 2 * j + HALF],
                                    start=(j == 0), stop=(j == PAIRS - 1))
                        mm.then_inc(conv_ready, 1)
                    for u in range(2):
                        pe.wait_ge(hT_ready, 2 * (2 * i + u) + 2)
                        pe.wait_ge(turned_free, 2 * i + (u + 1))
                        for t in range(NT):
                            mm = nc.tensor.transpose(psum[4 + 2 * u + t // 3][0:TT, (t % 3) * D:(t % 3 + 1) * D],
                                                     hT[:, u, t * TT:(t + 1) * TT], ident[:])
                        mm.then_inc(turned_ready, 1)

            @block.scalar
            def _(act):
                act.sem_inc(conv_free, 2)
                with act.Fori(0, B // 2) as i:
                    for u in range(2):
                        act.wait_ge(conv_ready, 2 * i + (u + 1))
                        act.wait_ge(hT_free, 2 * i + (u + 1))
                        for half in range(2):
                            ins = nc.scalar.activation(hT[:, u, half * HALF:(half + 1) * HALF],
                                                       psum[2 * u + half][:, 0:HALF], ACT.Identity, bias=cbias[:])
                            ins.then_inc(hT_ready, 1)
                        act.wait_ge(hT_ready, 2 * (2 * i + u) + 2)
                        act.sem_inc(conv_free, 1)

            @block.vector
            def _(dve):
                dve.sem_inc(turned_free, 2)
                dve.sem_inc(hT_free, 2)
                with dve.Fori(0, B // 2) as i:
                    for u in range(2):
                        dve.wait_ge(turned_ready, 2 * i + (u + 1))
                        dve.sem_inc(hT_free, 1)
                        for k in range(2):
                            nc.vector.tensor_copy(
                                h[0:TT, bass.ds((2 * i + u) * NT + 3 * k, 3), :],
                                psum[4 + 2 * u + k][0:TT, 0:3 * D].rearrange("p (t d) -> p t d", d=D)).then_inc(h_written, 1)
                        for t in range(NT):
                            nc.vector.bn_stats(stats[0:TT, bass.ds((2 * i + u) * NT + t, 1), :],
                                               psum[4 + 2 * u + t // 3][0:TT, (t % 3) * D:(t % 3 + 1) * D]
                                               ).then_inc(h_written, 1)
                        dve.wait_ge(h_written, (2 + NT) * (2 * i + u + 1))
                        dve.sem_inc(turned_free, 1)


def pass_gate(eng, sem, value, gate):
    eng.wait_ge(sem, value)
    eng.sem_inc(gate, 1)


class Chain:

    def __init__(self, eng, sem, base=0, anchor=None):
        self.eng, self.sem, self.base, self.n, self.anchor = eng, sem, base, 0, anchor

    def add(self, ins):
        ins.then_inc(self.sem, 1)
        self.n += 1

    def settle(self):
        self.eng.wait_ge(self.sem, self.base + self.n)
        if self.anchor is not None:
            self.eng.sem_inc(self.anchor, 1)

    def link(self, ins):
        self.add(ins)
        self.settle()


def spread(scalars, n):
    rows, tiles = scalars.shape
    return scalars.unsqueeze(2).broadcast_to([rows, tiles, n])


def moments(nc, dve, chain, stats, mean, var, tmp):
    even_mean, even_m2 = stats[0:TT, :, 1], stats[0:TT, :, 2]
    odd_mean, odd_m2 = stats[0:TT, :, 4], stats[0:TT, :, 5]
    chain.link(nc.vector.tensor_tensor(mean, even_mean, odd_mean, ALU.add))
    chain.link(nc.vector.tensor_scalar(mean, mean, 0.5, None, ALU.mult))
    chain.link(nc.vector.tensor_tensor(tmp, even_mean, odd_mean, ALU.subtract))
    chain.link(nc.vector.tensor_tensor(tmp, tmp, tmp, ALU.mult))
    chain.link(nc.vector.tensor_tensor(var, even_m2, odd_m2, ALU.add))
    chain.link(nc.vector.tensor_scalar(var, var, 1.0 / D, None, ALU.mult))
    chain.link(nc.vector.scalar_tensor_tensor(out=var, in0=tmp, scalar=0.25, in1=var, op0=ALU.mult, op1=ALU.add))
    chain.link(nc.vector.tensor_scalar(var, var, LN_EPS, None, ALU.add))


def refine_rsqrt(nc, chain, rstd, var, tmp):
    chain.link(nc.vector.tensor_tensor(tmp, rstd, rstd, ALU.mult))
    chain.link(nc.vector.tensor_tensor(tmp, tmp, var, ALU.mult))
    chain.link(nc.vector.tensor_scalar(tmp, tmp, -0.5, 1.5, ALU.mult, ALU.add))
    chain.link(nc.vector.tensor_tensor(rstd, rstd, tmp, ALU.mult))


def layernorm_scalars(nc, stage, stats, mean, rstd):
    with Memory(nc, stage) as m:
        var = m.sbuf("var", [128, NTILES])
        tmp = m.sbuf("tmp", [128, NTILES])
        var_ready, root_ready, done = m.sem("var_ready"), m.sem("root_ready"), m.sem("done")
        with nc.Block() as block:
            @block.vector
            def _(dve):
                chain = Chain(dve, done)
                moments(nc, dve, chain, stats, mean[0:TT, :], var[0:TT, :], tmp[0:TT, :])
                dve.sem_inc(var_ready, 1)
                dve.wait_ge(root_ready, 1)
                chain.link(nc.vector.reciprocal(rstd[0:TT, :], tmp[0:TT, :]))
                refine_rsqrt(nc, chain, rstd[0:TT, :], var[0:TT, :], tmp[0:TT, :])

            @block.scalar
            def _(act):
                act.wait_ge(var_ready, 1)
                nc.scalar.activation(tmp[0:TT, :], var[0:TT, :], ACT.Sqrt).then_inc(root_ready, 1)


def head_vectors(nc, io, h, mean, rstd, n3, dmax, pieces_dram, psum, ident, block_ones):
    with Memory(nc, "heads") as m:
        wT = m.sbuf("wT", [128, D])
        wTd = m.sbuf("wTd", [128, D])
        gcols = m.sbuf("gcols", [128, 2])
        pcol = m.sbuf("pcol", [128, 1])
        pabs = m.sbuf("pabs", [128, 1])
        eps = m.sbuf("eps", [128, 1])
        bound_w = m.sbuf("bound_w", [128, D])
        g3row = m.sbuf("g3row", [128, D])
        xn = m.sbuf("xn", [128, 2, NT, D])
        xnT = m.sbuf("xnT", [128, 2, L])
        sq = m.sbuf("sq", [128, 2, L])
        squares = m.sbuf("squares", [128, 2, NT, D])
        rms = m.sbuf("rms", [128, 2, NT * H])
        n_rows = m.sbuf("n_rows", [128, 2, NT, D])
        nT = m.sbuf("nT", [128, 2, L])
        pnT = m.sbuf("pnT", [128, 2, L])
        rest = m.sbuf("rest", [128, 2, 2, L])
        pieces = m.sbuf("pieces", [128, 2, 2 * PIECES, L], BF16)
        loaded = m.sem("loaded")
        setup = m.sem("setup")
        xn_ready, xnT_psum, xnT_ready, w_psum, sq_ready, ms_ready, rms_ready = (
            m.sem(s) for s in ("xn_ready", "xnT_psum", "xnT_ready", "w_psum", "sq_ready", "ms_ready", "rms_ready"))
        n_ready, nT_psum, nT_ready, nT_taken, a_done, bound_psum, dmax_ready = (
            m.sem(s) for s in ("n_ready", "nT_psum", "nT_ready", "nT_taken", "a_done", "bound_psum", "dmax_ready"))
        a_split, b_split, stored, dve_chain, pool_chain = (
            m.sem(s) for s in ("a_split", "b_split", "stored", "dve_chain", "pool_chain"))
        gate = m.sem("gate")
        pieces_free, nT_free = m.sem("pieces_free"), m.sem("nT_free")
        dmax2 = m.sbuf("dmax2", [128, 2 * B])

        def two_banks(bank):
            return [psum[bank][:, 0:HALF], psum[bank + 1][:, 0:HALF]]

        def split(eng, chain, source, rest, out, first):
            high, middle, low = (out[:, first + k, :] for k in range(PIECES))
            chain.link(eng.tensor_copy(high, source))
            chain.link(eng.tensor_tensor(rest, source, high, ALU.subtract))
            chain.link(eng.tensor_copy(middle, rest))
            return eng.tensor_tensor(low, rest, middle, ALU.subtract)

        with nc.Block() as block:
            @block.sync
            def _(sp):
                sp.dma_start(wT[:], io["w_qkv_T"]).then_inc(loaded, 16)
                sp.dma_start(wTd[:], io["w_delta_T"]).then_inc(loaded, 16)
                sp.dma_start(gcols[:], io["g12_cols"]).then_inc(loaded, 16)
                sp.dma_start(g3row[:], io["g3_row"].partition_broadcast(128)).then_inc(loaded, 16)
                sp.sem_inc(pieces_free, 2)
                with sp.Fori(0, B // 2) as i:
                    for u in range(2):
                        sp.wait_ge(a_split, 2 * i + (u + 1))
                        sp.wait_ge(b_split, 2 * i + (u + 1))
                        sp.dma_start(pieces_dram[bass.ds(2 * i + u, 1), :, :, :].rearrange("o k p t -> p (o k) t"),
                                     pieces[:, u, :, :]).then_inc(stored, 16)
                        sp.wait_ge(stored, 16 * (2 * i + u) + 16)
                        sp.sem_inc(pieces_free, 1)

            @block.tensor
            def _(pe):
                pe.wait_ge(setup, 1)
                with pe.Fori(0, B // 2) as i:
                    for u in range(2):
                        pe.wait_ge(xn_ready, 2 * i + (u + 1))
                        pe.wait_ge(nT_taken, 2 * i + (u + 1))
                        for t in range(NT):
                            mm = nc.tensor.transpose(psum[4 * u + t // 3][:, (t % 3) * TT:(t % 3 + 1) * TT],
                                                     xn[0:TT, u, t, :], ident[0:TT, 0:TT])
                        mm.then_inc(xnT_psum, 1)
                    for u in range(2):
                        pe.wait_ge(xnT_ready, 2 * (2 * i + u) + 2)
                        pe.wait_ge(dmax_ready, 2 * i + (u + 1))
                        for t in range(NT):
                            mm = nc.tensor.matmul(psum[4 * u + 2 + t // 3][0:TT, (t % 3) * D:(t % 3 + 1) * D],
                                                  xnT[:, u, t * TT:(t + 1) * TT], wT[:], start=True, stop=True)
                        mm.then_inc(w_psum, 1)
                    for u in range(2):
                        pe.wait_ge(n_ready, 2 * i + (u + 1))
                        for t in range(NT):
                            mm = nc.tensor.transpose(psum[4 * u + t // 3][:, (t % 3) * TT:(t % 3 + 1) * TT],
                                                     n_rows[0:TT, u, t, :], ident[0:TT, 0:TT])
                        mm.then_inc(nT_psum, 1)
                    for u in range(2):
                        pe.wait_ge(nT_ready, 4 * (2 * i + u) + 4)
                        for half in range(2):
                            mm = nc.tensor.matmul(psum[4 * u + 2 + half][:, 0:HALF], bound_w[:],
                                                  sq[:, u, half * HALF:(half + 1) * HALF], start=True, stop=True)
                        mm.then_inc(bound_psum, 1)

            @block.scalar
            def _(act):
                act.wait_ge(setup, 1)
                act.sem_inc(nT_taken, 2)
                with act.Fori(0, B // 2) as i:
                    for u in range(2):
                        act.wait_ge(xnT_psum, 2 * i + (u + 1))
                        for half in range(2):
                            nc.scalar.activation(xnT[:, u, half * HALF:(half + 1) * HALF],
                                                 psum[4 * u + half][:, 0:HALF], ACT.Identity).then_inc(xnT_ready, 1)
                    for u in range(2):
                        act.wait_ge(w_psum, 2 * i + (u + 1))
                        for k in range(2):
                            nc.scalar.activation(squares[0:TT, u, 3 * k:3 * k + 3, :].rearrange("p t d -> p (t d)"),
                                                 psum[4 * u + 2 + k][0:TT, 0:3 * D], ACT.Square).then_inc(sq_ready, 1)
                    for u in range(2):
                        act.wait_ge(ms_ready, 2 * i + (u + 1))
                        nc.scalar.activation(rms[0:TT, u, :], rms[0:TT, u, :], ACT.Sqrt, bias=eps[0:TT, :],
                                             scale=1.0 / F).then_inc(rms_ready, 1)
                    for u in range(2):
                        act.wait_ge(nT_psum, 2 * i + (u + 1))
                        act.wait_ge(nT_free, 2 * i + (u + 1))
                        act.wait_ge(a_done, 2 * i + (u + 1))
                        for half in range(2):
                            nc.scalar.activation(nT[:, u, half * HALF:(half + 1) * HALF],
                                                 psum[4 * u + half][:, 0:HALF], ACT.Identity).then_inc(nT_ready, 1)
                        for half in range(2):
                            nc.scalar.activation(sq[:, u, half * HALF:(half + 1) * HALF],
                                                 psum[4 * u + half][:, 0:HALF], ACT.Square).then_inc(nT_ready, 1)
                        act.wait_ge(nT_ready, 4 * (2 * i + u) + 4)
                        act.sem_inc(nT_taken, 1)

            @block.gpsimd
            def _(pool):
                pool.wait_ge(setup, 1)
                pool.sem_inc(nT_free, 2)
                with pool.Fori(0, B // 2) as i:
                    chain = Chain(pool, pool_chain, 8 * i, gate)
                    for u in range(2):
                        pool.wait_ge(nT_ready, 4 * (2 * i + u) + 2)
                        pass_gate(pool, pieces_free, 2 * i + (u + 1), gate)
                        chain.link(nc.gpsimd.tensor_scalar(pnT[:, u, :], nT[:, u, :], pcol[:], None, ALU.mult))
                        split(nc.gpsimd, chain, pnT[:, u, :], rest[:, 1, u, :], pieces[:, u], PIECES).then_inc(b_split, 1)
                        pool.wait_ge(b_split, 2 * i + (u + 1))
                        pool.sem_inc(nT_free, 1)

            @block.vector
            def _(dve):
                setup_chain = Chain(dve, dve_chain)
                dve.wait_ge(loaded, 64)
                dve.sem_inc(dmax_ready, 2)
                dve.sem_inc(a_done, 2)
                setup_chain.link(nc.vector.memset(eps[:], RMS_EPS))
                setup_chain.link(nc.vector.tensor_tensor(wT[:], wT[:], wTd[:], ALU.add))
                setup_chain.link(nc.vector.tensor_tensor(pcol[:], gcols[:, 0:1], gcols[:, 1:2], ALU.mult))
                setup_chain.link(nc.vector.tensor_scalar(pcol[:], pcol[:], F ** -0.5, None, ALU.mult))
                setup_chain.link(nc.vector.tensor_scalar(pabs[:], pcol[:], -1.0, None, ALU.mult))
                setup_chain.link(nc.vector.tensor_tensor(pabs[:], pabs[:], pcol[:], ALU.max))
                setup_chain.link(nc.vector.tensor_scalar(bound_w[:], block_ones[:], pabs[:], float(F), ALU.mult, ALU.mult))
                dve.sem_inc(setup, 1)
                with dve.Fori(0, B // 2) as i:
                    chain = Chain(dve, dve_chain, setup_chain.n + i * 28)
                    for u in range(2):
                        for t in range(NT):
                            col = (2 * i + u) * NT + t
                            chain.add(nc.vector.tensor_scalar(
                                xn[0:TT, u, t, :], h[0:TT, bass.ds(col, 1), :], mean[0:TT, bass.ds(col, 1)],
                                rstd[0:TT, bass.ds(col, 1)], ALU.subtract, ALU.mult))
                        chain.settle()
                        dve.sem_inc(xn_ready, 1)
                    for u in range(2):
                        dve.wait_ge(sq_ready, 2 * (2 * i + u) + 2)
                        chain.link(nc.vector.tensor_reduce(rms[0:TT, u, :], squares[0:TT, u, :, :].rearrange(
                            "p t (g f) -> p (t g) f", f=F), AX.X, ALU.add))
                        dve.sem_inc(ms_ready, 1)
                    for u in range(2):
                        dve.wait_ge(rms_ready, 2 * i + (u + 1))
                        chain.link(nc.vector.reciprocal(rms[0:TT, u, :], rms[0:TT, u, :]))
                        for k in range(2):
                            chain.add(nc.vector.tensor_tensor(
                                n_rows[0:TT, u, 3 * k:3 * k + 3, :].rearrange("p t (g f) -> p (t g) f", f=F),
                                psum[4 * u + 2 + k][0:TT, 0:3 * D].rearrange("p (g f) -> p g f", f=F),
                                spread(rms[0:TT, u, 3 * H * k:3 * H * (k + 1)], F), ALU.mult))
                        chain.settle()
                        dve.sem_inc(n_ready, 1)
                        chain.add(nc.vector.tensor_tensor(
                            n3[0:TT, bass.ds((2 * i + u) * NT, NT), :], n_rows[0:TT, u, :, :],
                            g3row[0:TT, :].unsqueeze(1).broadcast_to([TT, NT, D]), ALU.mult))
                    for u in range(2):
                        dve.wait_ge(nT_ready, 4 * (2 * i + u) + 2)
                        dve.wait_ge(pieces_free, 2 * i + (u + 1))
                        split(nc.vector, chain, nT[:, u, :], rest[:, 0, u, :], pieces[:, u], 0).then_inc(a_split, 1)
                        dve.wait_ge(bound_psum, 2 * i + (u + 1))
                        for half in range(2):
                            ins = nc.vector.tensor_reduce(dmax2[:, bass.ds(2 * (2 * i + u) + half, 1)],
                                                          psum[4 * u + 2 + half][:, 0:HALF], AX.X, ALU.max)
                        ins.then_inc(dmax_ready, 1)
                        dve.wait_ge(a_split, 2 * i + (u + 1))
                        dve.sem_inc(a_done, 1)
                    assert chain.n == 12 + 2 + 8 + 6
                dve.wait_ge(dmax_ready, B + 2)
                nc.vector.tensor_reduce(dmax[:], dmax2[:].rearrange("p (b k) -> p b k", k=2), AX.X, ALU.max).then_inc(setup, 1)


def attention(nc, io, h, stats, n3, dmax, pieces_dram, psum_banks, psum, ident, ones):
    EBUFS = 3
    with Memory(nc, "att") as m:
        piece_a = m.sbuf("piece_a", [KROWS, G, 4, L], BF16)
        piece_b = m.sbuf("piece_b", [KROWS, G, 4, L], BF16)
        w2 = m.sbuf("w2", [128, G, D])
        w2d = m.sbuf("w2d", [128, G, D])
        head_start = m.sbuf("head_start", [128, H])
        dsel = m.sbuf("dsel", [128, B, H])
        guard = m.sbuf("guard", [128, B * H])
        e = m.sbuf("e", [128, EBUFS, 4, L])
        z = m.sbuf("z", [128, EBUFS, 4])
        rz = m.sbuf("rz", [128, EBUFS, 4])
        values = m.sbuf("values", [128, EBUFS, 4, 2, F])
        scales = m.sbuf("scales", [128, G, NT, 4, 2, F])
        first_exp = m.sbuf("first_exp", [1, 1])
        scaleT = m.sbuf("scaleT", [128, L])
        ys = m.sbuf("ys", [128, G, L])
        loaded, setup = m.sem("loaded"), m.sem("setup")
        guard_psum = m.sem("guard_psum")
        ab_ready = [m.sem(f"ab_ready{g}") for g in range(G)]
        ab_free = [m.sem(f"ab_free{g}") for g in range(G)]
        att_ready, att_free, e_ready, e_free = (m.sem(s) for s in ("att_ready", "att_free", "e_ready", "e_free"))
        values_ready, scales_ready, scaleT_psum, scaleT_free = (
            m.sem(s) for s in ("values_ready", "scales_ready", "scaleT_psum", "scaleT_free"))
        y_psum, y_free, ys_ready, out_psum, out_free = (
            m.sem(s) for s in ("y_psum", "y_free", "ys_ready", "out_psum", "out_free"))
        dve_chain, dve_done = m.sem("dve_chain"), m.sem("dve_done")
        gate = m.sem("gate")
        SETS = G * NT
        assert SETS % EBUFS == 0
        LAG = 6
        CUTS = [(0, 0, 188), (0, 188, HALF), (1, 0, 188), (1, 188, HALF)]

        def batches(eng, body):
            body(0, True)
            with eng.Fori(1, B) as b:
                body(b, False)

        with nc.Block() as block:
            @block.sync
            def _(sp):
                sp.dma_start(w2[:], io["w_qkv_rows"]).then_inc(loaded, 16)
                sp.dma_start(w2d[:], io["w_delta_rows"]).then_inc(loaded, 16)
                sp.dma_start(head_start[:], io["head_start"]).then_inc(loaded, 16)
                with sp.Fori(0, B) as b:
                    for g in range(G):
                        sp.wait_ge(ab_free[g], b + 1)
                        for dst, which in ((piece_a, [0, 0, 1, 1, 0, 2]), (piece_b, [3, 4, 3, 4, 5, 3])):
                            for k, piece in enumerate(which):
                                src = pieces_dram[bass.ds(b, 1), piece, g * 64:(g + 1) * 64, :]
                                sp.dma_start(dst[k * F:(k + 1) * F, g, :, :],
                                             src.rearrange("o (q f) t -> f (o q) t", f=F)).then_inc(ab_ready[g], 16)

            @block.tensor
            def _(pe):
                pe.wait_ge(setup, 1)
                nc.tensor.matmul(psum[6][:, 0:B * H], ones[:], dsel[:].rearrange("p b h -> p (b h)"),
                                 start=True, stop=True).then_inc(guard_psum, 1)
                pe.sem_inc(ab_free[0], 1)
                pe.sem_inc(ab_free[1], 1)
                pe.wait_ge(setup, 2)

                def scores(b, s, q):
                    g, j = divmod(s, NT)
                    if j == 0 and q == 0:
                        pe.wait_ge(ab_ready[g], 192 * b + 192)
                    pe.wait_ge(att_free, 4 * SETS * b + (4 * s + q + 1))
                    for half in range(2):
                        mm = nc.tensor.matmul(psum[2 * (q % 2) + half][0:TT, 0:HALF],
                                              piece_a[:, g, q, j * TT:(j + 1) * TT],
                                              piece_b[:, g, q, half * HALF:(half + 1) * HALF], start=True, stop=True)
                    mm.then_inc(att_ready, 1)
                    if j == NT - 1 and q == 3:
                        pe.wait_ge(att_ready, 4 * SETS * b + (4 * s + q + 1))
                        pe.sem_inc(ab_free[g], 1)

                def weigh(b, s, k):
                    j = s % NT
                    half, lo, hi = CUTS[k]
                    if j == 0:
                        if k % 2 == 1:
                            lo = hi
                        else:
                            hi = HALF
                    if k == 0:
                        pe.wait_ge(values_ready, SETS * b + (s + 1))
                    if k % 2 == 0 and j == 0:
                        pe.wait_ge(y_free, 2 * G * b + (2 * (s // NT) + half + 1))
                    for q in range(4 if hi > lo else 0):
                        mm = nc.tensor.matmul(psum[4 + half][32 * q:32 * q + 32, lo:hi],
                                              values[0:TT, s % EBUFS, q, :, :].rearrange("p a f -> p (a f)"),
                                              e[0:TT, s % EBUFS, q, half * HALF + lo:half * HALF + hi],
                                              start=(j == 0), stop=(j == NT - 1), skip_group_check=True)
                    if k % 2 == (1 if j > 0 else 0):
                        mm.then_inc(e_free, 1)
                    if k % 2 == 1 and j == NT - 1:
                        pe.wait_ge(e_free, 2 * (SETS * b + s + EBUFS) + half + 1)
                        pe.sem_inc(y_psum, 1)

                def turn_scales(b, g, t):
                    pe.wait_ge(scales_ready, SETS * b + (g * NT + t + 1))
                    if t == 0:
                        pe.wait_ge(out_free, (G + 1) * b + (g + 1))
                    mm = nc.tensor.transpose(psum[6 + t // 3][:, (t % 3) * TT:(t % 3 + 1) * TT],
                                             scales[0:TT, g, t, :, :, :].rearrange("p q a f -> p (q a f)"),
                                             ident[0:TT, 0:TT])
                    if t == NT - 1:
                        mm.then_inc(scaleT_psum, 1)

                def project(b, n):
                    t, g = divmod(n, G)
                    if n == 0:
                        pe.wait_ge(ys_ready, 2 * G * b + 2 * G)
                        pe.wait_ge(out_free, (G + 1) * b + (G + 1))
                    mm = nc.tensor.matmul(psum[6 + t // 3][0:TT, (t % 3) * D:(t % 3 + 1) * D],
                                          ys[:, g, t * TT:(t + 1) * TT], w2[:, g, :],
                                          start=(g == 0), stop=(g == G - 1))
                    if n == G * NT - 1:
                        mm.then_inc(out_psum, 1)

                def body(b, first):
                    for s in range(SETS):
                        for q in range(4):
                            scores(b, s, q)
                            at = 4 * s + q + 1
                            if 4 * NT <= at < 4 * NT + NT:
                                turn_scales(b, 0, at - 4 * NT)
                            if at == 4 * SETS:
                                turn_scales(b, 1, 0)
                            if at < NT and not first:
                                turn_scales(b - 1, 1, at)
                            n = 4 * s + q - LAG
                            if n >= 0:
                                weigh(b, n // 4, n % 4)
                            elif not first:
                                weigh(b - 1, SETS + n // 4, n % 4)
                            at = 4 * s + q - LAG - 4
                            if 0 <= at < G * NT and not first:
                                project(b - 1, at)
                batches(pe, body)
                for n in range(4 * SETS - LAG, 4 * SETS):
                    weigh(B - 1, n // 4, n % 4)
                for t in range(1, NT):
                    turn_scales(B - 1, 1, t)
                for n in range(G * NT):
                    project(B - 1, n)

            @block.scalar
            def _(act):
                act.wait_ge(setup, 2)
                act.sem_inc(att_free, 2)
                act.sem_inc(e_free, 2 * EBUFS)
                act.wait_ge(loaded, 48)
                nc.scalar.activation(first_exp[:], guard[0:1, 0:1], ACT.Exp)
                with act.Fori(0, B) as b:
                    for s in range(SETS):
                        g = s // NT
                        act.wait_ge(e_free, 2 * (SETS * b + s) + 2)
                        for q in range(4):
                            pass_gate(act, att_ready, 4 * SETS * b + (4 * s + q + 1), gate)
                            nc.scalar.activation(
                                e[0:TT, s % EBUFS, q, :].rearrange("p (a t) -> p a t", a=2),
                                psum_banks[0:TT, 2 * (q % 2):2 * (q % 2) + 2, 0:HALF], ACT.Exp,
                                bias=guard[0:TT, bass.ds(H * b + 4 * g + q, 1)],
                                accum_out=z[0:TT, s % EBUFS, q:q + 1]).then_inc(att_free, 1)

            @block.vector
            def _(dve):
                chain = Chain(dve, dve_chain)
                dve.wait_ge(loaded, 48)
                chain.link(nc.vector.memset(scales[:], 1.0))
                chain.link(nc.vector.tensor_tensor(w2[:], w2[:], w2d[:], ALU.add))
                chain.link(nc.vector.tensor_tensor(dsel[:], dmax[:].unsqueeze(2).broadcast_to([128, B, H]),
                                                   head_start[:].unsqueeze(1).broadcast_to([128, B, H]), ALU.mult))
                dve.sem_inc(setup, 1)
                dve.wait_ge(guard_psum, 1)
                chain.link(nc.vector.tensor_scalar(guard[:], psum[6][:, 0:B * H], -1.0, None, ALU.mult))
                dve.sem_inc(y_free, 2)
                dve.sem_inc(out_free, 1)
                dve.sem_inc(setup, 1)

                def turned_scales(b, g, chain):
                    dve.wait_ge(scaleT_psum, G * b + (g + 1))
                    for half in range(2):
                        chain.add(nc.vector.tensor_copy(scaleT[:, half * HALF:(half + 1) * HALF],
                                                        psum[6 + half][:, 0:HALF]))
                    chain.settle()
                    dve.sem_inc(out_free, 1)

                def scaled(b, g, half, chain):
                    dve.wait_ge(y_psum, 2 * (G * b + g) + half + 1)
                    cols = slice(half * HALF, (half + 1) * HALF)
                    chain.link(nc.vector.tensor_tensor(ys[:, g, cols], psum[4 + half][:, 0:HALF],
                                                       scaleT[:, cols], ALU.mult))
                    dve.sem_inc(y_free, 1)
                    dve.sem_inc(ys_ready, 1)

                def residual(b, chain):
                    dve.wait_ge(out_psum, b + 1)
                    for k in range(2):
                        rows = h[0:TT, bass.ds(b * NT + 3 * k, 3), :]
                        chain.add(nc.vector.tensor_tensor(rows, rows, psum[6 + k][0:TT, 0:3 * D].rearrange(
                            "p (t d) -> p t d", d=D), ALU.add))
                    chain.settle()
                    dve.sem_inc(out_free, 1)

                def statistics(b, chain):
                    for t in range(NT):
                        chain.add(nc.vector.bn_stats(stats[0:TT, bass.ds(b * NT + t, 1), :],
                                                     h[0:TT, bass.ds(b * NT + t, 1), :]))
                    chain.settle()

                def weights(b, s, chain):
                    g, j = divmod(s, NT)
                    dve.wait_ge(att_free, 4 * SETS * b + (4 * s + 4 + 2))
                    v = n3[0:TT, bass.ds(b * NT + j, 1), g * 64:(g + 1) * 64].rearrange("p o (q f) -> p (o q) f", f=F)
                    dve.wait_ge(e_free, 2 * (SETS * b + s) + 2)
                    slot = s % EBUFS
                    chain.add(nc.vector.tensor_copy(values[0:TT, slot, :, 0, :], v))
                    chain.link(nc.vector.reciprocal(rz[0:TT, slot, :], z[0:TT, slot, :]))
                    z_inv = rz[0:TT, slot, :].unsqueeze(2).broadcast_to([TT, 4, F])
                    chain.link(nc.vector.tensor_tensor(values[0:TT, slot, :, 1, :], v, z_inv, ALU.mult))
                    dve.sem_inc(values_ready, 1)
                    chain.link(nc.vector.tensor_copy(scales[0:TT, g, j, :, 0, :], z_inv))
                    dve.sem_inc(scales_ready, 1)

                counted = []

                def body(b, first):
                    chain = Chain(dve, dve_done) if first else Chain(dve, dve_done, counted[0] + per_batch * (b - 1))
                    for s in range(SETS):
                        group_end = (b, 0) if s == NT else (b - 1, 1) if s == 0 and not first else None
                        if group_end:
                            turned_scales(*group_end, chain)
                            scaled(*group_end, 0, chain)
                        if s == 5 and not first:
                            residual(b - 1, chain)
                        weights(b, s, chain)
                        if group_end:
                            scaled(*group_end, 1, chain)
                        if s == 5 and not first:
                            statistics(b - 1, chain)
                    if first:
                        counted.append(chain.n)
                    else:
                        assert chain.n == per_batch
                end_of_batch = 2 + 2 + 2 + NT
                per_batch = 4 * SETS + 4 + end_of_batch
                batches(dve, body)
                assert counted[0] == per_batch - end_of_batch
                chain = Chain(dve, dve_done, counted[0] + per_batch * (B - 1))
                turned_scales(B - 1, 1, chain)
                scaled(B - 1, 1, 0, chain)
                scaled(B - 1, 1, 1, chain)
                residual(B - 1, chain)
                statistics(B - 1, chain)


def normalized_tiles(nc, dve, chain, xn, h, mean, rstd, batch):
    for t in range(NT):
        col = batch * NT + t
        chain.add(nc.vector.tensor_scalar(
            xn[0:TT, t, :], h[0:TT, bass.ds(col, 1), :], mean[0:TT, bass.ds(col, 1)],
            rstd[0:TT, bass.ds(col, 1)], ALU.subtract, ALU.mult))
    chain.settle()


def expert_of_batch(nc, io, h, stats, mean, rstd, slots_dram, psum, ident, ones):
    NE = 16
    with Memory(nc, "expert_of_batch") as m:
        xn = m.sbuf("xn", [128, 2, NT, D])
        xnT = m.sbuf("xnT", [128, B, L])
        sums = m.sbuf("sums", [128, B, 2])
        wg = m.sbuf("wg", [128, NE])
        bg = m.sbuf("bg", [1, NE])
        scores = m.sbuf("scores", [1, B, NE])
        best = m.sbuf("best", [1, B])
        picks = m.sbuf("picks", [1, B, NE])
        countdown = m.sbuf("countdown", [1, NE])
        gate = m.sbuf("gate", [1, B])
        index = m.sbuf("index", [1, B], I32)
        gates = m.sbuf("gates", [128, B])
        w_sel = m.sbuf("w_sel", [128, B, D])
        b_sel = m.sbuf("b_sel", [1, B, D])
        w_gated = m.sbuf("w_gated", [128, 2, D])
        b_gated = m.sbuf("b_gated", [1, 2, D])
        xT = m.sbuf("xT", [128, 2, L])
        loaded, xn_ready, xnT_psum, xnT_ready, scores_psum = (
            m.sem(s) for s in ("loaded", "xn_ready", "xnT_psum", "xnT_ready", "scores_psum"))
        dve_chain, exp_in, exp_out, index_ready, picked, gates_psum = (
            m.sem(s) for s in ("dve_chain", "exp_in", "exp_out", "index_ready", "picked", "gates_psum"))
        gates_ready, gated_ready, xT_ready, xT_free, y_psum, y_free = (
            m.sem(s) for s in ("gates_ready", "gated_ready", "xT_ready", "xT_free", "y_psum", "y_free"))
        zeros = m.sbuf("zeros", [128, NEXP * SLOTS * D // 128 // ZERO_PARTS])
        zeros_made, zeros_stored = m.sem("zeros_made"), m.sem("zeros_stored")
        slots_flat = slots_dram.rearrange("r d -> (r d)").rearrange("(k p n) -> k p n", k=ZERO_PARTS, p=128)
        with nc.Block() as block:
            @block.gpsimd
            def _(pool):
                nc.gpsimd.memset(zeros[:], 0.0).then_inc(zeros_made, 1)
                pool.wait_ge(zeros_made, 1)
                for k in range(ZERO_PARTS):
                    pool.dma_start(slots_flat[k], zeros[:]).then_inc(zeros_stored, 16)
                pool.wait_ge(zeros_stored, 16 * ZERO_PARTS)

            @block.sync
            def _(sp):
                sp.dma_start(wg[:], io["moe0_wg"]).then_inc(loaded, 16)
                sp.dma_start(bg[:], io["moe0_bg"]).then_inc(loaded, 16)
                sp.dma_start(countdown[:], io["countdown"]).then_inc(loaded, 16)
                sp.wait_ge(index_ready, 1)
                for b in range(B):
                    e = sp.value_load(index[0:1, b:b + 1], min_val=0, max_val=NE - 1)
                    sp.dma_start(w_sel[:, b, :], io["moe0_we"][bass.ds(e, 1), :, :].rearrange("o p n -> p (o n)")
                                 ).then_inc(picked, 16)
                    sp.dma_start(b_sel[:, b, :], io["moe0_be"][bass.ds(e, 1), :]).then_inc(picked, 16)

            @block.tensor
            def _(pe):
                with pe.Fori(0, B // 2) as i:
                    for u in range(2):
                        pe.wait_ge(xn_ready, 2 * i + (u + 1))
                        pe.wait_ge(xT_free, 2 * i + (u + 1))
                        for t in range(NT):
                            mm = nc.tensor.transpose(psum[2 * u + t // 3][:, (t % 3) * TT:(t % 3 + 1) * TT],
                                                     xn[0:TT, u, t, :], ident[0:TT, 0:TT])
                        mm.then_inc(xnT_psum, 1)
                pe.wait_ge(xnT_ready, 2 * B)
                pe.wait_ge(loaded, 48)
                for b in range(B):
                    for half in range(2):
                        mm = nc.tensor.matmul(psum[4][0:1, b * NE:(b + 1) * NE], sums[:, b, half:half + 1], wg[:],
                                              start=(half == 0), stop=(half == 1))
                mm.then_inc(scores_psum, 1)
                pe.wait_ge(gates_ready, 1)
                nc.tensor.matmul(psum[5][:, 0:B], ones[0:1, :], gate[:], start=True, stop=True).then_inc(gates_psum, 1)
                with pe.Fori(0, B // 2) as i:
                    for u in range(2):
                        pe.wait_ge(gated_ready, 2 * i + (u + 1))
                        pe.wait_ge(xT_ready, 2 * i + (u + 1))
                        pe.wait_ge(y_free, 2 * i + (u + 1))
                        for t in range(NT):
                            out = psum[2 * u + t // 3][0:TT, (t % 3) * D:(t % 3 + 1) * D]
                            nc.tensor.matmul(out, ones[0:1, 0:TT], b_gated[:, u, :], start=True, stop=False)
                            mm = nc.tensor.matmul(out, xT[:, u, t * TT:(t + 1) * TT], w_gated[:, u, :],
                                                  start=False, stop=True)
                        mm.then_inc(y_psum, 1)

            @block.scalar
            def _(act):
                act.sem_inc(xT_free, 2)
                with act.Fori(0, B // 2) as i:
                    for u in range(2):
                        act.wait_ge(xnT_psum, 2 * i + (u + 1))
                        for half in range(2):
                            nc.scalar.activation(
                                xnT[:, bass.ds(2 * i + u, 1), half * HALF:(half + 1) * HALF],
                                psum[2 * u + half][:, 0:HALF], ACT.Identity,
                                accum_out=sums[:, bass.ds(2 * i + u, 1), half:half + 1].rearrange("p a b -> p (a b)")
                            ).then_inc(xnT_ready, 1)
                        act.wait_ge(xnT_ready, 2 * (2 * i + u) + 2)
                        act.sem_inc(xT_free, 1)
                act.wait_ge(exp_in, 1)
                nc.scalar.activation(picks[:], scores[:], ACT.Exp).then_inc(exp_out, 1)
                with act.Fori(0, B // 2) as i:
                    for u in range(2):
                        act.wait_ge(y_free, 2 * i + (u + 1))
                        act.sem_inc(xT_free, 1)
                        nc.scalar.activation(xT[:, u, :], xnT[:, bass.ds(2 * i + u, 1), :],
                                             ACT.Identity).then_inc(xT_ready, 1)

            @block.vector
            def _(dve):
                with dve.Fori(0, B // 2) as i:
                    chain = Chain(dve, dve_chain, 2 * NT * i)
                    for u in range(2):
                        dve.wait_ge(xT_free, 2 * i + (u + 1))
                        normalized_tiles(nc, dve, chain, xn[:, u], h, mean, rstd, 2 * i + u)
                        dve.sem_inc(xn_ready, 1)
                chain = Chain(dve, dve_chain, NTILES)
                dve.wait_ge(scores_psum, 1)
                wide = best[:].unsqueeze(2).broadcast_to([1, B, NE])
                chain.link(nc.vector.scalar_tensor_tensor(
                    out=scores[:], in0=psum[4][0:1, 0:B * NE].rearrange("p (b e) -> p b e", e=NE), scalar=1.0 / L,
                    in1=bg[:].unsqueeze(1).broadcast_to([1, B, NE]), op0=ALU.mult, op1=ALU.add))
                chain.link(nc.vector.tensor_reduce(best[:], scores[:], AX.X, ALU.max))
                chain.link(nc.vector.tensor_tensor(scores[:], scores[:], wide, ALU.subtract))
                dve.sem_inc(exp_in, 1)
                dve.wait_ge(exp_out, 1)
                chain.link(nc.vector.tensor_reduce(gate[:], picks[:], AX.X, ALU.add))
                chain.link(nc.vector.reciprocal(gate[:], gate[:]))
                dve.sem_inc(gates_ready, 1)
                chain.link(nc.vector.tensor_scalar(picks[:], scores[:], 0.0, None, ALU.is_ge))
                chain.link(nc.vector.tensor_tensor(picks[:], picks[:], countdown[:].unsqueeze(1).broadcast_to([1, B, NE]), ALU.mult))
                chain.link(nc.vector.tensor_reduce(best[:], picks[:], AX.X, ALU.max))
                chain.link(nc.vector.tensor_scalar(index[:], best[:], -1.0, float(NE), ALU.mult, ALU.add))
                dve.sem_inc(index_ready, 1)
                dve.wait_ge(gates_psum, 1)
                chain.link(nc.vector.tensor_copy(gates[:], psum[5][:, 0:B]))
                dve.wait_ge(picked, 32 * B)
                dve.sem_inc(y_free, 2)
                after = NTILES + chain.n
                with dve.Fori(0, B // 2) as i:
                    chain = Chain(dve, dve_chain, after + 2 * (4 + NT) * i)
                    for u in range(2):
                        b = 2 * i + u
                        chain.add(nc.vector.tensor_scalar(w_gated[:, u, :], w_sel[:, bass.ds(b, 1), :],
                                                          gates[:, bass.ds(b, 1)], None, ALU.mult))
                        chain.add(nc.vector.tensor_scalar(b_gated[:, u, :], b_sel[:, bass.ds(b, 1), :],
                                                          gates[0:1, bass.ds(b, 1)], None, ALU.mult))
                        chain.settle()
                        dve.sem_inc(gated_ready, 1)
                    for u in range(2):
                        dve.wait_ge(y_psum, 2 * i + (u + 1))
                        for k in range(2):
                            rows = h[0:TT, bass.ds((2 * i + u) * NT + 3 * k, 3), :]
                            chain.add(nc.vector.tensor_tensor(rows, rows, psum[2 * u + k][0:TT, 0:3 * D].rearrange(
                                "p (t d) -> p t d", d=D), ALU.add))
                        chain.settle()
                        dve.sem_inc(y_free, 1)
                        for t in range(NT):
                            chain.add(nc.vector.bn_stats(stats[0:TT, bass.ds((2 * i + u) * NT + t, 1), :],
                                                         h[0:TT, bass.ds((2 * i + u) * NT + t, 1), :]))
                        chain.settle()
                    assert chain.n == 2 * (4 + NT)


C = 10
SUB = C // 2
NCH = L // C
HALVES = [(0, 38 * C), (38 * C, L)]
NCOEF = 3 * SUB * SUB


def delta_projections(nc, io, h, mean, rstd, kq_all, v_all, beta, k_rows_dram, psum, ident):
    with Memory(nc, "proj") as m:
        w_kq = m.sbuf("w_kq", [128, 2 * D])
        w_v = m.sbuf("w_v", [128, D])
        w_b = m.sbuf("w_b", [128, D])
        xn = m.sbuf("xn", [128, NT, D])
        xnT = m.sbuf("xnT", [128, L])
        sq = m.sbuf("sq", [128, NT, 2 * D])
        norm = m.sbuf("norm", [128, NT * 2 * H])
        kqn = m.sbuf("kqn", [128, NT, 2 * D])
        turned = m.sbuf("turned", [128, 2, L])
        names = ("loaded xn_ready xnT_psum xnT_ready v_psum v_taken kq_psum sq_ready norm_sq norm_ready kqn_ready "
                 "b_psum b_taken kT_psum kT_ready k_taken q_taken kT_free k_stored k_free xn_chain kept_chain dve_chain act_chain")
        s = {n: m.sem(n) for n in names.split()}

        def batches(eng, body):
            body(0, False, True)
            with eng.Fori(1, B - 1) as b:
                body(b, True, True)
            body(B - 1, True, False)

        with nc.Block() as block:
            @block.sync
            def _(sp):
                sp.dma_start(w_kq[:, 0:D], io["wk"]).then_inc(s["loaded"], 16)
                sp.dma_start(w_kq[:, D:2 * D], io["wq"]).then_inc(s["loaded"], 16)
                sp.dma_start(w_v[:], io["wv"]).then_inc(s["loaded"], 16)
                sp.dma_start(w_b[:], io["wb"]).then_inc(s["loaded"], 16)
                sp.sem_inc(s["k_free"], 1)
                with sp.Fori(0, B) as b:
                    sp.wait_ge(s["kqn_ready"], b + 1)
                    sp.dma_start(k_rows_dram[bass.ds(b, 1), :, :].rearrange("o (t p) d -> p (o t) d", p=TT),
                                 kqn[0:TT, :, 0:D]).then_inc(s["k_stored"], 16)
                    sp.wait_ge(s["k_stored"], 16 * b + 16)
                    sp.sem_inc(s["k_free"], 1)

            @block.tensor
            def _(pe):
                pe.wait_ge(s["loaded"], 64)

                def x_turned(b):
                    pe.wait_ge(s["xn_ready"], b + 1)
                    pe.wait_ge(s["q_taken"], b + 1)
                    for t in range(NT):
                        mm = nc.tensor.transpose(psum[t // 3][:, (t % 3) * TT:(t % 3 + 1) * TT],
                                                 xn[0:TT, t, :], ident[0:TT, 0:TT])
                    mm.then_inc(s["xnT_psum"], 1)

                def kq_turned(b):
                    for which, base in enumerate((5, 0)):
                        if which == 0:
                            pe.wait_ge(s["v_taken"], b + 1)
                        for t in range(NT):
                            mm = nc.tensor.transpose(psum[base + t // 3][:, (t % 3) * TT:(t % 3 + 1) * TT],
                                                     kqn[0:TT, t, which * D:(which + 1) * D], ident[0:TT, 0:TT])
                        mm.then_inc(s["kT_psum"], 1)

                def rates(b, half):
                    pe.wait_ge(s["b_taken"], 2 * b + half + 1)
                    lo, hi = HALVES[half]
                    nc.tensor.matmul(psum[7][:, 0:hi - lo], w_b[:], xnT[:, lo:hi], start=True, stop=True
                                     ).then_inc(s["b_psum"], 1)

                def body(b, before, follows):
                    pe.wait_ge(s["xnT_ready"], 2 * b + 2)
                    if before:
                        pe.wait_ge(s["kqn_ready"], b)
                    for t in range(NT):
                        mm = nc.tensor.matmul(psum[2 + t // 2][0:TT, (t % 2) * 2 * D:(t % 2 + 1) * 2 * D],
                                              xnT[:, t * TT:(t + 1) * TT], w_kq[:], start=True, stop=True)
                    mm.then_inc(s["kq_psum"], 1)
                    if before:
                        kq_turned(b - 1)
                    rates(b, 0)
                    pe.wait_ge(s["k_taken"], b + 1)
                    for half, (lo, hi) in enumerate(HALVES):
                        mm = nc.tensor.matmul(psum[5 + half][:, 0:hi - lo], w_v[:], xnT[:, lo:hi], start=True, stop=True)
                    mm.then_inc(s["v_psum"], 1)
                    rates(b, 1)
                    if follows:
                        x_turned(b + 1)
                x_turned(0)
                batches(pe, body)
                pe.wait_ge(s["kqn_ready"], B)
                kq_turned(B - 1)

            @block.scalar
            def _(act):
                act.sem_inc(s["k_taken"], 1)
                act.sem_inc(s["q_taken"], 2)
                act.sem_inc(s["b_taken"], 1)

                def x_turned(b):
                    act.wait_ge(s["xnT_psum"], b + 1)
                    for half in range(2):
                        nc.scalar.activation(xnT[:, half * HALF:(half + 1) * HALF], psum[half][:, 0:HALF],
                                             ACT.Identity).then_inc(s["xnT_ready"], 1)

                def kq_turned(b, which):
                    act.wait_ge(s["kT_psum"], 2 * b + which + 1)
                    act.wait_ge(s["kT_free"], 2 * b + which + 1)
                    base = 0 if which else 5
                    for half in range(2):
                        nc.scalar.activation(turned[:, which, half * HALF:(half + 1) * HALF],
                                             psum[base + half][:, 0:HALF], ACT.Identity).then_inc(s["kT_ready"], 1)
                    act.wait_ge(s["kT_ready"], 4 * b + 2 * which + 2)
                    act.sem_inc(s["q_taken" if which else "k_taken"], 1)

                def rates(b, half):
                    act.wait_ge(s["b_psum"], 2 * b + half + 1)
                    lo, hi = HALVES[half]
                    nc.scalar.activation(beta[:, bass.ds(b, 1), lo:hi], psum[7][:, 0:hi - lo], ACT.Identity
                                         ).then_inc(s["b_taken"], 1)

                def body(b, before, follows):
                    act.wait_ge(s["kq_psum"], b + 1)
                    for k in range(3):
                        ins = nc.scalar.activation(sq[0:TT, 2 * k:2 * k + 2, :], psum[2 + k][0:TT, :], ACT.Square)
                    ins.then_inc(s["sq_ready"], 1)
                    if before:
                        kq_turned(b - 1, 0)
                    act.wait_ge(s["norm_sq"], b + 1)
                    nc.scalar.activation(norm[0:TT, :], norm[0:TT, :], ACT.Sqrt).then_inc(s["norm_ready"], 1)
                    if before:
                        kq_turned(b - 1, 1)
                    rates(b, 0)
                    rates(b, 1)
                    if follows:
                        x_turned(b + 1)
                x_turned(0)
                batches(act, body)
                kq_turned(B - 1, 0)
                kq_turned(B - 1, 1)
                act.wait_ge(s["b_taken"], 2 * B + 1)
                nc.scalar.activation(beta[:], beta[:], ACT.Sigmoid).then_inc(s["act_chain"], 1)

            @block.vector
            def _(dve):
                dve.sem_inc(s["kT_free"], 2)

                def normalized(b):
                    if b is not first_batch:
                        dve.wait_ge(s["xnT_psum"], b)
                    chain = Chain(dve, s["xn_chain"], NT * b)
                    normalized_tiles(nc, dve, chain, xn, h, mean, rstd, b)
                    dve.sem_inc(s["xn_ready"], 1)

                def kept(b, which):
                    dve.wait_ge(s["kT_ready"], 4 * b + 2 * which + 2)
                    chain = Chain(dve, s["kept_chain"], 2 * b + which)
                    chain.link(nc.vector.tensor_copy(
                        kq_all[:, :, bass.ds(b, 1), which, :].rearrange("p c o t -> p c (o t)"),
                        turned[:, which, :].rearrange("p (c t) -> p c t", t=C)))
                    dve.sem_inc(s["kT_free"], 1)

                def body(b, before, follows):
                    if follows:
                        normalized(b + 1)
                    chain = Chain(dve, s["dve_chain"], 7 * b)
                    dve.wait_ge(s["sq_ready"], b + 1)
                    chain.link(nc.vector.tensor_reduce(norm[0:TT, :], sq[0:TT, :, :].rearrange("p t (g f) -> p (t g) f", f=F),
                                                       AX.X, ALU.add))
                    dve.sem_inc(s["norm_sq"], 1)
                    dve.wait_ge(s["norm_ready"], b + 1)
                    chain.link(nc.vector.reciprocal(norm[0:TT, :], norm[0:TT, :]))
                    if before:
                        dve.wait_ge(s["kT_ready"], 4 * b)
                    dve.wait_ge(s["k_free"], b + 1)
                    for k in range(3):
                        chain.add(nc.vector.tensor_tensor(
                            kqn[0:TT, 2 * k:2 * k + 2, :].rearrange("p t (g f) -> p (t g) f", f=F),
                            psum[2 + k][0:TT, :].rearrange("p (g f) -> p g f", f=F),
                            spread(norm[0:TT, 32 * k:32 * k + 32], F), ALU.mult))
                    chain.settle()
                    dve.sem_inc(s["kqn_ready"], 1)
                    if before:
                        kept(b - 1, 0)
                        kept(b - 1, 1)
                    dve.wait_ge(s["v_psum"], b + 1)
                    for half, (lo, hi) in enumerate(HALVES):
                        chain.add(nc.vector.tensor_copy(
                            v_all[:, lo // C:hi // C, bass.ds(b, 1), :].rearrange("p c o t -> p c (o t)"),
                            psum[5 + half][:, 0:hi - lo].rearrange("p (c t) -> p c t", t=C)))
                    chain.settle()
                    dve.sem_inc(s["v_taken"], 1)
                    assert chain.n == 7
                first_batch = 0
                normalized(first_batch)
                batches(dve, body)
                kept(B - 1, 0)
                kept(B - 1, 1)


def triangular_coefficients(nc, kq_all, beta, coef_dram, psum, block_sum):
    with Memory(nc, "coef") as m:
        products = m.sbuf("products", [128, 2, L])
        inv = m.sbuf("inv", [128, NCH, 2, SUB, SUB])
        neg = m.sbuf("neg", [128, NCH, 2, SUB, SUB])
        cross = m.sbuf("cross", [128, NCH, SUB * SUB])
        out = m.sbuf("out", [128, NCH, NCOEF])
        term = m.sbuf("term", [128, NCH, 2, SUB])
        names = "products_ready products_free dots_psum dots_free dve_chain pool_chain cross_ready cross_free out_ready out_free stored gate"
        s = {n: m.sem(n) for n in names.split()}
        groups = []
        for d in range(1, C):
            width = C - d
            per = 512 // width
            for lo in range(0, NCH, per):
                groups.append((d, width, lo, min(NCH, lo + per)))
        ND = C - 1
        RING = 6
        assert len(groups) % RING == 0

        with nc.Block() as block:
            @block.sync
            def _(sp):
                sp.sem_inc(s["out_free"], 1)
                with sp.Fori(0, B) as b:
                    sp.wait_ge(s["out_ready"], b + 1)
                    sp.dma_start(coef_dram[bass.ds(b, 1), :, :, :].rearrange("o p c k -> p (o c) k"),
                                 out[:]).then_inc(s["stored"], 16)
                    sp.wait_ge(s["stored"], 16 * b + 16)
                    sp.sem_inc(s["out_free"], 1)

            @block.gpsimd
            def _(pool):
                with pool.Fori(0, B) as b:
                    for d in range(1, C):
                        pass_gate(pool, s["products_free"], ND * b + d + (d == 1), s["gate"])
                        width = C - d
                        nc.gpsimd.tensor_tensor(
                            products[:, d % 2, 0:NCH * width].rearrange("p (c t) -> p c t", t=width),
                            kq_all[:, :, bass.ds(b, 1), 0, d:C].rearrange("p c o t -> p c (o t)"),
                            kq_all[:, :, bass.ds(b, 1), 0, 0:width].rearrange("p c o t -> p c (o t)"),
                            ALU.mult).then_inc(s["products_ready"], 1)

            @block.tensor
            def _(pe):
                pe.sem_inc(s["products_free"], 2)
                with pe.Fori(0, B) as b:
                    for n, (d, width, lo, hi) in enumerate(groups):
                        if lo == 0:
                            pe.wait_ge(s["products_ready"], ND * b + d)
                        pe.wait_ge(s["dots_free"], len(groups) * b + n + 1)
                        nc.tensor.matmul(psum[n % RING][:, 0:(hi - lo) * width], block_sum[:],
                                         products[:, d % 2, lo * width:hi * width], start=True, stop=True
                                         ).then_inc(s["dots_psum"], 1)
                        if hi == NCH:
                            pe.wait_ge(s["dots_psum"], len(groups) * b + n + 1)
                            pe.sem_inc(s["products_free"], 1)

            @block.scalar
            def _(act):
                act.sem_inc(s["cross_free"], 1)
                with act.Fori(0, B) as b:
                    act.wait_ge(s["cross_ready"], b + 1)
                    act.wait_ge(s["out_free"], b + 1)
                    nc.scalar.activation(out[:, :, SUB * SUB:2 * SUB * SUB], cross[:], ACT.Identity
                                         ).then_inc(s["cross_free"], 1)

            @block.vector
            def _(dve):
                first = Chain(dve, s["dve_chain"])
                first.add(nc.vector.memset(inv[:], 0.0))
                first.add(nc.vector.memset(neg[:], 0.0))
                first.settle()
                for t in range(SUB):
                    first.add(nc.vector.memset(inv[:, :, :, t, t], 1.0))
                first.settle()
                dve.sem_inc(s["dots_free"], RING)

                def batch(b, base):
                    chain = Chain(dve, s["dve_chain"], base)
                    dve.wait_ge(s["cross_free"], b + 1)
                    for n, (d, width, lo, hi) in enumerate(groups):
                        dve.wait_ge(s["dots_psum"], len(groups) * b + n + 1)
                        dots = psum[n % RING][:, 0:(hi - lo) * width].rearrange("p (c t) -> p c t", t=width)
                        before = chain.n
                        for part in range(2):
                            k = SUB - d
                            if k <= 0:
                                continue
                            dst = neg[:, lo:hi, part, :, :].rearrange("p c t s -> p c (t s)")[:, :, d * SUB:d * SUB + (k - 1) * (SUB + 1) + 1:SUB + 1]
                            times = beta[:, bass.ds(b, 1), :].rearrange("p o (c t) -> p (o c) t", t=C)[:, lo:hi, part * SUB + d:part * SUB + SUB]
                            chain.add(nc.vector.scalar_tensor_tensor(
                                out=dst, in0=dots[:, :, part * SUB:part * SUB + k], scalar=-1.0, in1=times,
                                op0=ALU.mult, op1=ALU.mult))
                        s0, s1 = max(0, SUB - d), min(SUB, C - d)
                        t0 = s0 + d - SUB
                        at = t0 * SUB + s0
                        dst = cross[:, lo:hi, at:at + (s1 - s0 - 1) * (SUB + 1) + 1:SUB + 1]
                        chain.add(nc.vector.tensor_scalar(dst, dots[:, :, s0:s1], -1.0, None, ALU.mult))
                        if n > 0:
                            dve.wait_ge(s["dve_chain"], base + before)
                            dve.sem_inc(s["dots_free"], 1)
                    chain.settle()
                    dve.sem_inc(s["dots_free"], 1)
                    dve.sem_inc(s["cross_ready"], 1)
                    flat_inv = inv[:].rearrange("p c a t s -> p (c a) t s")
                    flat_neg = neg[:].rearrange("p c a t s -> p (c a) t s")
                    flat_term = term[:].rearrange("p c a s -> p (c a) s")
                    NB = 2 * NCH
                    for t in range(1, SUB):
                        chain.add(nc.vector.tensor_copy(flat_inv[:, :, t, 0:t], flat_neg[:, :, t, 0:t]))
                    chain.settle()
                    for t in range(1, SUB):
                        for r in range(1, t):
                            chain.link(nc.vector.tensor_tensor(
                                flat_term[:, :, 0:r], flat_inv[:, :, r, 0:r],
                                flat_neg[:, :, t, r:r + 1].broadcast_to([128, NB, r]), ALU.mult))
                            chain.link(nc.vector.tensor_tensor(
                                flat_inv[:, :, t, 0:r], flat_inv[:, :, t, 0:r], flat_term[:, :, 0:r], ALU.add))
                    dve.wait_ge(s["out_free"], b + 1)
                    for part in range(2):
                        beta_s = beta[:, bass.ds(b, 1), :].rearrange("p o (c t) -> p (o c) t", t=C)[:, :, part * SUB:(part + 1) * SUB]
                        at = 2 * SUB * SUB * part
                        chain.add(nc.vector.tensor_tensor(
                            out[:, :, at:at + SUB * SUB].rearrange("p c (t s) -> p c t s", s=SUB), inv[:, :, part],
                            beta_s.unsqueeze(2).broadcast_to([128, NCH, SUB, SUB]), ALU.mult))
                    chain.settle()
                    dve.wait_ge(s["cross_free"], b + 2)
                    dve.sem_inc(s["out_ready"], 1)
                    return chain.n

                per = sum(1 + 2 * (SUB - d > 0) for d, _, _, _ in groups) + (SUB - 1) + 2 * sum(t - 1 for t in range(1, SUB)) + 2
                with dve.Fori(0, B) as b:
                    assert batch(b, first.n + per * b) == per


RING = 3
STREAMS = 2
BS = B // STREAMS


def delta_rule(nc, io, kq_all, v_all, u_all, o_all, k_rows_dram, coef_dram, psum_banks, psum):
    with Memory(nc, "delta") as m:
        masks = m.sbuf("masks", [128, 2])
        kq = m.sbuf("kq", [128, RING, B, 2 * C])
        k_rows = m.sbuf("k_rows", [128, RING, B, 32])
        coef = m.sbuf("coef", [128, 2, B, RING, NCOEF])
        state = m.sbuf("state", [128, B, 32])
        r = m.sbuf("r", [128, STREAMS, BS, SUB])
        prod = m.sbuf("prod", [128, STREAMS, BS, SUB, SUB])
        coupling = m.sbuf("coupling", [128, STREAMS, BS, SUB, SUB + 1])
        coupled = m.sbuf("coupled", [128, STREAMS, BS, SUB])
        u_pad = m.sbuf("u_pad", [128, RING, B, 32])
        u_rows = m.sbuf("u_rows", [128, RING, B, 32])
        loaded, gate, pool_gate, zeroed = m.sem("loaded"), m.sem("gate"), m.sem("pool_gate"), m.sem("zeroed")
        kq_ready, kq_free = m.sem("kq_ready"), m.sem("kq_free")
        rows_free = m.sem("rows_free")
        rows_ready = [m.sem(f"rows_ready{u}") for u in range(RING)]
        coef_ready = [m.sem(f"coef_ready{k}") for k in range(2)]
        coef_free = m.sem("coef_free")
        r_psum = [m.sem(f"r_psum{x}") for x in range(STREAMS)]
        u_ready = [m.sem(f"u_ready{x}") for x in range(STREAMS)]
        s_psum = [m.sem(f"s_psum{x}") for x in range(STREAMS)]
        s_ready = [m.sem(f"s_ready{x}") for x in range(STREAMS)]
        q_taken = [m.sem(f"q_taken{x}") for x in range(STREAMS)]
        r_taken = [m.sem(f"r_taken{x}") for x in range(STREAMS)]
        act_gate = m.sem("act_gate")
        u_kept = m.sem("u_kept")
        dve_chain = m.sem("dve_chain")
        SOLVE = 9

        def own(x):
            return slice(x * BS, (x + 1) * BS)

        def chunks(eng, body):
            for u in range(RING):
                body(u, u, u == 0, 0, 0, 1)
            with eng.Fori(0, (NCH - RING) // (2 * RING)) as i:
                for k in range(2):
                    for u in range(RING):
                        body(2 * RING * i + (RING * (k + 1) + u), u, False, 2 * i + (k + 1), 1 - k, i + (k + 1))

        with nc.Block() as block:
            @block.sync
            def _(sp):
                sp.dma_start(masks[:], io["pair_masks"]).then_inc(loaded, 16)

                def body(c, u, first, turn, half, uses):
                    sp.wait_ge(rows_free, c + 1)
                    for w in range(4):
                        src = k_rows_dram[:, bass.ds(c * C, C), 32 * w:32 * w + 32].rearrange("b t k -> t b k")
                        sp.dma_start(k_rows[32 * w:32 * w + C, u, :, :], src).then_inc(rows_ready[u], 16)
                    if u == 0:
                        sp.wait_ge(coef_free, turn + 1)
                        sp.dma_start(coef[:, half].rearrange("p b c k -> p b (c k)"),
                                     coef_dram[:, :, bass.ds(c, RING), :].rearrange("b p c k -> p b (c k)")
                                     ).then_inc(coef_ready[half], 16)
                chunks(sp, body)

            @block.gpsimd
            def _(pool):
                def body(c, u, first, turn, half, uses):
                    pass_gate(pool, kq_free, c + 1, pool_gate)
                    nc.gpsimd.tensor_copy(kq[:, u, :, :], kq_all[:, bass.ds(c, 1), :, :, :].rearrange(
                        "p o b a t -> p (o b) (a t)")).then_inc(kq_ready, 1)
                    if not first:
                        keep_u(c - 1, (u - 1) % RING)

                def keep_u(c, u):
                    pool.wait_ge(u_ready[0], c + 1)
                    pass_gate(pool, u_ready[1], c + 1, pool_gate)
                    nc.gpsimd.tensor_copy(u_all[:, bass.ds(c, 1), :, :].rearrange("p o b t -> p (o b) t"),
                                          u_pad[:, u, :, 0:C]).then_inc(u_kept, 1)
                pool.sem_inc(u_kept, RING)
                chunks(pool, body)
                keep_u(NCH - 1, RING - 1)

            @block.tensor
            def _(pe):
                pe.sem_inc(rows_free, RING)
                pe.sem_inc(kq_free, RING)
                pe.wait_ge(zeroed, 1)
                for w in range(4):
                    nc.tensor.matmul(psum[6][32 * w:32 * w + 32, 0:32 * B], state[32 * w:32 * w + 32, 0, :],
                                     state[32 * w:32 * w + 32, :, :].rearrange("p b k -> p (b k)"),
                                     start=True, stop=False, skip_group_check=True)
                for w in range(4):
                    nc.tensor.matmul(psum[7][32 * w:32 * w + 32, 0:32 * B], state[32 * w:32 * w + 32, 0, :],
                                     state[32 * w:32 * w + 32, :, :].rearrange("p b k -> p (b k)"),
                                     start=True, stop=False, skip_group_check=True)

                def residuals(c, u, x):
                    if x == 0:
                        pe.wait_ge(kq_ready, c + 1)
                    pe.wait_ge(q_taken[x], c + 1)
                    pass_gate(pe, s_ready[x], c + 1, gate)
                    for b in range(x * BS, (x + 1) * BS):
                        for w in range(4):
                            rows = slice(32 * w, 32 * w + 32)
                            mm = nc.tensor.matmul(psum[RING * x + u][rows, 2 * C * b:2 * C * (b + 1)], state[rows, b, :],
                                                  kq[rows, u, b, :], start=True, stop=True)
                    mm.then_inc(r_psum[x], 1)

                def add_updates(c, u, x, turn):
                    if x == 0:
                        pe.wait_ge(rows_ready[u], 64 * turn + 64)
                    pass_gate(pe, u_ready[x], c + 1, gate)
                    for b in range(x * BS, (x + 1) * BS):
                        for w in range(4):
                            rows = slice(32 * w, 32 * w + C)
                            mm = nc.tensor.matmul(psum[6 + x][32 * w:32 * w + 32, 32 * b:32 * b + 32], k_rows[rows, u, b, :],
                                                  u_rows[rows, u, b, :], start=False, stop=False, skip_group_check=True)
                    mm.then_inc(s_psum[x], 1)
                    if x == 1:
                        pass_gate(pe, s_psum[x], c + 1, gate)
                        pe.sem_inc(rows_free, 1)
                        pe.sem_inc(kq_free, 1)

                def body(c, u, first, turn, half, uses):
                    residuals(c, u, 0)
                    if not first:
                        add_updates(c - 1, (u - 1) % RING, 1, None)
                    residuals(c, u, 1)
                    add_updates(c, u, 0, turn)
                chunks(pe, body)
                add_updates(NCH - 1, RING - 1, 1, None)

            @block.scalar
            def _(act):
                act.wait_ge(loaded, 16)
                act.wait_ge(zeroed, 1)
                for x in range(STREAMS):
                    act.sem_inc(s_ready[x], 1)
                    act.sem_inc(q_taken[x], RING)

                def keep_q(c, u, x):
                    pass_gate(act, r_taken[x], c + 1, act_gate)
                    nc.scalar.activation(
                        o_all[:, bass.ds(c, 1), own(x), :].rearrange("p o b t -> p (o b) t"),
                        psum[RING * x + u][:, 2 * C * BS * x:2 * C * BS * (x + 1)].rearrange(
                            "p (b a) -> p b a", a=2 * C)[:, :, C:2 * C], ACT.Identity).then_inc(q_taken[x], 1)

                def new_state(c, x):
                    act.wait_ge(s_psum[x], c + 1)
                    for head in range(2):
                        ins = nc.scalar.activation(
                            state[:, own(x), F * head:F * head + F],
                            psum[6 + x][:, 32 * BS * x:32 * BS * (x + 1)].rearrange("p (b k) -> p b k", k=32)[:, :, F * head:F * head + F],
                            ACT.Identity, scale=masks[:, head:head + 1])
                    ins.then_inc(s_ready[x], 1)

                def body(c, u, first, turn, half, uses):
                    if not first:
                        new_state(c - 1, 1)
                    keep_q(c, u, 0)
                    new_state(c, 0)
                    keep_q(c, u, 1)
                chunks(act, body)

            @block.vector
            def _(dve):
                zero = Chain(dve, zeroed)
                zero.add(nc.vector.memset(state[:], 0.0))
                nc.vector.memset(u_pad[:], 0.0).then_inc(dve_chain, 1)
                dve.sem_inc(coef_free, 2)

                def body(c, u, first, turn, half, uses):
                    chain = Chain(dve, dve_chain, STREAMS * SOLVE * c + 1)
                    for x in range(STREAMS):
                        dve.wait_ge(r_psum[x], c + 1)
                        if x == 0:
                            dve.wait_ge(coef_ready[half], 16 * uses)
                            dve.wait_ge(u_kept, c + 1)
                        b = own(x)
                        r_x, p_x, w_x, terms = r[:, x], prod[:, x], coupled[:, x], coupling[:, x]
                        inv1, cross, inv2 = (coef[:, half, b, u, k * SUB * SUB:(k + 1) * SUB * SUB].rearrange(
                            "p b (t s) -> p b t s", s=SUB) for k in range(3))

                        def along(values):
                            return values.unsqueeze(2).broadcast_to([128, BS, SUB, SUB])

                        def residual(out, lo, hi):
                            return nc.vector.tensor_tensor(
                                out, v_all[:, bass.ds(c, 1), b, lo:hi].rearrange("p o b t -> p (o b) t"),
                                psum[RING * x + u][:, 2 * C * BS * x:2 * C * BS * (x + 1)].rearrange(
                                    "p (b a) -> p b a", a=2 * C)[:, :, lo:hi], ALU.subtract)
                        chain.add(residual(r_x, 0, SUB))
                        chain.link(residual(terms[:, :, :, SUB], SUB, C))
                        dve.sem_inc(r_taken[x], 1)
                        chain.link(nc.vector.tensor_tensor(p_x, inv1, along(r_x), ALU.mult))
                        chain.link(nc.vector.tensor_reduce(u_pad[:, u, b, 0:SUB], p_x, AX.X, ALU.add))
                        chain.link(nc.vector.tensor_tensor(terms[:, :, :, 0:SUB], cross, along(u_pad[:, u, b, 0:SUB]), ALU.mult))
                        chain.link(nc.vector.tensor_reduce(w_x, terms, AX.X, ALU.add))
                        chain.link(nc.vector.tensor_tensor(p_x, inv2, along(w_x), ALU.mult))
                        chain.link(nc.vector.tensor_reduce(u_pad[:, u, b, SUB:C], p_x, AX.X, ALU.add))
                        chain.link(nc.vector.transpose(u_rows[:, u, b, :].rearrange("p b k -> p (b k)"),
                                                       u_pad[:, u, b, :].rearrange("p b k -> p (b k)")))
                        dve.sem_inc(u_ready[x], 1)
                    if u == RING - 1:
                        dve.sem_inc(coef_free, 1)
                chunks(dve, body)


def within_chunks(nc, kq_all, u_all, o_all, psum, block_sum):
    BUFS = C // 2
    with Memory(nc, "within") as m:
        products = m.sbuf("products", [128, BUFS, L])
        terms = m.sbuf("terms", [128, 3, 512])
        names = "products_ready products_free dots_psum dots_free dve_chain gate"
        s = {n: m.sem(n) for n in names.split()}
        groups = []
        for d in range(C):
            width = C - d
            per = 512 // width
            for lo in range(0, NCH, per):
                groups.append((d, width, lo, min(NCH, lo + per)))
        BANKS = 7
        assert len(groups) % BANKS == 0 and C % 2 == 0

        with nc.Block() as block:
            @block.gpsimd
            def _(pool):
                with pool.Fori(0, B) as b:
                    for d in range(C):
                        pass_gate(pool, s["products_free"], C * b + d + 1, s["gate"])
                        width = C - d
                        nc.gpsimd.tensor_tensor(
                            products[:, d % BUFS, 0:NCH * width].rearrange("p (c t) -> p c t", t=width),
                            kq_all[:, :, bass.ds(b, 1), 1, d:C].rearrange("p c o t -> p c (o t)"),
                            kq_all[:, :, bass.ds(b, 1), 0, 0:width].rearrange("p c o t -> p c (o t)"),
                            ALU.mult).then_inc(s["products_ready"], 1)

            @block.tensor
            def _(pe):
                pe.sem_inc(s["products_free"], BUFS)
                with pe.Fori(0, B) as b:
                    for n, (d, width, lo, hi) in enumerate(groups):
                        if lo == 0:
                            pe.wait_ge(s["products_ready"], C * b + d + 1)
                        pe.wait_ge(s["dots_free"], len(groups) * b + n + 1)
                        nc.tensor.matmul(psum[n % BANKS][:, 0:(hi - lo) * width], block_sum[:],
                                         products[:, d % BUFS, lo * width:hi * width], start=True, stop=True
                                         ).then_inc(s["dots_psum"], 1)
                        if n > 0 and groups[n - 1][3] == NCH:
                            pe.wait_ge(s["dots_psum"], len(groups) * b + n)
                            pe.sem_inc(s["products_free"], 1)
                    pe.wait_ge(s["dots_psum"], len(groups) * b + len(groups))
                    pe.sem_inc(s["products_free"], 1)

            @block.vector
            def _(dve):
                dve.sem_inc(s["dots_free"], BANKS)
                with dve.Fori(0, B) as b:
                    chain = Chain(dve, s["dve_chain"], 2 * len(groups) * b)
                    for n in range(len(groups) + 1):
                        issued = chain.n
                        if n < len(groups):
                            d, width, lo, hi = groups[n]
                            dve.wait_ge(s["dots_psum"], len(groups) * b + n + 1)
                            dots = psum[n % BANKS][:, 0:(hi - lo) * width].rearrange("p (c t) -> p c t", t=width)
                            term = terms[:, n % 3, 0:(hi - lo) * width].rearrange("p (c t) -> p c t", t=width)
                            chain.add(nc.vector.tensor_tensor(term, dots, u_all[:, lo:hi, bass.ds(b, 1), 0:width].rearrange(
                                "p c o t -> p c (o t)"), ALU.mult))
                        if n > 0:
                            dve.wait_ge(s["dve_chain"], chain.base + issued)
                            dve.sem_inc(s["dots_free"], 1)
                            d, width, lo, hi = groups[n - 1]
                            term = terms[:, (n - 1) % 3, 0:(hi - lo) * width].rearrange("p (c t) -> p c t", t=width)
                            o = o_all[:, lo:hi, bass.ds(b, 1), d:C].rearrange("p c o t -> p c (o t)")
                            chain.add(nc.vector.tensor_tensor(o, o, term, ALU.add))
                    chain.settle()
                    assert chain.n == 2 * len(groups)


def delta_output(nc, io, h, stats, mean, rstd, o_all, psum, ident, ones):
    with Memory(nc, "output") as m:
        wo = m.sbuf("wo", [128, D])
        ln_cols = m.sbuf("ln_cols", [128, 2])
        wc = m.sbuf("wc", [128, D])
        b_wide = m.sbuf("b_wide", [128, TT])
        bwo = m.sbuf("bwo", [128, D])
        oT = m.sbuf("oT", [128, 2, L])
        yvar = m.sbuf("yvar", [128, NTILES])
        ytmp = m.sbuf("ytmp", [128, NTILES])
        names = "loaded oT_ready oT_free o_psum o_free wg_ready w_psum b_ready w_ready dve_chain var_ready root_ready o2_ready o2_free z_psum z_free"
        s = {n: m.sem(n) for n in names.split()}

        def batch_of_o(b):
            return o_all[:, :, bass.ds(b, 1), :].rearrange("p c o t -> p c (o t)")

        def turned(u):
            return oT[:, u, :].rearrange("p (c t) -> p c t", t=C)

        with nc.Block() as block:
            @block.sync
            def _(sp):
                sp.dma_start(wo[:], io["wo"]).then_inc(s["loaded"], 16)
                sp.dma_start(ln_cols[:], io["ln_cols"]).then_inc(s["loaded"], 16)

            @block.tensor
            def _(pe):
                pe.wait_ge(s["wg_ready"], 1)
                nc.tensor.matmul(psum[4][:, 0:D], ones[:], wc[:], start=True, stop=True)
                nc.tensor.matmul(psum[5][0:TT, 0:D], b_wide[:], wo[:], start=True, stop=True).then_inc(s["w_psum"], 1)
                with pe.Fori(0, B // 2) as i:
                    for u in range(2):
                        pe.wait_ge(s["oT_ready"], 2 * i + (u + 1))
                        pe.wait_ge(s["o_free"], 2 * i + (u + 1))
                        for t in range(NT):
                            mm = nc.tensor.transpose(psum[2 * u + t // 3][0:TT, (t % 3) * D:(t % 3 + 1) * D],
                                                     oT[:, u, t * TT:(t + 1) * TT], ident[:])
                        mm.then_inc(s["o_psum"], 1)
                pe.wait_ge(s["w_ready"], 1)
                with pe.Fori(0, B // 2) as i:
                    for u in range(2):
                        pe.wait_ge(s["o2_ready"], 2 * i + (u + 1))
                        pe.wait_ge(s["z_free"], 2 * i + (u + 1))
                        for t in range(NT):
                            mm = nc.tensor.matmul(psum[2 * u + t // 3][0:TT, (t % 3) * D:(t % 3 + 1) * D],
                                                  oT[:, u, t * TT:(t + 1) * TT], wc[:], start=True, stop=True)
                        mm.then_inc(s["z_psum"], 1)

            @block.scalar
            def _(act):
                act.sem_inc(s["oT_free"], 2)
                with act.Fori(0, B // 2) as i:
                    for u in range(2):
                        act.wait_ge(s["oT_free"], 2 * i + (u + 1))
                        nc.scalar.activation(turned(u), batch_of_o(2 * i + u), ACT.Identity).then_inc(s["oT_ready"], 1)
                        act.wait_ge(s["o_psum"], 2 * i + (u + 1))
                        act.sem_inc(s["oT_free"], 1)
                act.wait_ge(s["var_ready"], 1)
                nc.scalar.activation(ytmp[0:TT, :], yvar[0:TT, :], ACT.Sqrt).then_inc(s["root_ready"], 1)
                act.sem_inc(s["o2_free"], 2)
                with act.Fori(0, B // 2) as i:
                    for u in range(2):
                        act.wait_ge(s["o2_free"], 2 * i + (u + 1))
                        nc.scalar.activation(turned(u), batch_of_o(2 * i + u), ACT.Identity).then_inc(s["o2_ready"], 1)
                        act.wait_ge(s["z_psum"], 2 * i + (u + 1))
                        act.sem_inc(s["o2_free"], 1)

            @block.vector
            def _(dve):
                chain = Chain(dve, s["dve_chain"])
                dve.wait_ge(s["loaded"], 32)
                chain.link(nc.vector.tensor_scalar(wc[:], wo[:], ln_cols[:, 0:1], None, ALU.mult))
                chain.link(nc.vector.tensor_copy(b_wide[:], ln_cols[:, 1:2].broadcast_to([128, TT])))
                dve.sem_inc(s["wg_ready"], 1)
                dve.wait_ge(s["w_psum"], 1)
                chain.link(nc.vector.scalar_tensor_tensor(out=wc[:], in0=psum[4][:, 0:D], scalar=-1.0 / D, in1=wc[:],
                                                          op0=ALU.mult, op1=ALU.add))
                chain.link(nc.vector.tensor_copy(bwo[0:TT, :], psum[5][0:TT, 0:D]))
                dve.sem_inc(s["w_ready"], 1)
                dve.sem_inc(s["o_free"], 2)
                before = chain.n
                with dve.Fori(0, B // 2) as i:
                    chain = Chain(dve, s["dve_chain"], before + 2 * NT * i)
                    for u in range(2):
                        dve.wait_ge(s["o_psum"], 2 * i + (u + 1))
                        for t in range(NT):
                            chain.add(nc.vector.bn_stats(stats[0:TT, bass.ds((2 * i + u) * NT + t, 1), :],
                                                         psum[2 * u + t // 3][0:TT, (t % 3) * D:(t % 3 + 1) * D]))
                        chain.settle()
                        dve.sem_inc(s["o_free"], 1)
                chain = Chain(dve, s["dve_chain"], before + NTILES)
                moments(nc, dve, chain, stats, mean[0:TT, :], yvar[0:TT, :], ytmp[0:TT, :])
                dve.sem_inc(s["var_ready"], 1)
                dve.wait_ge(s["root_ready"], 1)
                chain.link(nc.vector.reciprocal(rstd[0:TT, :], ytmp[0:TT, :]))
                refine_rsqrt(nc, chain, rstd[0:TT, :], yvar[0:TT, :], ytmp[0:TT, :])
                dve.sem_inc(s["z_free"], 2)
                before += NTILES + chain.n
                with dve.Fori(0, B // 2) as i:
                    chain = Chain(dve, s["dve_chain"], before + 2 * (1 + 2 * NT) * i)
                    for u in range(2):
                        rows = h[0:TT, bass.ds((2 * i + u) * NT, NT), :]
                        chain.link(nc.vector.tensor_tensor(rows, rows, bwo[0:TT, :].unsqueeze(1).broadcast_to([TT, NT, D]), ALU.add))
                        dve.wait_ge(s["z_psum"], 2 * i + (u + 1))
                        for t in range(NT):
                            col = (2 * i + u) * NT + t
                            row = h[0:TT, bass.ds(col, 1), :].rearrange("p o d -> p (o d)")
                            chain.add(nc.vector.scalar_tensor_tensor(
                                out=row, in0=psum[2 * u + t // 3][0:TT, (t % 3) * D:(t % 3 + 1) * D],
                                scalar=rstd[0:TT, bass.ds(col, 1)], in1=row, op0=ALU.mult, op1=ALU.add))
                        chain.settle()
                        dve.sem_inc(s["z_free"], 1)
                        for t in range(NT):
                            chain.add(nc.vector.bn_stats(stats[0:TT, bass.ds((2 * i + u) * NT + t, 1), :],
                                                         h[0:TT, bass.ds((2 * i + u) * NT + t, 1), :]))
                        chain.settle()
                    assert chain.n == 2 * (1 + 2 * NT)


def route(nc, io, h, mean, rstd, xn, weight, slot_in, slot_out, psum, ident, ones):
    with Memory(nc, "route") as m:
        w_hash = m.sbuf("w_hash", [128, ACTIVE])
        buckets = m.sbuf("buckets", [128, NEXP])
        earlier = m.sbuf("earlier", [128, 128])
        earlier16 = m.sbuf("earlier16", [128, 128], BF16)
        ones16 = m.sbuf("ones16", [128, 128], BF16)
        xT = m.sbuf("xT", [128, 2, 3, TT])
        score = m.sbuf("score", [128, NTILES, ACTIVE])
        whole = m.sbuf("whole", [128, NTILES, ACTIVE], I32)
        floor = m.sbuf("floor", [128, NTILES, ACTIVE])
        above = m.sbuf("above", [128, NTILES, ACTIVE])
        expert = m.sbuf("expert", [128, NTILES, ACTIVE])
        hot = m.sbuf("hot", [128, ACTIVE, NTILES, NEXP], BF16)
        both = m.sbuf("both", [128, NTILES, NEXP], BF16)
        prior = m.sbuf("prior", [128, NTILES, NEXP], BF16)
        product = m.sbuf("product", [128, NTILES, NEXP])
        place = m.sbuf("place", [128, ACTIVE, NTILES])
        same = m.sbuf("same", [128, NTILES])
        full = m.sbuf("full", [128, ACTIVE, NTILES])
        slot = m.sbuf("slot", [128, ACTIVE, NTILES])
        names = "loaded chain x_ready xT_psum xT_ready xT_bank_free score_psum hot_ready prior_ready rank_psum"
        s = {n: m.sem(n) for n in names.split()}
        per_bank = 512 // NEXP
        BIG = float(2 * NEXP * SLOTS)

        with nc.Block() as block:
            @block.sync
            def _(sp):
                sp.dma_start(w_hash[:], io["w_hash_T"]).then_inc(s["loaded"], 16)
                sp.dma_start(buckets[:], io["buckets"].partition_broadcast(128)).then_inc(s["loaded"], 16)
                sp.dma_start(earlier[:], io["earlier"]).then_inc(s["loaded"], 16)

            @block.tensor
            def _(pe):
                pe.wait_ge(s["loaded"], 48)
                for g in range(NTILES // 3):
                    pe.wait_ge(s["x_ready"], g // 2 + 1)
                    if g >= 2:
                        pe.wait_ge(s["xT_ready"], g - 1)
                    for t in range(3):
                        mm = nc.tensor.transpose(psum[g % 2][:, t * TT:(t + 1) * TT], xn[0:TT, 3 * g + t, :],
                                                 ident[0:TT, 0:TT])
                    mm.then_inc(s["xT_psum"], 1)
                    if g >= 1:
                        pe.wait_ge(s["xT_ready"], g)
                        for t in range(3):
                            tile = 3 * (g - 1) + t
                            mm = nc.tensor.matmul(psum[2][0:TT, ACTIVE * tile:ACTIVE * (tile + 1)],
                                                  xT[:, (g - 1) % 2, t, :], w_hash[:], start=True, stop=True)
                        mm.then_inc(s["score_psum"], 1)
                g = NTILES // 3
                pe.wait_ge(s["xT_ready"], g)
                for t in range(3):
                    tile = 3 * (g - 1) + t
                    mm = nc.tensor.matmul(psum[2][0:TT, ACTIVE * tile:ACTIVE * (tile + 1)],
                                          xT[:, (g - 1) % 2, t, :], w_hash[:], start=True, stop=True)
                mm.then_inc(s["score_psum"], 1)
                pe.wait_ge(s["hot_ready"], 1)
                for k in range(NTILES // per_bank):
                    out = psum[k][0:TT, :].rearrange("p (t e) -> p t e", e=NEXP)
                    tiles = slice(k * per_bank, (k + 1) * per_bank)
                    nc.tensor.matmul(out, earlier16[0:TT, 0:TT], both[0:TT, tiles, :], start=True, stop=False)
                    pe.wait_ge(s["prior_ready"], 1)
                    mm = nc.tensor.matmul(out, ones16[0:TT, 0:TT], prior[0:TT, tiles, :], start=False, stop=True)
                    mm.then_inc(s["rank_psum"], 1)

            @block.scalar
            def _(act):
                for g in range(NTILES // 3):
                    act.wait_ge(s["xT_psum"], g + 1)
                    if g >= 2:
                        act.wait_ge(s["score_psum"], g - 1)
                    nc.scalar.activation(xT[:, g % 2, :, :].rearrange("p t k -> p (t k)"),
                                         psum[g % 2][:, 0:3 * TT], ACT.Identity).then_inc(s["xT_ready"], 1)

            @block.vector
            def _(dve):
                chain = Chain(dve, s["chain"])
                for b in range(B):
                    normalized_tiles(nc, dve, chain, xn[:, b * NT:(b + 1) * NT, :], h, mean, rstd, b)
                    dve.sem_inc(s["x_ready"], 1)
                dve.wait_ge(s["loaded"], 48)
                chain.add(nc.vector.tensor_copy(earlier16[:], earlier[:]))
                chain.add(nc.vector.tensor_copy(ones16[:], ones[:]))
                dve.wait_ge(s["score_psum"], NTILES // 3)
                chain.link(nc.vector.tensor_scalar(
                    score[0:TT], psum[2][0:TT, 0:NTILES * ACTIVE].rearrange("p (t a) -> p t a", a=ACTIVE),
                    BUCKET_SCALE, None, ALU.mult))
                chain.link(nc.vector.tensor_copy(whole[0:TT], score[0:TT]))
                chain.link(nc.vector.tensor_copy(floor[0:TT], whole[0:TT]))
                chain.link(nc.vector.tensor_tensor(above[0:TT], floor[0:TT], score[0:TT], ALU.is_gt))
                chain.link(nc.vector.tensor_tensor(floor[0:TT], floor[0:TT], above[0:TT], ALU.subtract))
                chain.link(nc.vector.tensor_copy(whole[0:TT], floor[0:TT]))
                chain.link(nc.vector.tensor_single_scalar(whole[0:TT], whole[0:TT], NEXP - 1, ALU.bitwise_and))
                chain.link(nc.vector.tensor_copy(expert[0:TT], whole[0:TT]))
                for a in range(ACTIVE):
                    chain.add(nc.vector.tensor_tensor(
                        hot[0:TT, a], expert[0:TT, :, a:a + 1].broadcast_to([TT, NTILES, NEXP]),
                        buckets[0:TT, :].unsqueeze(1).broadcast_to([TT, NTILES, NEXP]), ALU.is_equal))
                chain.settle()
                chain.link(nc.vector.tensor_tensor(both[0:TT], hot[0:TT, 0], hot[0:TT, 1], ALU.add))
                dve.sem_inc(s["hot_ready"], 1)
                chain.link(nc.vector.memset(prior[0:TT, 0, :], 0.0))
                for t in range(NTILES - 1):
                    chain.link(nc.vector.tensor_tensor(prior[0:TT, t + 1, :], prior[0:TT, t, :], both[0:TT, t, :], ALU.add))
                dve.sem_inc(s["prior_ready"], 1)
                chain.link(nc.vector.tensor_tensor(same[0:TT], expert[0:TT, :, 0], expert[0:TT, :, 1], ALU.is_equal))
                dve.wait_ge(s["rank_psum"], NTILES // per_bank)
                for a in range(ACTIVE):
                    for k in range(NTILES // per_bank):
                        tiles = slice(k * per_bank, (k + 1) * per_bank)
                        chain.add(nc.vector.tensor_tensor(
                            product[0:TT, tiles, :], psum[k][0:TT, :].rearrange("p (t e) -> p t e", e=NEXP),
                            hot[0:TT, a, tiles, :], ALU.mult))
                    chain.settle()
                    chain.link(nc.vector.tensor_reduce(place[0:TT, a], product[0:TT], AX.X, ALU.add))
                chain.link(nc.vector.tensor_tensor(place[0:TT, 1], place[0:TT, 1], same[0:TT], ALU.add))
                chain.link(nc.vector.tensor_scalar(full[0:TT], place[0:TT], float(CAP), None, ALU.is_ge))
                for a in range(ACTIVE):
                    chain.add(nc.vector.scalar_tensor_tensor(
                        out=slot[0:TT, a], in0=expert[0:TT, :, a], scalar=float(SLOTS), in1=place[0:TT, a],
                        op0=ALU.mult, op1=ALU.add))
                chain.settle()
                chain.link(nc.vector.scalar_tensor_tensor(
                    out=place[0:TT], in0=full[0:TT], scalar=BIG, in1=slot[0:TT], op0=ALU.mult, op1=ALU.add))
                chain.add(nc.vector.tensor_copy(slot_in[0:TT], place[0:TT]))
                chain.link(nc.vector.tensor_scalar(weight[0:TT], full[0:TT], -0.5, 0.5, ALU.mult, ALU.add))
                chain.link(nc.vector.tensor_scalar(same[0:TT], weight[0:TT, 0], 2.0, None, ALU.mult))
                chain.link(nc.vector.tensor_tensor(slot[0:TT, 0], slot[0:TT, 0], same[0:TT], ALU.mult))
                chain.link(nc.vector.tensor_scalar(same[0:TT], weight[0:TT, 1], 2.0, None, ALU.mult))
                chain.link(nc.vector.tensor_tensor(slot[0:TT, 1], slot[0:TT, 1], same[0:TT], ALU.mult))
                chain.link(nc.vector.tensor_copy(slot_out[0:TT], slot[0:TT]))


def experts(nc, io, xn, slot_in, slots_dram, y_dram, psum, ident):
    U = 4
    with Memory(nc, "experts") as m:
        w1 = m.sbuf("w1", [128, U, DFF])
        w2 = m.sbuf("w2", [128, U, FCH, D])
        b1 = m.sbuf("b1", [128, NEXP, FCH])
        b2 = m.sbuf("b2", [128, NEXP, D])
        x = m.sbuf("x", [128, U, 2, D])
        xT = m.sbuf("xT", [128, 2, SLOTS])
        inner = m.sbuf("inner", [128, 2, FCH, SLOTS])
        y = m.sbuf("y", [128, U, 2, D])
        biases, sent = m.sem("biases"), m.sem("sent")
        got = [m.sem(f"got_{u}") for u in range(U)]
        put = [m.sem(f"put_{u}") for u in range(U)]
        names = "turned_psum xT_ready inner_psum inner_ready y_psum y_ready y_free"
        s = {n: m.sem(n) for n in names.split()}
        ROUNDS = NEXP // U
        later = lambda i, u, n: (i + (u + n) // U, (u + n) % U)
        rows = lambda dram, e: dram[bass.ds(e * SLOTS, SLOTS), :].rearrange("(s p) d -> p s d", p=HP)
        w1_of = lambda e: io["moe1_w1"][bass.ds(e, 1), :, :].rearrange("o p f -> p (o f)")
        w2_of = lambda e: io["moe1_w2"][bass.ds(e, 1), :, :].rearrange("o (p j) d -> p (o j) d", j=FCH)

        with nc.Block() as block:
            @block.sync
            def _(sp):
                def load_weights(e, u):
                    sp.dma_start(w1[:, u, :], w1_of(e)).then_inc(got[u], 16)
                    sp.dma_start(w2[:, u], w2_of(e)).then_inc(got[u], 16)

                def load_x(e, u):
                    sp.dma_start(x[0:HP, u], rows(slots_dram, e)).then_inc(got[u], 16)

                for u in range(U):
                    load_weights(u, u)
                sp.dma_start(b1[:], io["moe1_b1"]).then_inc(biases, 16)
                sp.dma_start(b2[:], io["moe1_b2"].partition_broadcast(128)).then_inc(biases, 16)
                sp.wait_ge(sent, 16 * NTILES * ACTIVE)
                for u in range(U):
                    load_x(u, u)
                with sp.Fori(0, ROUNDS - 1) as i:
                    for u in range(U):
                        sp.wait_ge(s["y_psum"], U * i + (u + 1) + 2)
                        load_weights(U * (i + 1) + u, u)
                        load_x(U * (i + 1) + u, u)

            @block.gpsimd
            def _(pool):
                for t in range(NTILES):
                    for a in range(ACTIVE):
                        nc.gpsimd.indirect_dma_start(
                            slots_dram, bass.IndirectOffsetOnAxis(slot_in[0:TT, a, t:t + 1], 0), xn[0:TT, t, :], None,
                            bounds_check=NEXP * SLOTS - 1, oob_is_err=False).then_inc(sent, 16)
                with pool.Fori(0, ROUNDS) as i:
                    for u in range(U):
                        pool.wait_ge(s["y_ready"], U * i + (u + 1) + 2)
                        pool.dma_start(rows(y_dram, U * i + u), y[0:HP, u]).then_inc(put[u], 16)
                        pool.wait_ge(put[u], 16 * i + 16)
                        pool.sem_inc(s["y_free"], 1)

            @block.tensor
            def _(pe):
                def turn(i, u):
                    e = U * i + u
                    pe.wait_ge(got[u], 48 * i + 48)
                    pe.wait_ge(s["xT_ready"], e + 1)
                    for k in range(2):
                        mm = nc.tensor.transpose(psum[4 + u % 2][:, k * HP:(k + 1) * HP], x[0:HP, u, k, :],
                                                 ident[0:HP, 0:HP])
                    mm.then_inc(s["turned_psum"], 1)

                def first(i, u):
                    e = U * i + u
                    pe.wait_ge(s["xT_ready"], e + 1 + 2)
                    for j in range(FCH):
                        pe.wait_ge(s["inner_ready"], FCH * e + (j + 1))
                        nc.tensor.matmul(psum[j][:, 0:SLOTS], w1[:, u, :].rearrange("p (k j) -> p k j", j=FCH)[:, :, j],
                                         xT[:, u % 2, :], start=True, stop=True).then_inc(s["inner_psum"], 1)

                def second(i, u):
                    e = U * i + u
                    pe.wait_ge(s["y_ready"], e + 1)
                    for k in range(2):
                        for j in range(FCH):
                            pe.wait_ge(s["inner_ready"], FCH * e + (j + 1) + FCH)
                            mm = nc.tensor.matmul(psum[6 + u % 2][0:HP, k * D:(k + 1) * D],
                                                  inner[:, u % 2, j, k * HP:(k + 1) * HP], w2[:, u, j, :],
                                                  start=(j == 0), stop=(j == FCH - 1))
                    mm.then_inc(s["y_psum"], 1)

                turn(0, 0)
                first(0, 0)
                turn(0, 1)
                with pe.Fori(0, ROUNDS - 1) as i:
                    for u in range(U):
                        first(*later(i, u, 1))
                        turn(*later(i, u, 2))
                        second(i, u)
                for u in range(U):
                    if u + 1 < U:
                        first(ROUNDS - 1, u + 1)
                    if u + 2 < U:
                        turn(ROUNDS - 1, u + 2)
                    second(ROUNDS - 1, u)

            @block.scalar
            def _(act):
                act.sem_inc(s["inner_ready"], FCH)
                act.wait_ge(biases, 32)
                with act.Fori(0, ROUNDS) as i:
                    for u in range(U):
                        e = U * i + u
                        act.wait_ge(s["y_psum"], e + 1)
                        for j in range(FCH):
                            act.wait_ge(s["inner_psum"], FCH * e + (j + 1) + 2 * FCH)
                            nc.scalar.activation(inner[:, u % 2, j, :], psum[j][:, 0:SLOTS], ACT.Gelu,
                                                 bias=b1[:, bass.ds(e, 1), j:j + 1].rearrange("p o j -> p (o j)")
                                                 ).then_inc(s["inner_ready"], 1)

            @block.vector
            def _(dve):
                dve.sem_inc(s["xT_ready"], 2)
                dve.sem_inc(s["y_ready"], 2)
                dve.sem_inc(s["inner_psum"], 2 * FCH)
                dve.sem_inc(s["y_psum"], 2)
                dve.sem_inc(s["y_free"], U)

                def turned(i, u):
                    e = U * i + u
                    dve.wait_ge(s["turned_psum"], e + 1)
                    dve.wait_ge(s["inner_psum"], FCH * (e + 1))
                    nc.vector.tensor_copy(xT[:, u % 2, :], psum[4 + u % 2][:, 0:SLOTS]).then_inc(s["xT_ready"], 1)

                def biased(i, u):
                    e = U * i + u
                    if u == 0:
                        dve.wait_ge(biases, 32)
                    dve.wait_ge(s["y_psum"], e + 1 + 2)
                    dve.wait_ge(s["y_free"], e + 1)
                    nc.vector.tensor_tensor(
                        y[0:HP, u], psum[6 + u % 2][0:HP, 0:2 * D].rearrange("p (k d) -> p k d", d=D),
                        b2[0:HP, bass.ds(e, 1), :].broadcast_to([HP, 2, D]), ALU.add).then_inc(s["y_ready"], 1)

                turned(0, 0)
                turned(0, 1)
                with dve.Fori(0, ROUNDS - 1) as i:
                    for u in range(U):
                        turned(*later(i, u, 2))
                        biased(i, u)
                for u in range(U):
                    if u + 2 < U:
                        turned(ROUNDS - 1, u + 2)
                    biased(ROUNDS - 1, u)


def combine(nc, h, weight, slot_out, y_dram, out):
    R = 4
    with Memory(nc, "combine") as m:
        y = m.sbuf("y", [128, R, ACTIVE, D])
        got = [m.sem(f"got_{r}") for r in range(R)]
        used, done, chain_sem, stored = m.sem("used"), m.sem("done"), m.sem("chain"), m.sem("stored")
        out_tiles = out.rearrange("b (t p) d -> p (b t) d", p=TT)
        with nc.Block() as block:
            @block.gpsimd
            def _(pool):
                for t in range(NTILES):
                    if t >= R:
                        pool.wait_ge(used, t - R + 1)
                    for a in range(ACTIVE):
                        nc.gpsimd.indirect_dma_start(
                            y[0:TT, t % R, a, :], None, y_dram,
                            bass.IndirectOffsetOnAxis(slot_out[0:TT, a, t:t + 1], 0),
                            bounds_check=NEXP * SLOTS - 1, oob_is_err=False).then_inc(got[t % R], 16)

            @block.vector
            def _(dve):
                chain = Chain(dve, chain_sem)
                for t in range(NTILES):
                    dve.wait_ge(got[t % R], 16 * ACTIVE * (t // R + 1))
                    for a in range(ACTIVE):
                        chain.link(nc.vector.scalar_tensor_tensor(
                            out=h[0:TT, t, :], in0=y[0:TT, t % R, a, :], scalar=weight[0:TT, a, t:t + 1],
                            in1=h[0:TT, t, :], op0=ALU.mult, op1=ALU.add))
                    dve.sem_inc(used, 1)

            @block.sync
            def _(sp):
                for g in range(NTILES // NT):
                    sp.wait_ge(used, NT * (g + 1))
                    tiles = slice(g * NT, (g + 1) * NT)
                    sp.dma_start(out_tiles[:, tiles, :], h[0:TT, tiles, :]).then_inc(stored, 16)
                sp.wait_ge(stored, 16 * (NTILES // NT))


def tower(nc, io, out):
    pieces_dram = nc.dram_tensor("head_pieces", (B, 2 * PIECES, D, L), BF16).ap()
    k_rows_dram = nc.dram_tensor("key_rows", (B, L, D), FP32).ap()
    coef_dram = nc.dram_tensor("chunk_coefficients", (B, 128, NCH, NCOEF), FP32).ap()
    slots_dram = nc.dram_tensor("slot_rows", (NEXP * SLOTS, D), FP32).ap()
    y_dram = nc.dram_tensor("result_rows", (NEXP * SLOTS, D), FP32).ap()
    with Memory(nc, "tower") as m:
        h = m.sbuf("h", [128, NTILES, D])
        stats = m.sbuf("stats", [128, NTILES, 6])
        mean = m.sbuf("mean", [128, NTILES])
        rstd = m.sbuf("rstd", [128, NTILES])
        ident = m.sbuf("ident", [128, 128])
        ones = m.sbuf("ones", [128, 128])
        banks = m.stack.enter_context(nc.psum_tensor("tower_banks", [128, 8, 512], FP32))
        psum = [banks[:, i, :] for i in range(8)]
        load_constants(nc, "constants", [(ident, io["ident"]), (ones, io["ones"])])

        convolution(nc, io, h, stats, psum, ident)

        layernorm_scalars(nc, "ln1", stats, mean, rstd)
        with Memory(nc, "attention_values") as a:
            n3 = a.sbuf("n3", [128, NTILES, D])
            dmax = a.sbuf("dmax", [128, B])
            block_ones = a.sbuf("block_ones", [128, 128])
            load_constants(nc, "block_constants", [(block_ones, io["block_ones"])])
            head_vectors(nc, io, h, mean, rstd, n3, dmax, pieces_dram, psum, ident, block_ones)
            attention(nc, io, h, stats, n3, dmax, pieces_dram, banks, psum, ident, ones)
        layernorm_scalars(nc, "ln2", stats, mean, rstd)
        expert_of_batch(nc, io, h, stats, mean, rstd, slots_dram, psum, ident, ones)

        layernorm_scalars(nc, "ln3", stats, mean, rstd)
        with Memory(nc, "delta_values") as a:
            kq_all = a.sbuf("kq_all", [128, NCH, B, 2, C])
            v_all = a.sbuf("v_all", [128, NCH, B, C])
            block_sum = a.sbuf("block_sum", [128, 128])
            load_constants(nc, "sum_constants", [(block_sum, io["block_sum"])])
            with Memory(nc, "delta_rates") as r:
                beta = r.sbuf("beta", [128, B, L])
                delta_projections(nc, io, h, mean, rstd, kq_all, v_all, beta, k_rows_dram, psum, ident)
                triangular_coefficients(nc, kq_all, beta, coef_dram, psum, block_sum)
            u_all = a.sbuf("u_all", [128, NCH, B, C])
            o_all = a.sbuf("o_all", [128, NCH, B, C])
            delta_rule(nc, io, kq_all, v_all, u_all, o_all, k_rows_dram, coef_dram, banks, psum)
            within_chunks(nc, kq_all, u_all, o_all, psum, block_sum)
            delta_output(nc, io, h, stats, mean, rstd, o_all, psum, ident, ones)

        layernorm_scalars(nc, "ln4", stats, mean, rstd)
        with Memory(nc, "routing") as a:
            xn = a.sbuf("xn", [128, NTILES, D])
            weight = a.sbuf("weight", [128, ACTIVE, NTILES])
            slot_in = a.sbuf("slot_in", [128, ACTIVE, NTILES], I32)
            slot_out = a.sbuf("slot_out", [128, ACTIVE, NTILES], I32)
            route(nc, io, h, mean, rstd, xn, weight, slot_in, slot_out, psum, ident, ones)
            experts(nc, io, xn, slot_in, slots_dram, y_dram, psum, ident)
            combine(nc, h, weight, slot_out, y_dram, out)


def load_constants(nc, stage, pairs):
    with Memory(nc, stage) as m:
        loaded = m.sem("loaded")
        with nc.Block() as block:
            @block.sync
            def _(sp):
                for buffer, source in pairs:
                    sp.dma_start(buffer[:], source).then_inc(loaded, 16)
                sp.wait_ge(loaded, 16 * len(pairs))


def kernel(**inputs):
    import concourse.bacc as bacc
    from concourse.bass_utils import run_bass_kernel_spmd

    given = {name: np.asarray(a) for name, a in inputs.items()}
    f32 = np.float32

    def head_rows(w):
        return np.repeat(w.reshape(G, 4, 1, F, D), 2, axis=2).reshape(G, 128, D).transpose(1, 0, 2)

    taps = given["L0_tok_weight"].transpose(1, 2, 0)
    partition = np.arange(128)
    arrays = {
        "x": given["x"], "conv_w_even": taps[:, 0::2], "conv_w_odd": taps[:, 1::2],
        "conv_b": given["L0_tok_bias"].reshape(D, 1),
        "w_qkv_T": given["L0_attn_qkv_w"].T, "w_delta_T": given["L0_attn_delta_w"].T,
        "g12_cols": np.stack([np.tile(given["L0_attn_g1"], H), np.tile(given["L0_attn_g2"], H)], 1),
        "g3_row": np.tile(given["L0_attn_g3"], H),
        "w_qkv_rows": head_rows(given["L0_attn_qkv_w"]), "w_delta_rows": head_rows(given["L0_attn_delta_w"]),
        "moe0_wg": given["L0_ffn_Wg"], "moe0_bg": given["L0_ffn_bg"].reshape(1, -1),
        "moe0_we": given["L0_ffn_We"], "moe0_be": given["L0_ffn_be"],
        "wq": given["L1_attn_Wq"], "wk": given["L1_attn_Wk"], "wv": given["L1_attn_Wv"],
        "wb": given["L1_attn_Wb"], "wo": given["L1_attn_Wo"],
        "ln_cols": np.stack([given["L1_attn_ln_g"], given["L1_attn_ln_b"]], 1),
        "w_hash_T": given["L1_ffn_W_hash"][:ACTIVE].T,
        "moe1_w1": given["L1_ffn_W1"], "moe1_w2": given["L1_ffn_W2"],
        "moe1_b1": given["L1_ffn_b1"].reshape(NEXP, D, FCH).transpose(1, 0, 2), "moe1_b2": given["L1_ffn_b2"],
        "ident": np.eye(128, dtype=f32), "ones": np.ones((128, 128), f32),
        "block_ones": np.kron(np.eye(H), np.full((F, F), 1.0 / F)).astype(f32),
        "block_sum": np.kron(np.eye(H), np.ones((F, F))).astype(f32),
        "head_start": (partition[:, None] == F * np.arange(H)).astype(f32),
        "countdown": (16 - np.arange(16)).astype(f32).reshape(1, 16),
        "pair_masks": np.stack([partition // F % 2 == 0, partition // F % 2 == 1], 1).astype(f32),
        "buckets": np.arange(NEXP).astype(f32),
        "earlier": np.triu(np.ones((128, 128), f32), 1),
    }
    arrays = {name: np.ascontiguousarray(a) for name, a in arrays.items()}
    nc = bacc.Bacc("TRN2", target_bir_lowering=False, num_devices=1)
    io = {name: nc.dram_tensor(name, a.shape, mybir.dt.from_np(a.dtype), kind="ExternalInput").ap()
          for name, a in arrays.items()}
    out = nc.dram_tensor("out", (B, L, D), FP32, kind="ExternalOutput").ap()
    tower(nc, io, out)
    return run_bass_kernel_spmd(nc, [arrays], core_ids=[0]).results[0]["out"]
```

```python
import numpy as np
import concourse.bass as bass
from concourse import mybir
from contextlib import ExitStack

FP32 = mybir.dt.float32
BF16 = mybir.dt.bfloat16
I32 = mybir.dt.int32
ALU = mybir.AluOpType
ACT = mybir.ActivationFunctionType
AX = mybir.AxisListType

B, CIN, L = 8, 64, 750
D, H, F = 128, 8, 16
TT, NT = 125, 6
NTILES = B * NT
HALF = L // 2
TAPS, PAIRS = 9, 5
PAD = 4
XW = L + 2 * PAD
G = 2
NEXP, DFF = 64, 512
ACTIVE = 2
CAP = 235
HP = (CAP + 1) // 2
SLOTS = 2 * HP
FCH = DFF // D
BUCKET_SCALE = 8.0
EXPERTS_AHEAD = 4
ROW = D + 1
ZERO_PARTS = 6
LN_EPS = 1e-5
RMS_EPS = 1.1920929e-07
PIECES = 3
PIECES_A = [0, 0, 1, 1, 0, 2]
PIECES_B = [0, 1, 0, 1, 2, 0]
KROWS = len(PIECES_A) * F


class Memory:

    def __init__(self, nc, stage):
        self.nc, self.stage, self.stack, self.sems = nc, stage, ExitStack(), []

    def __enter__(self):
        return self

    def __exit__(self, *error):
        self.stack.close()
        if self.sems:
            self.nc.clear_and_free_semaphores(self.sems)
            self.nc.all_engine_barrier()

    def sbuf(self, name, shape, dt=FP32):
        return self.stack.enter_context(self.nc.sbuf_tensor(f"{self.stage}_{name}", shape, dt))

    def sem(self, name):
        self.sems.append(self.nc.alloc_semaphore(name=f"{self.stage}_{name}"))
        return self.sems[-1]


def convolution(nc, io, h, stats, constants, psum, ident):
    with Memory(nc, "conv") as m:
        xpad = m.sbuf("xpad", [128, B, XW])
        wconv = m.sbuf("w", [128, PAIRS, D])
        cbias = m.sbuf("bias", [128, 1])
        hT = m.sbuf("hT", [128, 2, L])
        loaded, rest_loaded = m.sem("loaded"), m.sem("rest_loaded")
        constants_loaded = m.sem("constants_loaded")
        padded = m.sem("padded")
        conv_ready, conv_free = m.sem("conv_ready"), m.sem("conv_free")
        hT_ready, hT_free = m.sem("hT_ready"), m.sem("hT_free")
        turned_ready, turned_free = m.sem("turned_ready"), m.sem("turned_free")
        h_written = m.sem("h_written")
        with nc.Block() as block:
            @block.sync
            def _(sp):
                sp.dma_start(wconv[0:64, :, :], io["conv_w_even"]).then_inc(loaded, 16)
                sp.dma_start(wconv[64:128, 0:PAIRS - 1, :], io["conv_w_odd"]).then_inc(loaded, 16)
                sp.dma_start(cbias[:], io["conv_b"]).then_inc(loaded, 16)
                x_cbl = io["x"].rearrange("b c l -> c b l")
                for lo, hi, sem in ((0, 2, loaded), (2, B, rest_loaded)):
                    sp.dma_start(xpad[0:64, lo:hi, PAD:PAD + L], x_cbl[:, lo:hi, :]).then_inc(sem, 16)
                    sp.dma_start(xpad[64:128, lo:hi, PAD - 1:PAD - 1 + L], x_cbl[:, lo:hi, :]).then_inc(sem, 16)
                for buffer, source in constants:
                    sp.dma_start(buffer[:], source).then_inc(constants_loaded, 16)

            @block.gpsimd
            def _(pool):
                nc.gpsimd.memset(xpad[0:64, :, 0:PAD], 0.0).then_inc(padded, 1)
                nc.gpsimd.memset(xpad[0:64, :, PAD + L:XW], 0.0).then_inc(padded, 1)
                nc.gpsimd.memset(xpad[64:128, :, 0:PAD - 1], 0.0).then_inc(padded, 1)
                nc.gpsimd.memset(xpad[64:128, :, PAD - 1 + L:XW], 0.0).then_inc(padded, 1)

            @block.tensor
            def _(pe):
                pe.wait_ge(loaded, 80)
                pe.wait_ge(padded, 4)

                def pair(i, first):
                    for u in range(2):
                        pe.wait_ge(conv_free, 2 * i + (u + 1))
                        for half in range(2):
                            for j in range(PAIRS):
                                rows = 128 if j < PAIRS - 1 else 64
                                mm = nc.tensor.matmul(
                                    psum[2 * u + half][:, 0:HALF], wconv[0:rows, j, :],
                                    xpad[0:rows, bass.ds(2 * i + u, 1), half * HALF + 2 * j:half * HALF + 2 * j + HALF],
                                    start=(j == 0), stop=(j == PAIRS - 1))
                        mm.then_inc(conv_ready, 1)
                    if first:
                        pe.wait_ge(constants_loaded, 16 * len(constants))
                        pe.wait_ge(rest_loaded, 32)
                    for u in range(2):
                        pe.wait_ge(hT_ready, 2 * (2 * i + u) + 2)
                        pe.wait_ge(turned_free, 2 * i + (u + 1))
                        for t in range(NT):
                            mm = nc.tensor.transpose(psum[4 + 2 * u + t // 3][0:TT, (t % 3) * D:(t % 3 + 1) * D],
                                                     hT[:, u, t * TT:(t + 1) * TT], ident[:])
                        mm.then_inc(turned_ready, 1)
                pair(0, True)
                with pe.Fori(1, B // 2) as i:
                    pair(i, False)

            @block.scalar
            def _(act):
                act.sem_inc(conv_free, 2)
                with act.Fori(0, B // 2) as i:
                    for u in range(2):
                        act.wait_ge(conv_ready, 2 * i + (u + 1))
                        act.wait_ge(hT_free, 2 * i + (u + 1))
                        for half in range(2):
                            ins = nc.scalar.activation(hT[:, u, half * HALF:(half + 1) * HALF],
                                                       psum[2 * u + half][:, 0:HALF], ACT.Identity, bias=cbias[:])
                            ins.then_inc(hT_ready, 1)
                        act.wait_ge(hT_ready, 2 * (2 * i + u) + 2)
                        act.sem_inc(conv_free, 1)

            @block.vector
            def _(dve):
                dve.sem_inc(turned_free, 2)
                dve.sem_inc(hT_free, 2)
                with dve.Fori(0, B // 2) as i:
                    for u in range(2):
                        dve.wait_ge(turned_ready, 2 * i + (u + 1))
                        dve.sem_inc(hT_free, 1)
                        for k in range(2):
                            nc.vector.tensor_copy(
                                h[0:TT, bass.ds((2 * i + u) * NT + 3 * k, 3), :],
                                psum[4 + 2 * u + k][0:TT, 0:3 * D].rearrange("p (t d) -> p t d", d=D)).then_inc(h_written, 1)
                        for t in range(NT):
                            nc.vector.bn_stats(stats[0:TT, bass.ds((2 * i + u) * NT + t, 1), :],
                                               psum[4 + 2 * u + t // 3][0:TT, (t % 3) * D:(t % 3 + 1) * D]
                                               ).then_inc(h_written, 1)
                        dve.wait_ge(h_written, (2 + NT) * (2 * i + u + 1))
                        dve.sem_inc(turned_free, 1)


def pass_gate(eng, sem, value, gate):
    eng.wait_ge(sem, value)
    eng.sem_inc(gate, 1)


class Chain:

    def __init__(self, eng, sem, base=0, anchor=None):
        self.eng, self.sem, self.base, self.n, self.anchor = eng, sem, base, 0, anchor

    def add(self, ins):
        ins.then_inc(self.sem, 1)
        self.n += 1

    def settle(self):
        self.eng.wait_ge(self.sem, self.base + self.n)
        if self.anchor is not None:
            self.eng.sem_inc(self.anchor, 1)

    def link(self, ins):
        self.add(ins)
        self.settle()


def spread(scalars, n):
    rows, tiles = scalars.shape
    return scalars.unsqueeze(2).broadcast_to([rows, tiles, n])


def moments(nc, dve, chain, stats, mean, var, tmp):
    even_mean, even_m2 = stats[0:TT, :, 1], stats[0:TT, :, 2]
    odd_mean, odd_m2 = stats[0:TT, :, 4], stats[0:TT, :, 5]
    chain.add(nc.vector.tensor_tensor(mean, even_mean, odd_mean, ALU.add))
    chain.add(nc.vector.tensor_tensor(tmp, even_mean, odd_mean, ALU.subtract))
    chain.link(nc.vector.tensor_tensor(var, even_m2, odd_m2, ALU.add))
    chain.add(nc.vector.tensor_scalar(mean, mean, 0.5, None, ALU.mult))
    chain.add(nc.vector.tensor_tensor(tmp, tmp, tmp, ALU.mult))
    chain.link(nc.vector.tensor_scalar(var, var, 1.0 / D, LN_EPS, ALU.mult, ALU.add))
    chain.link(nc.vector.scalar_tensor_tensor(out=var, in0=tmp, scalar=0.25, in1=var, op0=ALU.mult, op1=ALU.add))


def refine_rsqrt(nc, chain, rstd, var, tmp):
    chain.link(nc.vector.tensor_tensor(tmp, rstd, rstd, ALU.mult))
    chain.link(nc.vector.tensor_tensor(tmp, tmp, var, ALU.mult))
    chain.link(nc.vector.tensor_scalar(tmp, tmp, -0.5, 1.5, ALU.mult, ALU.add))
    chain.link(nc.vector.tensor_tensor(rstd, rstd, tmp, ALU.mult))


def layernorm_scalars(nc, stage, stats, mean, rstd):
    with Memory(nc, stage) as m:
        var = m.sbuf("var", [128, NTILES])
        tmp = m.sbuf("tmp", [128, NTILES])
        var_ready, root_ready, done = m.sem("var_ready"), m.sem("root_ready"), m.sem("done")
        with nc.Block() as block:
            @block.vector
            def _(dve):
                chain = Chain(dve, done)
                moments(nc, dve, chain, stats, mean[0:TT, :], var[0:TT, :], tmp[0:TT, :])
                dve.sem_inc(var_ready, 1)
                dve.wait_ge(root_ready, 1)
                chain.link(nc.vector.reciprocal(rstd[0:TT, :], tmp[0:TT, :]))
                refine_rsqrt(nc, chain, rstd[0:TT, :], var[0:TT, :], tmp[0:TT, :])

            @block.scalar
            def _(act):
                act.wait_ge(var_ready, 1)
                nc.scalar.activation(tmp[0:TT, :], var[0:TT, :], ACT.Sqrt).then_inc(root_ready, 1)


def head_vectors(nc, io, h, mean, rstd, n3, dmax, pieces_dram, psum, ident, block_ones):
    with Memory(nc, "heads") as m:
        wT = m.sbuf("wT", [128, D])
        wTd = m.sbuf("wTd", [128, D])
        gcols = m.sbuf("gcols", [128, 2])
        pcol = m.sbuf("pcol", [128, 1])
        pabs = m.sbuf("pabs", [128, 1])
        eps = m.sbuf("eps", [128, 1])
        bound_w = m.sbuf("bound_w", [128, D])
        g3row = m.sbuf("g3row", [128, D])
        xn = m.sbuf("xn", [128, 2, NT, D])
        xnT = m.sbuf("xnT", [128, 2, L])
        sq = m.sbuf("sq", [128, 2, L])
        squares = m.sbuf("squares", [128, 2, NT, D])
        rms = m.sbuf("rms", [128, 2, NT * H])
        n_rows = m.sbuf("n_rows", [128, 2, NT, D])
        nT = m.sbuf("nT", [128, 2, L])
        pnT = m.sbuf("pnT", [128, 2, L])
        rest = m.sbuf("rest", [128, 2, 2, L])
        pieces = m.sbuf("pieces", [128, 2, 2 * PIECES, L], BF16)
        loaded = m.sem("loaded")
        setup = m.sem("setup")
        xn_ready, xnT_psum, xnT_ready, w_psum, sq_ready, ms_ready, rms_ready = (
            m.sem(s) for s in ("xn_ready", "xnT_psum", "xnT_ready", "w_psum", "sq_ready", "ms_ready", "rms_ready"))
        n_ready, nT_psum, nT_ready, nT_taken, a_done, bound_psum, dmax_ready = (
            m.sem(s) for s in ("n_ready", "nT_psum", "nT_ready", "nT_taken", "a_done", "bound_psum", "dmax_ready"))
        a_split, b_split, stored, dve_chain, pool_chain = (
            m.sem(s) for s in ("a_split", "b_split", "stored", "dve_chain", "pool_chain"))
        gate, pn_ready, xn_chain = m.sem("gate"), m.sem("pn_ready"), m.sem("xn_chain")
        pieces_free, nT_free = m.sem("pieces_free"), m.sem("nT_free")
        dmax2 = m.sbuf("dmax2", [128, 2 * B])

        def two_banks(bank):
            return [psum[bank][:, 0:HALF], psum[bank + 1][:, 0:HALF]]

        def split(eng, chain, source, rest, out, first, high_done):
            high, middle, low = (out[:, first + k, :] for k in range(PIECES))
            if not high_done:
                chain.link(eng.tensor_copy(high, source))
            chain.link(eng.tensor_tensor(rest, source, high, ALU.subtract))
            chain.link(eng.tensor_copy(middle, rest))
            return eng.tensor_tensor(low, rest, middle, ALU.subtract)

        def pairs(eng, ahead, body):
            ahead(0)
            with eng.Fori(0, B // 2 - 1) as i:
                body(i, lambda: ahead(i + 1))
            body(B // 2 - 1, lambda: None)

        with nc.Block() as block:
            @block.sync
            def _(sp):
                sp.dma_start(wT[:], io["w_qkv_T"]).then_inc(loaded, 16)
                sp.dma_start(wTd[:], io["w_delta_T"]).then_inc(loaded, 16)
                sp.dma_start(gcols[:], io["g12_cols"]).then_inc(loaded, 16)
                sp.dma_start(g3row[:], io["g3_row"].partition_broadcast(128)).then_inc(loaded, 16)
                sp.sem_inc(pieces_free, 2)
                with sp.Fori(0, B // 2) as i:
                    for u in range(2):
                        sp.wait_ge(a_split, 2 * i + (u + 1))
                        sp.wait_ge(b_split, 2 * i + (u + 1))
                        sp.dma_start(pieces_dram[bass.ds(2 * i + u, 1), :, :, :].rearrange("o k p t -> p (o k) t"),
                                     pieces[:, u, :, :]).then_inc(stored, 16)
                        sp.wait_ge(stored, 16 * (2 * i + u) + 16)
                        sp.sem_inc(pieces_free, 1)

            @block.tensor
            def _(pe):
                pe.wait_ge(setup, 1)

                def ahead(i):
                    for u in range(2):
                        pe.wait_ge(xn_ready, 2 * i + (u + 1))
                        pe.wait_ge(nT_taken, 2 * i + (u + 1))
                        for t in range(NT):
                            mm = nc.tensor.transpose(psum[4 * u + t // 3][:, (t % 3) * TT:(t % 3 + 1) * TT],
                                                     xn[0:TT, u, t, :], ident[0:TT, 0:TT])
                        mm.then_inc(xnT_psum, 1)

                def body(i, next_pair):
                    for u in range(2):
                        pe.wait_ge(xnT_ready, 2 * (2 * i + u) + 2)
                        pe.wait_ge(dmax_ready, 2 * i + (u + 1))
                        for t in range(NT):
                            mm = nc.tensor.matmul(psum[4 * u + 2 + t // 3][0:TT, (t % 3) * D:(t % 3 + 1) * D],
                                                  xnT[:, u, t * TT:(t + 1) * TT], wT[:], start=True, stop=True)
                        mm.then_inc(w_psum, 1)
                    for u in range(2):
                        pe.wait_ge(n_ready, 2 * i + (u + 1))
                        for t in range(NT):
                            mm = nc.tensor.transpose(psum[4 * u + t // 3][:, (t % 3) * TT:(t % 3 + 1) * TT],
                                                     n_rows[0:TT, u, t, :], ident[0:TT, 0:TT])
                        mm.then_inc(nT_psum, 1)
                    for u in range(2):
                        pe.wait_ge(nT_ready, 4 * (2 * i + u) + 4)
                        for half in range(2):
                            mm = nc.tensor.matmul(psum[4 * u + 2 + half][:, 0:HALF], bound_w[:],
                                                  sq[:, u, half * HALF:(half + 1) * HALF], start=True, stop=True)
                        mm.then_inc(bound_psum, 1)
                    next_pair()
                pairs(pe, ahead, body)

            @block.scalar
            def _(act):
                act.wait_ge(setup, 1)
                act.sem_inc(nT_taken, 2)

                def ahead(i):
                    for u in range(2):
                        act.wait_ge(xnT_psum, 2 * i + (u + 1))
                        for half in range(2):
                            nc.scalar.activation(xnT[:, u, half * HALF:(half + 1) * HALF],
                                                 psum[4 * u + half][:, 0:HALF], ACT.Identity).then_inc(xnT_ready, 1)

                def body(i, next_pair):
                    for u in range(2):
                        act.wait_ge(w_psum, 2 * i + (u + 1))
                        for k in range(2):
                            nc.scalar.activation(squares[0:TT, u, 3 * k:3 * k + 3, :].rearrange("p t d -> p (t d)"),
                                                 psum[4 * u + 2 + k][0:TT, 0:3 * D], ACT.Square).then_inc(sq_ready, 1)
                    for u in range(2):
                        act.wait_ge(ms_ready, 2 * i + (u + 1))
                        nc.scalar.activation(rms[0:TT, u, :], rms[0:TT, u, :], ACT.Sqrt, bias=eps[0:TT, :],
                                             scale=1.0 / F).then_inc(rms_ready, 1)
                    for u in range(2):
                        act.wait_ge(nT_psum, 2 * i + (u + 1))
                        act.wait_ge(nT_free, 2 * i + (u + 1))
                        act.wait_ge(a_done, 2 * i + (u + 1))
                        for half in range(2):
                            nc.scalar.activation(nT[:, u, half * HALF:(half + 1) * HALF],
                                                 psum[4 * u + half][:, 0:HALF], ACT.Identity).then_inc(nT_ready, 1)
                        for half in range(2):
                            nc.scalar.activation(sq[:, u, half * HALF:(half + 1) * HALF],
                                                 psum[4 * u + half][:, 0:HALF], ACT.Square).then_inc(nT_ready, 1)
                        act.wait_ge(pieces_free, 2 * i + (u + 1))
                        for half in range(2):
                            cols = slice(half * HALF, (half + 1) * HALF)
                            nc.scalar.activation(pnT[:, u, cols], psum[4 * u + half][:, 0:HALF], ACT.Identity,
                                                 scale=pcol[:]).then_inc(pn_ready, 1)
                            nc.scalar.activation(pieces[:, u, PIECES, cols], psum[4 * u + half][:, 0:HALF],
                                                 ACT.Identity, scale=pcol[:]).then_inc(pn_ready, 1)
                        act.wait_ge(nT_ready, 4 * (2 * i + u) + 4)
                        act.wait_ge(pn_ready, 4 * (2 * i + u) + 4)
                        act.sem_inc(nT_taken, 1)
                    next_pair()
                pairs(act, ahead, body)

            @block.gpsimd
            def _(pool):
                pool.wait_ge(setup, 1)
                pool.sem_inc(nT_free, 2)
                with pool.Fori(0, B // 2) as i:
                    chain = Chain(pool, pool_chain, 4 * i, gate)
                    for u in range(2):
                        pass_gate(pool, pn_ready, 4 * (2 * i + u) + 4, gate)
                        split(nc.gpsimd, chain, pnT[:, u, :], rest[:, 1, u, :], pieces[:, u], PIECES, True).then_inc(b_split, 1)
                        pool.wait_ge(b_split, 2 * i + (u + 1))
                        pool.sem_inc(nT_free, 1)

            @block.vector
            def _(dve):
                setup_chain = Chain(dve, dve_chain)
                dve.wait_ge(loaded, 64)
                dve.sem_inc(dmax_ready, 2)
                dve.sem_inc(a_done, 2)
                setup_chain.link(nc.vector.memset(eps[:], RMS_EPS))
                setup_chain.link(nc.vector.tensor_tensor(wT[:], wT[:], wTd[:], ALU.add))
                setup_chain.link(nc.vector.tensor_tensor(pcol[:], gcols[:, 0:1], gcols[:, 1:2], ALU.mult))
                setup_chain.link(nc.vector.tensor_scalar(pcol[:], pcol[:], F ** -0.5, None, ALU.mult))
                setup_chain.link(nc.vector.tensor_scalar(pabs[:], pcol[:], -1.0, None, ALU.mult))
                setup_chain.link(nc.vector.tensor_tensor(pabs[:], pabs[:], pcol[:], ALU.max))
                setup_chain.link(nc.vector.tensor_scalar(bound_w[:], block_ones[:], pabs[:], float(F), ALU.mult, ALU.mult))
                dve.sem_inc(setup, 1)

                def ahead(i):
                    chain = Chain(dve, xn_chain, 2 * NT * i)
                    for u in range(2):
                        for t in range(NT):
                            col = (2 * i + u) * NT + t
                            chain.add(nc.vector.tensor_scalar(
                                xn[0:TT, u, t, :], h[0:TT, bass.ds(col, 1), :], mean[0:TT, bass.ds(col, 1)],
                                rstd[0:TT, bass.ds(col, 1)], ALU.subtract, ALU.mult))
                        chain.settle()
                        dve.sem_inc(xn_ready, 1)

                def body(i, next_pair):
                    chain = Chain(dve, dve_chain, setup_chain.n + i * 16)
                    for u in range(2):
                        dve.wait_ge(sq_ready, 2 * (2 * i + u) + 2)
                        chain.link(nc.vector.tensor_reduce(rms[0:TT, u, :], squares[0:TT, u, :, :].rearrange(
                            "p t (g f) -> p (t g) f", f=F), AX.X, ALU.add))
                        dve.sem_inc(ms_ready, 1)
                    for u in range(2):
                        dve.wait_ge(rms_ready, 2 * i + (u + 1))
                        chain.link(nc.vector.reciprocal(rms[0:TT, u, :], rms[0:TT, u, :]))
                        for k in range(2):
                            chain.add(nc.vector.tensor_tensor(
                                n_rows[0:TT, u, 3 * k:3 * k + 3, :].rearrange("p t (g f) -> p (t g) f", f=F),
                                psum[4 * u + 2 + k][0:TT, 0:3 * D].rearrange("p (g f) -> p g f", f=F),
                                spread(rms[0:TT, u, 3 * H * k:3 * H * (k + 1)], F), ALU.mult))
                        chain.settle()
                        dve.sem_inc(n_ready, 1)
                        chain.add(nc.vector.tensor_tensor(
                            n3[0:TT, bass.ds((2 * i + u) * NT, NT), :], n_rows[0:TT, u, :, :],
                            g3row[0:TT, :].unsqueeze(1).broadcast_to([TT, NT, D]), ALU.mult))
                    next_pair()
                    for u in range(2):
                        dve.wait_ge(nT_ready, 4 * (2 * i + u) + 2)
                        dve.wait_ge(pieces_free, 2 * i + (u + 1))
                        split(nc.vector, chain, nT[:, u, :], rest[:, 0, u, :], pieces[:, u], 0, False).then_inc(a_split, 1)
                        dve.wait_ge(bound_psum, 2 * i + (u + 1))
                        for half in range(2):
                            ins = nc.vector.tensor_reduce(dmax2[:, bass.ds(2 * (2 * i + u) + half, 1)],
                                                          psum[4 * u + 2 + half][:, 0:HALF], AX.X, ALU.max)
                        ins.then_inc(dmax_ready, 1)
                        dve.wait_ge(a_split, 2 * i + (u + 1))
                        dve.sem_inc(a_done, 1)
                    assert chain.n == 2 + 8 + 6
                pairs(dve, ahead, body)
                dve.wait_ge(dmax_ready, B + 2)
                nc.vector.tensor_reduce(dmax[:], dmax2[:].rearrange("p (b k) -> p b k", k=2), AX.X, ALU.max).then_inc(setup, 1)


def attention(nc, io, h, stats, n3, dmax, pieces_dram, psum_banks, psum, ident, ones):
    EBUFS = 3
    with Memory(nc, "att") as m:
        piece_a = m.sbuf("piece_a", [KROWS, G, 4, L], BF16)
        piece_b = m.sbuf("piece_b", [KROWS, G, 4, L], BF16)
        w2 = m.sbuf("w2", [128, G, D])
        w2d = m.sbuf("w2d", [128, G, D])
        head_start = m.sbuf("head_start", [128, H])
        dsel = m.sbuf("dsel", [128, B, H])
        guard = m.sbuf("guard", [128, B * H])
        e = m.sbuf("e", [128, EBUFS, 4, L])
        z = m.sbuf("z", [128, EBUFS, 4])
        rz = m.sbuf("rz", [128, EBUFS, 4])
        values = m.sbuf("values", [128, EBUFS, 4, 2, F])
        scales = m.sbuf("scales", [128, G, NT, 4, 2, F])
        first_exp = m.sbuf("first_exp", [1, 1])
        scaleT = m.sbuf("scaleT", [128, L])
        ys = m.sbuf("ys", [128, G, L])
        loaded, setup = m.sem("loaded"), m.sem("setup")
        guard_psum = m.sem("guard_psum")
        ab_ready = [m.sem(f"ab_ready{g}") for g in range(G)]
        ab_free = [m.sem(f"ab_free{g}") for g in range(G)]
        att_ready, att_free, e_free = (m.sem(s) for s in ("att_ready", "att_free", "e_free"))
        values_ready, scales_ready, scaleT_psum = (
            m.sem(s) for s in ("values_ready", "scales_ready", "scaleT_psum"))
        y_psum, y_free, ys_ready, out_psum, out_free = (
            m.sem(s) for s in ("y_psum", "y_free", "ys_ready", "out_psum", "out_free"))
        dve_chain, dve_done = m.sem("dve_chain"), m.sem("dve_done")
        gate = m.sem("gate")
        SETS = G * NT
        assert SETS % EBUFS == 0
        LAG = 6
        CUTS = [(0, 0, 188), (0, 188, HALF), (1, 0, 188), (1, 188, HALF)]

        def batches(eng, body):
            body(0, True)
            with eng.Fori(1, B) as b:
                body(b, False)

        with nc.Block() as block:
            @block.sync
            def _(sp):
                sp.dma_start(w2[:], io["w_qkv_rows"]).then_inc(loaded, 16)
                sp.dma_start(w2d[:], io["w_delta_rows"]).then_inc(loaded, 16)
                sp.dma_start(head_start[:], io["head_start"]).then_inc(loaded, 16)
                with sp.Fori(0, B) as b:
                    for g in range(G):
                        sp.wait_ge(ab_free[g], b + 1)
                        for dst, which in ((piece_a, [0, 0, 1, 1, 0, 2]), (piece_b, [3, 4, 3, 4, 5, 3])):
                            for k, piece in enumerate(which):
                                src = pieces_dram[bass.ds(b, 1), piece, g * 64:(g + 1) * 64, :]
                                sp.dma_start(dst[k * F:(k + 1) * F, g, :, :],
                                             src.rearrange("o (q f) t -> f (o q) t", f=F)).then_inc(ab_ready[g], 16)

            @block.tensor
            def _(pe):
                pe.wait_ge(setup, 1)
                nc.tensor.matmul(psum[6][:, 0:B * H], ones[:], dsel[:].rearrange("p b h -> p (b h)"),
                                 start=True, stop=True).then_inc(guard_psum, 1)
                pe.sem_inc(ab_free[0], 1)
                pe.sem_inc(ab_free[1], 1)
                pe.wait_ge(setup, 2)

                def scores(b, s, q):
                    g, j = divmod(s, NT)
                    if j == 0 and q == 0:
                        pe.wait_ge(ab_ready[g], 192 * b + 192)
                    pe.wait_ge(att_free, 4 * SETS * b + (4 * s + q + 1))
                    for half in range(2):
                        mm = nc.tensor.matmul(psum[2 * (q % 2) + half][0:TT, 0:HALF],
                                              piece_a[:, g, q, j * TT:(j + 1) * TT],
                                              piece_b[:, g, q, half * HALF:(half + 1) * HALF], start=True, stop=True)
                    mm.then_inc(att_ready, 1)
                    if j == NT - 1 and q == 3:
                        pe.wait_ge(att_ready, 4 * SETS * b + (4 * s + q + 1))
                        pe.sem_inc(ab_free[g], 1)

                def weigh(b, s, k):
                    j = s % NT
                    half, lo, hi = CUTS[k]
                    if j == 0:
                        if k % 2 == 1:
                            lo = hi
                        else:
                            hi = HALF
                    if k == 0:
                        pe.wait_ge(values_ready, SETS * b + (s + 1))
                    if k % 2 == 0 and j == 0:
                        pe.wait_ge(y_free, 2 * G * b + (2 * (s // NT) + half + 1))
                    for q in range(4 if hi > lo else 0):
                        mm = nc.tensor.matmul(psum[4 + half][32 * q:32 * q + 32, lo:hi],
                                              values[0:TT, s % EBUFS, q, :, :].rearrange("p a f -> p (a f)"),
                                              e[0:TT, s % EBUFS, q, half * HALF + lo:half * HALF + hi],
                                              start=(j == 0), stop=(j == NT - 1), skip_group_check=True)
                    if k % 2 == (1 if j > 0 else 0):
                        mm.then_inc(e_free, 1)
                    if k % 2 == 1 and j == NT - 1:
                        pe.wait_ge(e_free, 2 * (SETS * b + s + EBUFS) + half + 1)
                        pe.sem_inc(y_psum, 1)

                def turn_scales(b, g, t):
                    pe.wait_ge(scales_ready, SETS * b + (g * NT + t + 1))
                    if t == 0:
                        pe.wait_ge(out_free, (G + 1) * b + (g + 1))
                    mm = nc.tensor.transpose(psum[6 + t // 3][:, (t % 3) * TT:(t % 3 + 1) * TT],
                                             scales[0:TT, g, t, :, :, :].rearrange("p q a f -> p (q a f)"),
                                             ident[0:TT, 0:TT])
                    if t == NT - 1:
                        mm.then_inc(scaleT_psum, 1)

                def project(b, n):
                    t, g = divmod(n, G)
                    if n == 0:
                        pe.wait_ge(ys_ready, 2 * G * b + 2 * G)
                        pe.wait_ge(out_free, (G + 1) * b + (G + 1))
                    mm = nc.tensor.matmul(psum[6 + t // 3][0:TT, (t % 3) * D:(t % 3 + 1) * D],
                                          ys[:, g, t * TT:(t + 1) * TT], w2[:, g, :],
                                          start=(g == 0), stop=(g == G - 1))
                    if n == G * NT - 1:
                        mm.then_inc(out_psum, 1)

                def body(b, first):
                    for s in range(SETS):
                        for q in range(4):
                            scores(b, s, q)
                            at = 4 * s + q + 1
                            if 4 * NT <= at < 4 * NT + NT:
                                turn_scales(b, 0, at - 4 * NT)
                            if at == 4 * SETS:
                                turn_scales(b, 1, 0)
                            if at < NT and not first:
                                turn_scales(b - 1, 1, at)
                            n = 4 * s + q - LAG
                            if n >= 0:
                                weigh(b, n // 4, n % 4)
                            elif not first:
                                weigh(b - 1, SETS + n // 4, n % 4)
                            at = 4 * s + q - LAG - 4
                            if 0 <= at < G * NT and not first:
                                project(b - 1, at)
                batches(pe, body)
                for n in range(4 * SETS - LAG, 4 * SETS):
                    weigh(B - 1, n // 4, n % 4)
                for t in range(1, NT):
                    turn_scales(B - 1, 1, t)
                for n in range(G * NT):
                    project(B - 1, n)

            @block.scalar
            def _(act):
                act.wait_ge(setup, 2)
                act.sem_inc(att_free, 2)
                act.sem_inc(e_free, 2 * EBUFS)
                act.wait_ge(loaded, 48)
                nc.scalar.activation(first_exp[:], guard[0:1, 0:1], ACT.Exp)
                with act.Fori(0, B) as b:
                    for s in range(SETS):
                        g = s // NT
                        act.wait_ge(e_free, 2 * (SETS * b + s) + 2)
                        for q in range(4):
                            pass_gate(act, att_ready, 4 * SETS * b + (4 * s + q + 1), gate)
                            nc.scalar.activation(
                                e[0:TT, s % EBUFS, q, :].rearrange("p (a t) -> p a t", a=2),
                                psum_banks[0:TT, 2 * (q % 2):2 * (q % 2) + 2, 0:HALF], ACT.Exp,
                                bias=guard[0:TT, bass.ds(H * b + 4 * g + q, 1)],
                                accum_out=z[0:TT, s % EBUFS, q:q + 1]).then_inc(att_free, 1)

            @block.vector
            def _(dve):
                chain = Chain(dve, dve_chain)
                dve.wait_ge(loaded, 48)
                chain.link(nc.vector.memset(scales[:], 1.0))
                chain.link(nc.vector.tensor_tensor(w2[:], w2[:], w2d[:], ALU.add))
                chain.link(nc.vector.tensor_tensor(dsel[:], dmax[:].unsqueeze(2).broadcast_to([128, B, H]),
                                                   head_start[:].unsqueeze(1).broadcast_to([128, B, H]), ALU.mult))
                dve.sem_inc(setup, 1)
                dve.wait_ge(guard_psum, 1)
                chain.link(nc.vector.tensor_scalar(guard[:], psum[6][:, 0:B * H], -1.0, None, ALU.mult))
                dve.sem_inc(y_free, 2)
                dve.sem_inc(out_free, 1)
                dve.sem_inc(setup, 1)

                def turned_scales(b, g, chain):
                    dve.wait_ge(scaleT_psum, G * b + (g + 1))
                    for half in range(2):
                        chain.add(nc.vector.tensor_copy(scaleT[:, half * HALF:(half + 1) * HALF],
                                                        psum[6 + half][:, 0:HALF]))
                    chain.settle()
                    dve.sem_inc(out_free, 1)

                def scaled(b, g, half, chain):
                    dve.wait_ge(y_psum, 2 * (G * b + g) + half + 1)
                    cols = slice(half * HALF, (half + 1) * HALF)
                    chain.link(nc.vector.tensor_tensor(ys[:, g, cols], psum[4 + half][:, 0:HALF],
                                                       scaleT[:, cols], ALU.mult))
                    dve.sem_inc(y_free, 1)
                    dve.sem_inc(ys_ready, 1)

                def residual(b, chain):
                    dve.wait_ge(out_psum, b + 1)
                    for k in range(2):
                        rows = h[0:TT, bass.ds(b * NT + 3 * k, 3), :]
                        chain.add(nc.vector.tensor_tensor(rows, rows, psum[6 + k][0:TT, 0:3 * D].rearrange(
                            "p (t d) -> p t d", d=D), ALU.add))
                    chain.settle()
                    dve.sem_inc(out_free, 1)

                def statistics(b, chain):
                    for t in range(NT):
                        chain.add(nc.vector.bn_stats(stats[0:TT, bass.ds(b * NT + t, 1), :],
                                                     h[0:TT, bass.ds(b * NT + t, 1), :]))
                    chain.settle()

                def weights(b, s, chain):
                    g, j = divmod(s, NT)
                    dve.wait_ge(att_free, 4 * SETS * b + (4 * s + 4 + 2))
                    v = n3[0:TT, bass.ds(b * NT + j, 1), g * 64:(g + 1) * 64].rearrange("p o (q f) -> p (o q) f", f=F)
                    dve.wait_ge(e_free, 2 * (SETS * b + s) + 2)
                    slot = s % EBUFS
                    chain.add(nc.vector.tensor_copy(values[0:TT, slot, :, 0, :], v))
                    chain.link(nc.vector.reciprocal(rz[0:TT, slot, :], z[0:TT, slot, :]))
                    z_inv = rz[0:TT, slot, :].unsqueeze(2).broadcast_to([TT, 4, F])
                    chain.link(nc.vector.tensor_tensor(values[0:TT, slot, :, 1, :], v, z_inv, ALU.mult))
                    dve.sem_inc(values_ready, 1)
                    chain.link(nc.vector.tensor_copy(scales[0:TT, g, j, :, 0, :], z_inv))
                    dve.sem_inc(scales_ready, 1)

                counted = []

                def body(b, first):
                    chain = Chain(dve, dve_done) if first else Chain(dve, dve_done, counted[0] + per_batch * (b - 1))
                    for s in range(SETS):
                        group_end = (b, 0) if s == NT else (b - 1, 1) if s == 0 and not first else None
                        if group_end:
                            turned_scales(*group_end, chain)
                            scaled(*group_end, 0, chain)
                        if s == 5 and not first:
                            residual(b - 1, chain)
                        weights(b, s, chain)
                        if group_end:
                            scaled(*group_end, 1, chain)
                        if s == 5 and not first:
                            statistics(b - 1, chain)
                    if first:
                        counted.append(chain.n)
                    else:
                        assert chain.n == per_batch
                end_of_batch = 2 + 2 + 2 + NT
                per_batch = 4 * SETS + 4 + end_of_batch
                batches(dve, body)
                assert counted[0] == per_batch - end_of_batch
                chain = Chain(dve, dve_done, counted[0] + per_batch * (B - 1))
                turned_scales(B - 1, 1, chain)
                scaled(B - 1, 1, 0, chain)
                scaled(B - 1, 1, 1, chain)
                residual(B - 1, chain)
                statistics(B - 1, chain)


def normalized_tiles(nc, dve, chain, xn, h, mean, rstd, batch):
    for t in range(NT):
        col = batch * NT + t
        chain.add(nc.vector.tensor_scalar(
            xn[0:TT, t, :], h[0:TT, bass.ds(col, 1), :], mean[0:TT, bass.ds(col, 1)],
            rstd[0:TT, bass.ds(col, 1)], ALU.subtract, ALU.mult))
    chain.settle()


def expert_of_batch(nc, io, h, stats, mean, rstd, slots_dram, pairs_dram, psum, ident, ones):
    NE = 16
    with Memory(nc, "expert_of_batch") as m:
        xn = m.sbuf("xn", [128, 2, NT, D])
        xnT = m.sbuf("xnT", [128, B, L])
        sums = m.sbuf("sums", [128, B, 2])
        wg = m.sbuf("wg", [128, NE])
        bg = m.sbuf("bg", [1, NE])
        scores = m.sbuf("scores", [1, B, NE])
        best = m.sbuf("best", [1, B])
        picks = m.sbuf("picks", [1, B, NE])
        countdown = m.sbuf("countdown", [1, NE])
        gate = m.sbuf("gate", [1, B])
        index = m.sbuf("index", [1, B], I32)
        gates = m.sbuf("gates", [128, B])
        w_sel = m.sbuf("w_sel", [128, B, D])
        b_sel = m.sbuf("b_sel", [1, B, D])
        xT = m.sbuf("xT", [128, 2, L])
        loaded, xn_ready, xnT_psum, xnT_ready, scores_psum = (
            m.sem(s) for s in ("loaded", "xn_ready", "xnT_psum", "xnT_ready", "scores_psum"))
        dve_chain, exp_in, exp_out, index_ready, picked, gates_psum = (
            m.sem(s) for s in ("dve_chain", "exp_in", "exp_out", "index_ready", "picked", "gates_psum"))
        gates_ready, gated_ready, xT_ready, xT_free, y_psum, y_free = (
            m.sem(s) for s in ("gates_ready", "gated_ready", "xT_ready", "xT_free", "y_psum", "y_free"))
        per_part = [NEXP * SLOTS * ROW // 128 // ZERO_PARTS, B * L * ACTIVE * D // 128 // ZERO_PARTS]
        assert NEXP * SLOTS * ROW % (128 * ZERO_PARTS) == 0 and B * L * ACTIVE * D % (128 * ZERO_PARTS) == 0
        zeros = m.sbuf("zeros", [128, max(per_part)])
        zeros_made, zeros_stored = m.sem("zeros_made"), m.sem("zeros_stored")
        flats = [dram.rearrange("r d -> (r d)").rearrange("(k p n) -> k p n", k=ZERO_PARTS, p=128)
                 for dram in (slots_dram, pairs_dram)]
        with nc.Block() as block:
            @block.gpsimd
            def _(pool):
                nc.gpsimd.memset(zeros[:], 0.0).then_inc(zeros_made, 1)
                pool.wait_ge(zeros_made, 1)
                for flat, n in zip(flats, per_part):
                    for k in range(ZERO_PARTS):
                        pool.dma_start(flat[k], zeros[:, 0:n]).then_inc(zeros_stored, 16)
                pool.wait_ge(zeros_stored, 2 * 16 * ZERO_PARTS)

            @block.sync
            def _(sp):
                sp.dma_start(wg[:], io["moe0_wg"]).then_inc(loaded, 16)
                sp.dma_start(bg[:], io["moe0_bg"]).then_inc(loaded, 16)
                sp.dma_start(countdown[:], io["countdown"]).then_inc(loaded, 16)
                sp.wait_ge(index_ready, 1)
                for b in range(B):
                    e = sp.value_load(index[0:1, b:b + 1], min_val=0, max_val=NE - 1)
                    sp.dma_start(w_sel[:, b, :], io["moe0_we"][bass.ds(e, 1), :, :].rearrange("o p n -> p (o n)")
                                 ).then_inc(picked, 16)
                    sp.dma_start(b_sel[:, b, :], io["moe0_be"][bass.ds(e, 1), :]).then_inc(picked, 16)

            @block.tensor
            def _(pe):
                with pe.Fori(0, B // 2) as i:
                    for u in range(2):
                        pe.wait_ge(xn_ready, 2 * i + (u + 1))
                        pe.wait_ge(xT_free, 2 * i + (u + 1))
                        for t in range(NT):
                            mm = nc.tensor.transpose(psum[2 * u + t // 3][:, (t % 3) * TT:(t % 3 + 1) * TT],
                                                     xn[0:TT, u, t, :], ident[0:TT, 0:TT])
                        mm.then_inc(xnT_psum, 1)
                pe.wait_ge(xnT_ready, 2 * B)
                pe.wait_ge(loaded, 48)
                for b in range(B):
                    for half in range(2):
                        mm = nc.tensor.matmul(psum[4][0:1, b * NE:(b + 1) * NE], sums[:, b, half:half + 1], wg[:],
                                              start=(half == 0), stop=(half == 1))
                mm.then_inc(scores_psum, 1)
                pe.wait_ge(gates_ready, 1)
                nc.tensor.matmul(psum[5][:, 0:B], ones[0:1, :], gate[:], start=True, stop=True).then_inc(gates_psum, 1)
                pe.wait_ge(gated_ready, 1)
                with pe.Fori(0, B // 2) as i:
                    for u in range(2):
                        pe.wait_ge(xT_ready, 2 * i + (u + 1))
                        pe.wait_ge(y_free, 2 * i + (u + 1))
                        for t in range(NT):
                            out = psum[2 * u + t // 3][0:TT, (t % 3) * D:(t % 3 + 1) * D]
                            nc.tensor.matmul(out, ones[0:1, 0:TT], b_sel[:, bass.ds(2 * i + u, 1), :], start=True, stop=False)
                            mm = nc.tensor.matmul(out, xT[:, u, t * TT:(t + 1) * TT], w_sel[:, bass.ds(2 * i + u, 1), :],
                                                  start=False, stop=True)
                        mm.then_inc(y_psum, 1)

            @block.scalar
            def _(act):
                act.sem_inc(xT_free, 2)
                with act.Fori(0, B // 2) as i:
                    for u in range(2):
                        act.wait_ge(xnT_psum, 2 * i + (u + 1))
                        for half in range(2):
                            nc.scalar.activation(
                                xnT[:, bass.ds(2 * i + u, 1), half * HALF:(half + 1) * HALF],
                                psum[2 * u + half][:, 0:HALF], ACT.Identity,
                                accum_out=sums[:, bass.ds(2 * i + u, 1), half:half + 1].rearrange("p a b -> p (a b)")
                            ).then_inc(xnT_ready, 1)
                        act.wait_ge(xnT_ready, 2 * (2 * i + u) + 2)
                        act.sem_inc(xT_free, 1)
                act.wait_ge(exp_in, 1)
                nc.scalar.activation(picks[:], scores[:], ACT.Exp).then_inc(exp_out, 1)
                with act.Fori(0, B // 2) as i:
                    for u in range(2):
                        act.wait_ge(y_free, 2 * i + (u + 1))
                        act.sem_inc(xT_free, 1)
                        nc.scalar.activation(xT[:, u, :], xnT[:, bass.ds(2 * i + u, 1), :],
                                             ACT.Identity).then_inc(xT_ready, 1)

            @block.vector
            def _(dve):
                with dve.Fori(0, B // 2) as i:
                    chain = Chain(dve, dve_chain, 2 * NT * i)
                    for u in range(2):
                        dve.wait_ge(xT_free, 2 * i + (u + 1))
                        normalized_tiles(nc, dve, chain, xn[:, u], h, mean, rstd, 2 * i + u)
                        dve.sem_inc(xn_ready, 1)
                chain = Chain(dve, dve_chain, NTILES)
                dve.wait_ge(scores_psum, 1)
                wide = best[:].unsqueeze(2).broadcast_to([1, B, NE])
                chain.link(nc.vector.scalar_tensor_tensor(
                    out=scores[:], in0=psum[4][0:1, 0:B * NE].rearrange("p (b e) -> p b e", e=NE), scalar=1.0 / L,
                    in1=bg[:].unsqueeze(1).broadcast_to([1, B, NE]), op0=ALU.mult, op1=ALU.add))
                chain.link(nc.vector.tensor_reduce(best[:], scores[:], AX.X, ALU.max))
                chain.link(nc.vector.tensor_tensor(scores[:], scores[:], wide, ALU.subtract))
                dve.sem_inc(exp_in, 1)
                dve.wait_ge(exp_out, 1)
                chain.link(nc.vector.tensor_reduce(gate[:], picks[:], AX.X, ALU.add))
                chain.link(nc.vector.reciprocal(gate[:], gate[:]))
                dve.sem_inc(gates_ready, 1)
                chain.link(nc.vector.tensor_scalar(picks[:], scores[:], 0.0, None, ALU.is_ge))
                chain.link(nc.vector.tensor_tensor(picks[:], picks[:], countdown[:].unsqueeze(1).broadcast_to([1, B, NE]), ALU.mult))
                chain.link(nc.vector.tensor_reduce(best[:], picks[:], AX.X, ALU.max))
                chain.link(nc.vector.tensor_scalar(index[:], best[:], -1.0, float(NE), ALU.mult, ALU.add))
                dve.sem_inc(index_ready, 1)
                dve.wait_ge(gates_psum, 1)
                chain.link(nc.vector.tensor_copy(gates[:], psum[5][:, 0:B]))
                dve.wait_ge(picked, 32 * B)
                chain.add(nc.vector.tensor_tensor(w_sel[:], w_sel[:], spread(gates[:], D), ALU.mult))
                chain.link(nc.vector.tensor_tensor(b_sel[:], b_sel[:], spread(gates[0:1, :], D), ALU.mult))
                dve.sem_inc(gated_ready, 1)
                dve.sem_inc(y_free, 2)
                after = NTILES + chain.n
                with dve.Fori(0, B // 2) as i:
                    chain = Chain(dve, dve_chain, after + 2 * (2 + NT) * i)
                    for u in range(2):
                        dve.wait_ge(y_psum, 2 * i + (u + 1))
                        for k in range(2):
                            rows = h[0:TT, bass.ds((2 * i + u) * NT + 3 * k, 3), :]
                            chain.add(nc.vector.tensor_tensor(rows, rows, psum[2 * u + k][0:TT, 0:3 * D].rearrange(
                                "p (t d) -> p t d", d=D), ALU.add))
                        chain.settle()
                        dve.sem_inc(y_free, 1)
                        for t in range(NT):
                            chain.add(nc.vector.bn_stats(stats[0:TT, bass.ds((2 * i + u) * NT + t, 1), :],
                                                         h[0:TT, bass.ds((2 * i + u) * NT + t, 1), :]))
                        chain.settle()
                    assert chain.n == 2 * (2 + NT)


C = 10
SUB = C // 2
NCH = L // C
HALVES = [(0, 38 * C), (38 * C, L)]
NCOEF = 3 * SUB * SUB


def delta_projections(nc, io, h, mean, rstd, kq_all, v_all, beta, k_rows_dram, psum, ident):
    with Memory(nc, "proj") as m:
        w_kq = m.sbuf("w_kq", [128, 2 * D])
        w_v = m.sbuf("w_v", [128, D])
        w_b = m.sbuf("w_b", [128, D])
        xn = m.sbuf("xn", [128, NT, D])
        xnT = m.sbuf("xnT", [128, L])
        sq = m.sbuf("sq", [128, NT, 2 * D])
        norm = m.sbuf("norm", [128, NT * 2 * H])
        kqn = m.sbuf("kqn", [128, NT, 2 * D])
        turned = m.sbuf("turned", [128, 2, L])
        names = ("loaded xn_ready xnT_psum xnT_ready v_psum v_taken kq_psum sq_ready norm_sq norm_ready kqn_ready "
                 "b_psum b_taken kT_psum kT_ready k_taken q_taken kT_free k_stored k_free xn_chain kept_chain dve_chain")
        s = {n: m.sem(n) for n in names.split()}

        def batches(eng, body):
            body(0, False, True)
            with eng.Fori(1, B - 1) as b:
                body(b, True, True)
            body(B - 1, True, False)

        with nc.Block() as block:
            @block.sync
            def _(sp):
                sp.dma_start(w_kq[:, 0:D], io["wk"]).then_inc(s["loaded"], 16)
                sp.dma_start(w_kq[:, D:2 * D], io["wq"]).then_inc(s["loaded"], 16)
                sp.dma_start(w_v[:], io["wv"]).then_inc(s["loaded"], 16)
                sp.dma_start(w_b[:], io["wb"]).then_inc(s["loaded"], 16)
                sp.sem_inc(s["k_free"], 1)
                with sp.Fori(0, B) as b:
                    sp.wait_ge(s["kqn_ready"], b + 1)
                    sp.dma_start(k_rows_dram[bass.ds(b, 1), :, :].rearrange("o (t p) d -> p (o t) d", p=TT),
                                 kqn[0:TT, :, 0:D]).then_inc(s["k_stored"], 16)
                    sp.wait_ge(s["k_stored"], 16 * b + 16)
                    sp.sem_inc(s["k_free"], 1)

            @block.tensor
            def _(pe):
                pe.wait_ge(s["loaded"], 64)

                def x_turned(b):
                    pe.wait_ge(s["xn_ready"], b + 1)
                    pe.wait_ge(s["q_taken"], b + 1)
                    for t in range(NT):
                        mm = nc.tensor.transpose(psum[t // 3][:, (t % 3) * TT:(t % 3 + 1) * TT],
                                                 xn[0:TT, t, :], ident[0:TT, 0:TT])
                    mm.then_inc(s["xnT_psum"], 1)

                def kq_turned(b):
                    for which, base in enumerate((5, 0)):
                        if which == 0:
                            pe.wait_ge(s["v_taken"], b + 1)
                        for t in range(NT):
                            mm = nc.tensor.transpose(psum[base + t // 3][:, (t % 3) * TT:(t % 3 + 1) * TT],
                                                     kqn[0:TT, t, which * D:(which + 1) * D], ident[0:TT, 0:TT])
                        mm.then_inc(s["kT_psum"], 1)

                def rates(b, half):
                    pe.wait_ge(s["b_taken"], 2 * b + half + 1)
                    lo, hi = HALVES[half]
                    nc.tensor.matmul(psum[7][:, 0:hi - lo], w_b[:], xnT[:, lo:hi], start=True, stop=True
                                     ).then_inc(s["b_psum"], 1)

                def body(b, before, follows):
                    pe.wait_ge(s["xnT_ready"], 2 * b + 2)
                    if before:
                        pe.wait_ge(s["kqn_ready"], b)
                    for t in range(NT):
                        mm = nc.tensor.matmul(psum[2 + t // 2][0:TT, (t % 2) * 2 * D:(t % 2 + 1) * 2 * D],
                                              xnT[:, t * TT:(t + 1) * TT], w_kq[:], start=True, stop=True)
                    mm.then_inc(s["kq_psum"], 1)
                    if before:
                        kq_turned(b - 1)
                    rates(b, 0)
                    pe.wait_ge(s["k_taken"], b + 1)
                    for half, (lo, hi) in enumerate(HALVES):
                        mm = nc.tensor.matmul(psum[5 + half][:, 0:hi - lo], w_v[:], xnT[:, lo:hi], start=True, stop=True)
                    mm.then_inc(s["v_psum"], 1)
                    rates(b, 1)
                    if follows:
                        x_turned(b + 1)
                x_turned(0)
                batches(pe, body)
                pe.wait_ge(s["kqn_ready"], B)
                kq_turned(B - 1)

            @block.scalar
            def _(act):
                act.sem_inc(s["k_taken"], 1)
                act.sem_inc(s["q_taken"], 2)
                act.sem_inc(s["b_taken"], 1)

                def x_turned(b):
                    act.wait_ge(s["xnT_psum"], b + 1)
                    for half in range(2):
                        nc.scalar.activation(xnT[:, half * HALF:(half + 1) * HALF], psum[half][:, 0:HALF],
                                             ACT.Identity).then_inc(s["xnT_ready"], 1)

                def kq_turned(b, which):
                    act.wait_ge(s["kT_psum"], 2 * b + which + 1)
                    act.wait_ge(s["kT_free"], 2 * b + which + 1)
                    base = 0 if which else 5
                    for half in range(2):
                        nc.scalar.activation(turned[:, which, half * HALF:(half + 1) * HALF],
                                             psum[base + half][:, 0:HALF], ACT.Identity).then_inc(s["kT_ready"], 1)
                    act.wait_ge(s["kT_ready"], 4 * b + 2 * which + 2)
                    act.sem_inc(s["q_taken" if which else "k_taken"], 1)

                def rates(b, half):
                    act.wait_ge(s["b_psum"], 2 * b + half + 1)
                    lo, hi = HALVES[half]
                    nc.scalar.activation(beta[:, bass.ds(b, 1), lo:hi], psum[7][:, 0:hi - lo], ACT.Identity
                                         ).then_inc(s["b_taken"], 1)

                def body(b, before, follows):
                    act.wait_ge(s["kq_psum"], b + 1)
                    for k in range(3):
                        ins = nc.scalar.activation(sq[0:TT, 2 * k:2 * k + 2, :], psum[2 + k][0:TT, :], ACT.Square)
                    ins.then_inc(s["sq_ready"], 1)
                    if before:
                        kq_turned(b - 1, 0)
                    act.wait_ge(s["norm_sq"], b + 1)
                    nc.scalar.activation(norm[0:TT, :], norm[0:TT, :], ACT.Sqrt).then_inc(s["norm_ready"], 1)
                    if before:
                        kq_turned(b - 1, 1)
                    rates(b, 0)
                    rates(b, 1)
                    if follows:
                        x_turned(b + 1)
                x_turned(0)
                batches(act, body)
                kq_turned(B - 1, 0)
                kq_turned(B - 1, 1)

            @block.vector
            def _(dve):
                dve.sem_inc(s["kT_free"], 2)

                def normalized(b):
                    if b is not first_batch:
                        dve.wait_ge(s["xnT_psum"], b)
                    chain = Chain(dve, s["xn_chain"], NT * b)
                    normalized_tiles(nc, dve, chain, xn, h, mean, rstd, b)
                    dve.sem_inc(s["xn_ready"], 1)

                def kept(b, which):
                    dve.wait_ge(s["kT_ready"], 4 * b + 2 * which + 2)
                    chain = Chain(dve, s["kept_chain"], 2 * b + which)
                    chain.link(nc.vector.tensor_copy(
                        kq_all[:, :, bass.ds(b, 1), which, :].rearrange("p c o t -> p c (o t)"),
                        turned[:, which, :].rearrange("p (c t) -> p c t", t=C)))
                    dve.sem_inc(s["kT_free"], 1)

                def body(b, before, follows):
                    if follows:
                        normalized(b + 1)
                    chain = Chain(dve, s["dve_chain"], 7 * b)
                    dve.wait_ge(s["sq_ready"], b + 1)
                    chain.link(nc.vector.tensor_reduce(norm[0:TT, :], sq[0:TT, :, :].rearrange("p t (g f) -> p (t g) f", f=F),
                                                       AX.X, ALU.add))
                    dve.sem_inc(s["norm_sq"], 1)
                    dve.wait_ge(s["norm_ready"], b + 1)
                    chain.link(nc.vector.reciprocal(norm[0:TT, :], norm[0:TT, :]))
                    if before:
                        dve.wait_ge(s["kT_ready"], 4 * b)
                    dve.wait_ge(s["k_free"], b + 1)
                    for k in range(3):
                        chain.add(nc.vector.tensor_tensor(
                            kqn[0:TT, 2 * k:2 * k + 2, :].rearrange("p t (g f) -> p (t g) f", f=F),
                            psum[2 + k][0:TT, :].rearrange("p (g f) -> p g f", f=F),
                            spread(norm[0:TT, 32 * k:32 * k + 32], F), ALU.mult))
                    chain.settle()
                    dve.sem_inc(s["kqn_ready"], 1)
                    if before:
                        kept(b - 1, 0)
                        kept(b - 1, 1)
                    dve.wait_ge(s["v_psum"], b + 1)
                    for half, (lo, hi) in enumerate(HALVES):
                        chain.add(nc.vector.tensor_copy(
                            v_all[:, lo // C:hi // C, bass.ds(b, 1), :].rearrange("p c o t -> p c (o t)"),
                            psum[5 + half][:, 0:hi - lo].rearrange("p (c t) -> p c t", t=C)))
                    chain.settle()
                    dve.sem_inc(s["v_taken"], 1)
                    assert chain.n == 7
                first_batch = 0
                normalized(first_batch)
                batches(dve, body)
                kept(B - 1, 0)
                kept(B - 1, 1)


def triangular_coefficients(nc, kq_all, beta, coef_dram, psum, block_sum):
    with Memory(nc, "coef") as m:
        products = m.sbuf("products", [128, 3, L])
        inv = m.sbuf("inv", [128, NCH, 2, SUB, SUB])
        neg = m.sbuf("neg", [128, NCH, 2, SUB, SUB])
        cross = m.sbuf("cross", [128, NCH, SUB * SUB])
        out = m.sbuf("out", [128, NCH, NCOEF])
        term = m.sbuf("term", [128, 2 * NCH, SUB - 1])
        names = "products_ready products_free dots_psum dots_free dve_chain beta_ready cross_ready cross_free out_ready out_free stored gate"
        s = {n: m.sem(n) for n in names.split()}
        groups = []
        for d in range(1, C):
            width = C - d
            per = 512 // width
            for lo in range(0, NCH, per):
                groups.append((d, width, lo, min(NCH, lo + per)))
        ND = C - 1
        RING = 6
        assert len(groups) % RING == 0

        with nc.Block() as block:
            @block.sync
            def _(sp):
                sp.sem_inc(s["out_free"], 1)
                with sp.Fori(0, B) as b:
                    sp.wait_ge(s["out_ready"], b + 1)
                    sp.dma_start(coef_dram[bass.ds(b, 1), :, :, :].rearrange("o p c k -> p (o c) k"),
                                 out[:]).then_inc(s["stored"], 16)
                    sp.wait_ge(s["stored"], 16 * b + 16)
                    sp.sem_inc(s["out_free"], 1)

            @block.gpsimd
            def _(pool):
                with pool.Fori(0, B) as b:
                    for d in range(1, C):
                        pass_gate(pool, s["products_free"], ND * b + d, s["gate"])
                        width = C - d
                        nc.gpsimd.tensor_tensor(
                            products[:, d % 3, 0:NCH * width].rearrange("p (c t) -> p c t", t=width),
                            kq_all[:, :, bass.ds(b, 1), 0, d:C].rearrange("p c o t -> p c (o t)"),
                            kq_all[:, :, bass.ds(b, 1), 0, 0:width].rearrange("p c o t -> p c (o t)"),
                            ALU.mult).then_inc(s["products_ready"], 1)

            @block.tensor
            def _(pe):
                pe.sem_inc(s["products_free"], 3)
                with pe.Fori(0, B) as b:
                    for n, (d, width, lo, hi) in enumerate(groups):
                        if lo == 0:
                            pe.wait_ge(s["products_ready"], ND * b + d)
                        pe.wait_ge(s["dots_free"], len(groups) * b + n + 1)
                        nc.tensor.matmul(psum[n % RING][:, 0:(hi - lo) * width], block_sum[:],
                                         products[:, d % 3, lo * width:hi * width], start=True, stop=True
                                         ).then_inc(s["dots_psum"], 1)
                        if n > 0 and groups[n - 1][3] == NCH:
                            pe.wait_ge(s["dots_psum"], len(groups) * b + n)
                            pe.sem_inc(s["products_free"], 1)
                    pe.wait_ge(s["dots_psum"], len(groups) * b + len(groups))
                    pe.sem_inc(s["products_free"], 1)

            @block.scalar
            def _(act):
                act.sem_inc(s["cross_free"], 1)
                for b in range(B):
                    nc.scalar.activation(beta[:, b, :], beta[:, b, :], ACT.Sigmoid).then_inc(s["beta_ready"], 1)
                with act.Fori(0, B) as b:
                    act.wait_ge(s["cross_ready"], b + 1)
                    act.wait_ge(s["out_free"], b + 1)
                    nc.scalar.activation(out[:, :, SUB * SUB:2 * SUB * SUB], cross[:], ACT.Identity
                                         ).then_inc(s["cross_free"], 1)

            @block.vector
            def _(dve):
                first = Chain(dve, s["dve_chain"])
                first.add(nc.vector.memset(inv[:], 0.0))
                first.settle()
                for t in range(SUB):
                    first.add(nc.vector.memset(inv[:, :, :, t, t], 1.0))
                first.settle()
                dve.sem_inc(s["dots_free"], RING)

                def batch(b, base):
                    chain = Chain(dve, s["dve_chain"], base)
                    dve.wait_ge(s["cross_free"], b + 1)
                    dve.wait_ge(s["beta_ready"], b + 1)
                    for n, (d, width, lo, hi) in enumerate(groups):
                        dve.wait_ge(s["dots_psum"], len(groups) * b + n + 1)
                        dots = psum[n % RING][:, 0:(hi - lo) * width].rearrange("p (c t) -> p c t", t=width)
                        before = chain.n
                        for part in range(2):
                            k = SUB - d
                            if k <= 0:
                                continue
                            dst = neg[:, lo:hi, part, :, :].rearrange("p c t s -> p c (t s)")[:, :, d * SUB:d * SUB + (k - 1) * (SUB + 1) + 1:SUB + 1]
                            times = beta[:, bass.ds(b, 1), :].rearrange("p o (c t) -> p (o c) t", t=C)[:, lo:hi, part * SUB + d:part * SUB + SUB]
                            chain.add(nc.vector.scalar_tensor_tensor(
                                out=dst, in0=dots[:, :, part * SUB:part * SUB + k], scalar=-1.0, in1=times,
                                op0=ALU.mult, op1=ALU.mult))
                        s0, s1 = max(0, SUB - d), min(SUB, C - d)
                        t0 = s0 + d - SUB
                        at = t0 * SUB + s0
                        dst = cross[:, lo:hi, at:at + (s1 - s0 - 1) * (SUB + 1) + 1:SUB + 1]
                        chain.add(nc.vector.tensor_scalar(dst, dots[:, :, s0:s1], -1.0, None, ALU.mult))
                        if n > 0:
                            dve.wait_ge(s["dve_chain"], base + before)
                            dve.sem_inc(s["dots_free"], 1)
                    chain.settle()
                    dve.sem_inc(s["dots_free"], 1)
                    dve.sem_inc(s["cross_ready"], 1)
                    flat_inv = inv[:].rearrange("p c a t s -> p (c a) t s")
                    flat_neg = neg[:].rearrange("p c a t s -> p (c a) t s")
                    NB = 2 * NCH
                    for t in range(1, SUB):
                        chain.add(nc.vector.tensor_copy(flat_inv[:, :, t, 0:t], flat_neg[:, :, t, 0:t]))
                    chain.settle()
                    for r in range(1, SUB - 1):
                        later = SUB - 1 - r
                        added = term[:, :, 0:later * r].rearrange("p c (t s) -> p c t s", s=r)
                        chain.link(nc.vector.tensor_tensor(
                            added, flat_inv[:, :, r:r + 1, 0:r].broadcast_to([128, NB, later, r]),
                            flat_neg[:, :, r + 1:SUB, r:r + 1].broadcast_to([128, NB, later, r]), ALU.mult))
                        rows = flat_inv[:, :, r + 1:SUB, 0:r]
                        chain.link(nc.vector.tensor_tensor(rows, rows, added, ALU.add))
                    dve.wait_ge(s["out_free"], b + 1)
                    for part in range(2):
                        beta_s = beta[:, bass.ds(b, 1), :].rearrange("p o (c t) -> p (o c) t", t=C)[:, :, part * SUB:(part + 1) * SUB]
                        at = 2 * SUB * SUB * part
                        chain.add(nc.vector.tensor_tensor(
                            out[:, :, at:at + SUB * SUB].rearrange("p c (t s) -> p c t s", s=SUB), inv[:, :, part],
                            beta_s.unsqueeze(2).broadcast_to([128, NCH, SUB, SUB]), ALU.mult))
                    chain.settle()
                    dve.wait_ge(s["cross_free"], b + 2)
                    dve.sem_inc(s["out_ready"], 1)
                    return chain.n

                per = sum(1 + 2 * (SUB - d > 0) for d, _, _, _ in groups) + (SUB - 1) + 2 * (SUB - 2) + 2
                with dve.Fori(0, B) as b:
                    assert batch(b, first.n + per * b) == per


RING = 3
STREAMS = 2
BS = B // STREAMS


def delta_rule(nc, io, kq_all, v_all, u_all, o_all, k_rows_dram, coef_dram, psum_banks, psum):
    with Memory(nc, "delta") as m:
        masks = m.sbuf("masks", [128, 2])
        kq = m.sbuf("kq", [128, RING, B, 2 * C])
        k_rows = m.sbuf("k_rows", [128, RING, B, 32])
        coef = m.sbuf("coef", [128, 2, B, RING, NCOEF])
        state = m.sbuf("state", [128, B, 32])
        first_terms = m.sbuf("first_terms", [128, RING, B, SUB, 2 * SUB])
        prod = m.sbuf("prod", [128, STREAMS, BS, SUB, SUB])
        coupling = m.sbuf("coupling", [128, STREAMS, BS, SUB, SUB + 1])
        coupled = m.sbuf("coupled", [128, STREAMS, BS, SUB])
        u_pad = m.sbuf("u_pad", [128, RING, B, 32])
        u_rows = m.sbuf("u_rows", [128, RING, B, 32])
        loaded, gate, pool_gate, zeroed = m.sem("loaded"), m.sem("gate"), m.sem("pool_gate"), m.sem("zeroed")
        kq_ready, kq_free = m.sem("kq_ready"), m.sem("kq_free")
        rows_free = m.sem("rows_free")
        rows_ready = [m.sem(f"rows_ready{u}") for u in range(RING)]
        coef_ready = [m.sem(f"coef_ready{k}") for k in range(2)]
        coef_free = m.sem("coef_free")
        r_psum = [m.sem(f"r_psum{x}") for x in range(STREAMS)]
        u_ready = [m.sem(f"u_ready{x}") for x in range(STREAMS)]
        s_psum = [m.sem(f"s_psum{x}") for x in range(STREAMS)]
        s_ready = [m.sem(f"s_ready{x}") for x in range(STREAMS)]
        q_taken = [m.sem(f"q_taken{x}") for x in range(STREAMS)]
        r_taken = [m.sem(f"r_taken{x}") for x in range(STREAMS)]
        act_gate = m.sem("act_gate")
        terms_ready, terms_free = m.sem("terms_ready"), m.sem("terms_free")
        u_kept = m.sem("u_kept")
        dve_chain = m.sem("dve_chain")
        SOLVE = 7

        def state_bank(x, part):
            return psum[4 + 2 * x + part][:, 0:32 * BS // 2]

        def own(x):
            return slice(x * BS, (x + 1) * BS)

        def chunks(eng, body):
            for u in range(RING):
                body(u, u, u == 0, 0, 0, 1, u % 2)
            with eng.Fori(0, (NCH - RING) // (2 * RING)) as i:
                for k in range(2):
                    for u in range(RING):
                        body(2 * RING * i + (RING * (k + 1) + u), u, False, 2 * i + (k + 1), 1 - k, i + (k + 1),
                             (RING * (k + 1) + u) % 2)

        with nc.Block() as block:
            @block.sync
            def _(sp):
                sp.dma_start(masks[:], io["pair_masks"]).then_inc(loaded, 16)

                def body(c, u, first, turn, half, uses, bank):
                    sp.wait_ge(rows_free, c + 1)
                    for w in range(4):
                        src = k_rows_dram[:, bass.ds(c * C, C), 32 * w:32 * w + 32].rearrange("b t k -> t b k")
                        sp.dma_start(k_rows[32 * w:32 * w + C, u, :, :], src).then_inc(rows_ready[u], 16)
                    if u == 0:
                        sp.wait_ge(coef_free, turn + 1)
                        sp.dma_start(coef[:, half].rearrange("p b c k -> p b (c k)"),
                                     coef_dram[:, :, bass.ds(c, RING), :].rearrange("b p c k -> p b (c k)")
                                     ).then_inc(coef_ready[half], 16)
                chunks(sp, body)

            @block.gpsimd
            def _(pool):
                def body(c, u, first, turn, half, uses, bank):
                    pass_gate(pool, kq_free, c + 1, pool_gate)
                    nc.gpsimd.tensor_copy(kq[:, u, :, :], kq_all[:, bass.ds(c, 1), :, :, :].rearrange(
                        "p o b a t -> p (o b) (a t)")).then_inc(kq_ready, 1)
                    pass_gate(pool, coef_ready[half], 16 * uses, pool_gate)
                    pass_gate(pool, terms_free, c + 1, pool_gate)
                    nc.gpsimd.tensor_tensor(
                        first_terms[:, u, :, :, SUB:2 * SUB],
                        coef[:, half, :, u, 0:SUB * SUB].rearrange("p b (t s) -> p b t s", s=SUB),
                        v_all[:, bass.ds(c, 1), :, 0:SUB].rearrange("p o b t -> p (o b) t").unsqueeze(2).broadcast_to(
                            [128, B, SUB, SUB]), ALU.mult).then_inc(terms_ready, 1)
                    if not first:
                        keep_u(c - 1, (u - 1) % RING)

                def keep_u(c, u):
                    pool.wait_ge(u_ready[0], c + 1)
                    pass_gate(pool, u_ready[1], c + 1, pool_gate)
                    nc.gpsimd.tensor_copy(u_all[:, bass.ds(c, 1), :, :].rearrange("p o b t -> p (o b) t"),
                                          u_pad[:, u, :, 0:C]).then_inc(u_kept, 1)
                pool.sem_inc(u_kept, RING)
                chunks(pool, body)
                keep_u(NCH - 1, RING - 1)

            @block.tensor
            def _(pe):
                pe.sem_inc(rows_free, RING)
                pe.sem_inc(kq_free, RING)
                pe.wait_ge(zeroed, 1)
                for x in range(STREAMS):
                    for part in range(2):
                        for w in range(4):
                            nc.tensor.matmul(state_bank(x, part)[32 * w:32 * w + 32, :], state[32 * w:32 * w + 32, 0, :],
                                             state[32 * w:32 * w + 32, 0:BS // 2, :].rearrange("p b k -> p (b k)"),
                                             start=True, stop=False, skip_group_check=True)

                def residuals(c, u, x, bank):
                    if x == 0:
                        pe.wait_ge(kq_ready, c + 1)
                    pe.wait_ge(q_taken[x], c + 1)
                    for b in range(x * BS, (x + 1) * BS):
                        if b % (BS // 2) == 0:
                            pass_gate(pe, s_ready[x], 2 * c + b % BS // (BS // 2) + 1, gate)
                        for w in range(4):
                            rows = slice(32 * w, 32 * w + 32)
                            mm = nc.tensor.matmul(psum[2 * x + bank][rows, 2 * C * b:2 * C * (b + 1)], state[rows, b, :],
                                                  kq[rows, u, b, :], start=True, stop=True)
                    mm.then_inc(r_psum[x], 1)

                def add_updates(c, u, x, turn):
                    if x == 0:
                        pe.wait_ge(rows_ready[u], 64 * turn + 64)
                    pass_gate(pe, u_ready[x], c + 1, gate)
                    for b in range(x * BS, (x + 1) * BS):
                        for w in range(4):
                            rows = slice(32 * w, 32 * w + C)
                            part, at = divmod(b % BS, BS // 2)
                            mm = nc.tensor.matmul(state_bank(x, part)[32 * w:32 * w + 32, 32 * at:32 * at + 32],
                                                  k_rows[rows, u, b, :], u_rows[rows, u, b, :],
                                                  start=False, stop=False, skip_group_check=True)
                        if at == BS // 2 - 1:
                            mm.then_inc(s_psum[x], 1)
                    if x == 1:
                        pass_gate(pe, s_psum[x], 2 * c + 2, gate)
                        pe.sem_inc(rows_free, 1)
                        pe.sem_inc(kq_free, 1)

                def body(c, u, first, turn, half, uses, bank):
                    residuals(c, u, 0, bank)
                    if not first:
                        add_updates(c - 1, (u - 1) % RING, 1, None)
                    residuals(c, u, 1, bank)
                    add_updates(c, u, 0, turn)
                chunks(pe, body)
                add_updates(NCH - 1, RING - 1, 1, None)

            @block.scalar
            def _(act):
                act.wait_ge(loaded, 16)
                act.wait_ge(zeroed, 1)
                for x in range(STREAMS):
                    act.sem_inc(s_ready[x], 2)
                    act.sem_inc(q_taken[x], 2)

                def keep_q(c, x, bank):
                    pass_gate(act, r_taken[x], c + 1, act_gate)
                    nc.scalar.activation(
                        o_all[:, bass.ds(c, 1), own(x), :].rearrange("p o b t -> p (o b) t"),
                        psum[2 * x + bank][:, 2 * C * BS * x:2 * C * BS * (x + 1)].rearrange(
                            "p (b a) -> p b a", a=2 * C)[:, :, C:2 * C], ACT.Identity, scale=-1.0).then_inc(q_taken[x], 1)

                def new_state(c, x):
                    for part in range(2):
                        act.wait_ge(s_psum[x], 2 * c + part + 1)
                        lo = x * BS + part * BS // 2
                        for head in range(2):
                            ins = nc.scalar.activation(
                                state[:, lo:lo + BS // 2, F * head:F * head + F],
                                state_bank(x, part).rearrange("p (b k) -> p b k", k=32)[:, :, F * head:F * head + F],
                                ACT.Identity, scale=masks[:, head:head + 1])
                        ins.then_inc(s_ready[x], 1)

                def body(c, u, first, turn, half, uses, bank):
                    if not first:
                        new_state(c - 1, 1)
                    keep_q(c, 0, bank)
                    new_state(c, 0)
                    keep_q(c, 1, bank)
                chunks(act, body)

            @block.vector
            def _(dve):
                zero = Chain(dve, zeroed)
                zero.add(nc.vector.memset(state[:], 0.0))
                nc.vector.memset(u_pad[:], 0.0).then_inc(dve_chain, 1)
                dve.sem_inc(coef_free, 2)
                dve.sem_inc(terms_free, RING)

                def body(c, u, first, turn, half, uses, bank):
                    chain = Chain(dve, dve_chain, STREAMS * SOLVE * c + 1)
                    for x in range(STREAMS):
                        if x == 0:
                            dve.wait_ge(u_kept, c + 1)
                            dve.wait_ge(terms_ready, c + 1)
                        dve.wait_ge(r_psum[x], c + 1)
                        b = own(x)
                        p_x, w_x, terms = prod[:, x], coupled[:, x], coupling[:, x]
                        inv1, cross, inv2 = (coef[:, half, b, u, k * SUB * SUB:(k + 1) * SUB * SUB].rearrange(
                            "p b (t s) -> p b t s", s=SUB) for k in range(3))

                        def along(values):
                            return values.unsqueeze(2).broadcast_to([128, BS, SUB, SUB])

                        k_s = psum[2 * x + bank][:, 2 * C * BS * x:2 * C * BS * (x + 1)].rearrange(
                            "p (b a) -> p b a", a=2 * C)
                        chain.add(nc.vector.tensor_tensor(first_terms[:, u, b, :, 0:SUB], inv1, along(k_s[:, :, 0:SUB]), ALU.mult))
                        m1_done = chain.n
                        chain.add(nc.vector.tensor_tensor(
                            terms[:, :, :, SUB], v_all[:, bass.ds(c, 1), b, SUB:C].rearrange("p o b t -> p (o b) t"),
                            k_s[:, :, SUB:C], ALU.add))
                        dve.wait_ge(dve_chain, chain.base + m1_done)
                        chain.add(nc.vector.tensor_reduce(u_pad[:, u, b, 0:SUB], first_terms[:, u, b], AX.X, ALU.add))
                        chain.settle()
                        dve.sem_inc(r_taken[x], 1)
                        if x == STREAMS - 1:
                            dve.sem_inc(terms_free, 1)
                        chain.link(nc.vector.tensor_tensor(terms[:, :, :, 0:SUB], cross, along(u_pad[:, u, b, 0:SUB]), ALU.mult))
                        chain.link(nc.vector.tensor_reduce(w_x, terms, AX.X, ALU.add))
                        chain.link(nc.vector.tensor_tensor(p_x, inv2, along(w_x), ALU.mult))
                        chain.link(nc.vector.tensor_reduce(u_pad[:, u, b, SUB:C], p_x, AX.X, ALU.add))
                        nc.vector.transpose(u_rows[:, u, b, :].rearrange("p b k -> p (b k)"),
                                            u_pad[:, u, b, :].rearrange("p b k -> p (b k)")).then_inc(u_ready[x], 1)
                    if u == RING - 1:
                        dve.sem_inc(coef_free, 1)
                chunks(dve, body)


def within_chunks(nc, kq_all, u_all, o_all, psum, block_sum):
    BUFS = C // 2
    with Memory(nc, "within") as m:
        products = m.sbuf("products", [128, BUFS, L])
        terms = m.sbuf("terms", [128, 3, 512])
        names = "products_ready products_free dots_psum dots_free dve_chain gate"
        s = {n: m.sem(n) for n in names.split()}
        groups = []
        for d in range(C):
            width = C - d
            per = 512 // width
            for lo in range(0, NCH, per):
                groups.append((d, width, lo, min(NCH, lo + per)))
        BANKS = 7
        assert len(groups) % BANKS == 0 and C % 2 == 0

        with nc.Block() as block:
            @block.gpsimd
            def _(pool):
                with pool.Fori(0, B) as b:
                    for d in range(C):
                        pass_gate(pool, s["products_free"], C * b + d + 1, s["gate"])
                        width = C - d
                        nc.gpsimd.tensor_tensor(
                            products[:, d % BUFS, 0:NCH * width].rearrange("p (c t) -> p c t", t=width),
                            kq_all[:, :, bass.ds(b, 1), 1, d:C].rearrange("p c o t -> p c (o t)"),
                            kq_all[:, :, bass.ds(b, 1), 0, 0:width].rearrange("p c o t -> p c (o t)"),
                            ALU.mult).then_inc(s["products_ready"], 1)

            @block.tensor
            def _(pe):
                pe.sem_inc(s["products_free"], BUFS)
                with pe.Fori(0, B) as b:
                    for n, (d, width, lo, hi) in enumerate(groups):
                        if lo == 0:
                            pe.wait_ge(s["products_ready"], C * b + d + 1)
                        pe.wait_ge(s["dots_free"], len(groups) * b + n + 1)
                        nc.tensor.matmul(psum[n % BANKS][:, 0:(hi - lo) * width], block_sum[:],
                                         products[:, d % BUFS, lo * width:hi * width], start=True, stop=True
                                         ).then_inc(s["dots_psum"], 1)
                        if n > 0 and groups[n - 1][3] == NCH:
                            pe.wait_ge(s["dots_psum"], len(groups) * b + n)
                            pe.sem_inc(s["products_free"], 1)
                    pe.wait_ge(s["dots_psum"], len(groups) * b + len(groups))
                    pe.sem_inc(s["products_free"], 1)

            @block.vector
            def _(dve):
                dve.sem_inc(s["dots_free"], BANKS)
                with dve.Fori(0, B) as b:
                    chain = Chain(dve, s["dve_chain"], 2 * len(groups) * b)
                    for n in range(len(groups) + 1):
                        issued = chain.n
                        if n < len(groups):
                            d, width, lo, hi = groups[n]
                            dve.wait_ge(s["dots_psum"], len(groups) * b + n + 1)
                            dots = psum[n % BANKS][:, 0:(hi - lo) * width].rearrange("p (c t) -> p c t", t=width)
                            term = terms[:, n % 3, 0:(hi - lo) * width].rearrange("p (c t) -> p c t", t=width)
                            chain.add(nc.vector.tensor_tensor(term, dots, u_all[:, lo:hi, bass.ds(b, 1), 0:width].rearrange(
                                "p c o t -> p c (o t)"), ALU.mult))
                        if n > 0:
                            dve.wait_ge(s["dve_chain"], chain.base + issued)
                            dve.sem_inc(s["dots_free"], 1)
                            d, width, lo, hi = groups[n - 1]
                            term = terms[:, (n - 1) % 3, 0:(hi - lo) * width].rearrange("p (c t) -> p c t", t=width)
                            o = o_all[:, lo:hi, bass.ds(b, 1), d:C].rearrange("p c o t -> p c (o t)")
                            chain.add(nc.vector.tensor_tensor(o, o, term, ALU.add))
                    chain.settle()
                    assert chain.n == 2 * len(groups)


def delta_output(nc, io, h, stats, mean, rstd, o_all, psum, ident, ones):
    with Memory(nc, "output") as m:
        wo = m.sbuf("wo", [128, D])
        ln_cols = m.sbuf("ln_cols", [128, 2])
        wc = m.sbuf("wc", [128, D])
        b_wide = m.sbuf("b_wide", [128, TT])
        bwo = m.sbuf("bwo", [128, D])
        oT = m.sbuf("oT", [128, 2, L])
        yvar = m.sbuf("yvar", [128, NTILES])
        ytmp = m.sbuf("ytmp", [128, NTILES])
        names = "loaded oT_ready oT_free o_psum o_free wg_ready w_psum w_ready dve_chain var_ready root_ready o2_ready o2_free z_psum z_free"
        s = {n: m.sem(n) for n in names.split()}

        def batch_of_o(b):
            return o_all[:, :, bass.ds(b, 1), :].rearrange("p c o t -> p c (o t)")

        def turned(u):
            return oT[:, u, :].rearrange("p (c t) -> p c t", t=C)

        with nc.Block() as block:
            @block.sync
            def _(sp):
                sp.dma_start(wo[:], io["wo"]).then_inc(s["loaded"], 16)
                sp.dma_start(ln_cols[:], io["ln_cols"]).then_inc(s["loaded"], 16)

            @block.tensor
            def _(pe):
                pe.wait_ge(s["wg_ready"], 1)
                nc.tensor.matmul(psum[4][:, 0:D], ones[:], wc[:], start=True, stop=True)
                nc.tensor.matmul(psum[5][0:TT, 0:D], b_wide[:], wo[:], start=True, stop=True).then_inc(s["w_psum"], 1)
                with pe.Fori(0, B // 2) as i:
                    for u in range(2):
                        pe.wait_ge(s["oT_ready"], 2 * i + (u + 1))
                        pe.wait_ge(s["o_free"], 2 * i + (u + 1))
                        for t in range(NT):
                            mm = nc.tensor.transpose(psum[2 * u + t // 3][0:TT, (t % 3) * D:(t % 3 + 1) * D],
                                                     oT[:, u, t * TT:(t + 1) * TT], ident[:])
                        mm.then_inc(s["o_psum"], 1)
                pe.wait_ge(s["w_ready"], 1)
                with pe.Fori(0, B // 2) as i:
                    for u in range(2):
                        pe.wait_ge(s["o2_ready"], 2 * i + (u + 1))
                        pe.wait_ge(s["z_free"], 2 * i + (u + 1))
                        for t in range(NT):
                            mm = nc.tensor.matmul(psum[2 * u + t // 3][0:TT, (t % 3) * D:(t % 3 + 1) * D],
                                                  oT[:, u, t * TT:(t + 1) * TT], wc[:], start=True, stop=True)
                        mm.then_inc(s["z_psum"], 1)

            @block.scalar
            def _(act):
                act.sem_inc(s["oT_free"], 2)
                with act.Fori(0, B // 2) as i:
                    for u in range(2):
                        act.wait_ge(s["oT_free"], 2 * i + (u + 1))
                        nc.scalar.activation(turned(u), batch_of_o(2 * i + u), ACT.Identity).then_inc(s["oT_ready"], 1)
                act.wait_ge(s["var_ready"], 1)
                nc.scalar.activation(ytmp[0:TT, :], yvar[0:TT, :], ACT.Sqrt).then_inc(s["root_ready"], 1)
                act.sem_inc(s["o2_free"], 2)
                with act.Fori(0, B // 2) as i:
                    for u in range(2):
                        act.wait_ge(s["o2_free"], 2 * i + (u + 1))
                        nc.scalar.activation(turned(u), batch_of_o(2 * i + u), ACT.Identity).then_inc(s["o2_ready"], 1)

            @block.vector
            def _(dve):
                chain = Chain(dve, s["dve_chain"])
                dve.wait_ge(s["loaded"], 32)
                chain.link(nc.vector.tensor_scalar(wc[:], wo[:], ln_cols[:, 0:1], None, ALU.mult))
                chain.link(nc.vector.tensor_copy(b_wide[:], ln_cols[:, 1:2].broadcast_to([128, TT])))
                dve.sem_inc(s["wg_ready"], 1)
                dve.wait_ge(s["w_psum"], 1)
                chain.link(nc.vector.scalar_tensor_tensor(out=wc[:], in0=psum[4][:, 0:D], scalar=-1.0 / D, in1=wc[:],
                                                          op0=ALU.mult, op1=ALU.add))
                chain.link(nc.vector.tensor_copy(bwo[0:TT, :], psum[5][0:TT, 0:D]))
                dve.sem_inc(s["w_ready"], 1)
                dve.sem_inc(s["o_free"], 2)
                before = chain.n
                with dve.Fori(0, B // 2) as i:
                    chain = Chain(dve, s["dve_chain"], before + 2 * NT * i)
                    for u in range(2):
                        dve.wait_ge(s["o_psum"], 2 * i + (u + 1))
                        dve.sem_inc(s["oT_free"], 1)
                        for t in range(NT):
                            chain.add(nc.vector.bn_stats(stats[0:TT, bass.ds((2 * i + u) * NT + t, 1), :],
                                                         psum[2 * u + t // 3][0:TT, (t % 3) * D:(t % 3 + 1) * D]))
                        chain.settle()
                        dve.sem_inc(s["o_free"], 1)
                chain = Chain(dve, s["dve_chain"], before + NTILES)
                moments(nc, dve, chain, stats, mean[0:TT, :], yvar[0:TT, :], ytmp[0:TT, :])
                dve.sem_inc(s["var_ready"], 1)
                dve.wait_ge(s["root_ready"], 1)
                chain.link(nc.vector.reciprocal(rstd[0:TT, :], ytmp[0:TT, :]))
                refine_rsqrt(nc, chain, rstd[0:TT, :], yvar[0:TT, :], ytmp[0:TT, :])
                dve.sem_inc(s["z_free"], 2)
                before += NTILES + chain.n
                with dve.Fori(0, B // 2) as i:
                    chain = Chain(dve, s["dve_chain"], before + 2 * (1 + 2 * NT) * i)
                    for u in range(2):
                        rows = h[0:TT, bass.ds((2 * i + u) * NT, NT), :]
                        chain.link(nc.vector.tensor_tensor(rows, rows, bwo[0:TT, :].unsqueeze(1).broadcast_to([TT, NT, D]), ALU.add))
                        dve.wait_ge(s["z_psum"], 2 * i + (u + 1))
                        dve.sem_inc(s["o2_free"], 1)
                        for t in range(NT):
                            col = (2 * i + u) * NT + t
                            row = h[0:TT, bass.ds(col, 1), :].rearrange("p o d -> p (o d)")
                            chain.add(nc.vector.scalar_tensor_tensor(
                                out=row, in0=psum[2 * u + t // 3][0:TT, (t % 3) * D:(t % 3 + 1) * D],
                                scalar=rstd[0:TT, bass.ds(col, 1)], in1=row, op0=ALU.mult, op1=ALU.add))
                        chain.settle()
                        dve.sem_inc(s["z_free"], 1)
                        for t in range(NT):
                            chain.add(nc.vector.bn_stats(stats[0:TT, bass.ds((2 * i + u) * NT + t, 1), :],
                                                         h[0:TT, bass.ds((2 * i + u) * NT + t, 1), :]))
                        chain.settle()
                    assert chain.n == 2 * (1 + 2 * NT)


def load_weights(sp, io, weights, e, u):
    sp.dma_start(weights["w1"][:, u, :], io["moe1_w1"][bass.ds(e, 1), :, :].rearrange("o p f -> p (o f)")
                 ).then_inc(weights["got"][u], 16)
    sp.dma_start(weights["w2"][:, u], io["moe1_w2"][bass.ds(e, 1), :, :].rearrange("o (p j) d -> p (o j) d", j=FCH)
                 ).then_inc(weights["got"][u], 16)


def route(nc, io, h, mean, rstd, weights, slots_dram, psum, ident, ones):
    GT = 16
    NGROUPS = NTILES // GT
    QUAD = 4
    SCORE_BANKS = (2, 7)
    with Memory(nc, "route") as m:
        w_hash = m.sbuf("w_hash", [128, ACTIVE])
        buckets = m.sbuf("buckets", [128, NEXP])
        earlier = m.sbuf("earlier", [128, 128])
        earlier16 = m.sbuf("earlier16", [128, 128], BF16)
        ones16 = m.sbuf("ones16", [128, 128], BF16)
        rows = m.sbuf("rows", [128, ACTIVE, NTILES, ROW])
        numbers = m.sbuf("numbers", [128, ACTIVE, NTILES])
        slot_in = m.sbuf("slot_in", [128, ACTIVE, NTILES], I32)
        xT = m.sbuf("xT", [128, 2, QUAD, TT])
        score = m.sbuf("score", [128, NTILES, ACTIVE])
        whole = m.sbuf("whole", [128, NTILES, ACTIVE], I32)
        floor = m.sbuf("floor", [128, NTILES, ACTIVE])
        above = m.sbuf("above", [128, NTILES, ACTIVE])
        expert = m.sbuf("expert", [128, NTILES, ACTIVE])
        hot = m.sbuf("hot", [128, ACTIVE, NTILES, NEXP], BF16)
        both = m.sbuf("both", [128, NTILES, NEXP], BF16)
        prior = m.sbuf("prior", [128, NTILES, NEXP], BF16)
        product = m.sbuf("product", [128, ACTIVE, GT, NEXP])
        place = m.sbuf("place", [128, ACTIVE, NTILES])
        same = m.sbuf("same", [128, NTILES])
        full = m.sbuf("full", [128, ACTIVE, NTILES])
        slot = m.sbuf("slot", [128, ACTIVE, NTILES])
        names = "loaded chain x_ready xT_psum xT_ready score_psum prior_ready rank_psum slots_ready copied numbered rows_numbered sent"
        s = {n: m.sem(n) for n in names.split()}
        per_bank = 512 // NEXP
        BIG = float(2 * NEXP * SLOTS)

        with nc.Block() as block:
            @block.sync
            def _(sp):
                sp.dma_start(w_hash[:], io["w_hash_T"]).then_inc(s["loaded"], 16)
                sp.dma_start(buckets[:], io["buckets"].partition_broadcast(128)).then_inc(s["loaded"], 16)
                sp.dma_start(earlier[:], io["earlier"]).then_inc(s["loaded"], 16)
                sp.dma_start(numbers[0:TT], io["numbers"]).then_inc(s["numbered"], 16)
                for u in range(EXPERTS_AHEAD):
                    load_weights(sp, io, weights, u, u)
                sp.dma_start(weights["b1"][:], io["moe1_b1"]).then_inc(weights["biases"], 16)
                sp.dma_start(weights["b2"][:], io["moe1_b2"].partition_broadcast(128)).then_inc(weights["biases"], 16)

            @block.gpsimd
            def _(pool):
                pool.wait_ge(s["numbered"], 16)
                nc.gpsimd.tensor_copy(rows[0:TT, :, :, D], numbers[0:TT]).then_inc(s["rows_numbered"], 1)
                pool.wait_ge(s["rows_numbered"], 1)
                for g in range(NGROUPS):
                    pool.wait_ge(s["copied"], GT // QUAD * (g + 1))
                    pool.wait_ge(s["slots_ready"], g + 1)
                    for t in range(GT * g, GT * (g + 1)):
                        for a in range(ACTIVE):
                            nc.gpsimd.indirect_dma_start(
                                slots_dram, bass.IndirectOffsetOnAxis(slot_in[0:TT, a, t:t + 1], 0), rows[0:TT, a, t, :],
                                None, bounds_check=NEXP * SLOTS - 1, oob_is_err=False).then_inc(s["sent"], 16)
                pool.wait_ge(s["sent"], 16 * NTILES * ACTIVE)

            @block.tensor
            def _(pe):
                pe.wait_ge(s["loaded"], 48)

                def scores(q):
                    pe.wait_ge(s["xT_ready"], q + 1)
                    for t in range(QUAD):
                        tile = QUAD * q + t
                        mm = nc.tensor.matmul(psum[SCORE_BANKS[tile // GT % 2]][0:TT, ACTIVE * tile:ACTIVE * (tile + 1)],
                                              xT[:, q % 2, t, :], w_hash[:], start=True, stop=True)
                    mm.then_inc(s["score_psum"], 1)

                def turn(q):
                    pe.wait_ge(s["x_ready"], q + 1)
                    if q >= 2:
                        pe.wait_ge(s["xT_ready"], q - 1)
                    for t in range(QUAD):
                        mm = nc.tensor.transpose(psum[q % 2][:, t * TT:(t + 1) * TT], rows[0:TT, 0, QUAD * q + t, 0:D],
                                                 ident[0:TT, 0:TT])
                    mm.then_inc(s["xT_psum"], 1)

                def ranks(g):
                    pe.wait_ge(s["prior_ready"], g + 1)
                    for k in range(GT // per_bank):
                        out = psum[3 + 2 * (g % 2) + k][0:TT, :].rearrange("p (t e) -> p t e", e=NEXP)
                        tiles = slice(g * GT + k * per_bank, g * GT + (k + 1) * per_bank)
                        nc.tensor.matmul(out, earlier16[0:TT, 0:TT], both[0:TT, tiles, :], start=True, stop=False)
                        mm = nc.tensor.matmul(out, ones16[0:TT, 0:TT], prior[0:TT, tiles, :], start=False, stop=True)
                        mm.then_inc(s["rank_psum"], 1)

                quads = NTILES // QUAD
                turn(0)
                for q in range(quads):
                    if q + 1 < quads:
                        turn(q + 1)
                    scores(q)
                    if q == 2 * GT // QUAD - 1:
                        ranks(0)
                for g in range(1, NGROUPS):
                    ranks(g)

            @block.scalar
            def _(act):
                for q in range(NTILES // QUAD):
                    act.wait_ge(s["xT_psum"], q + 1)
                    if q >= 2:
                        act.wait_ge(s["score_psum"], q - 1)
                    nc.scalar.activation(xT[:, q % 2, :, :].rearrange("p t k -> p (t k)"),
                                         psum[q % 2][:, 0:QUAD * TT], ACT.Identity).then_inc(s["xT_ready"], 1)
                    tiles = slice(QUAD * q, QUAD * (q + 1))
                    nc.scalar.activation(rows[0:TT, 1, tiles, 0:D], rows[0:TT, 0, tiles, 0:D], ACT.Identity
                                         ).then_inc(s["copied"], 1)

            @block.vector
            def _(dve):
                chain = Chain(dve, s["chain"])
                for q in range(NTILES // QUAD):
                    for col in range(QUAD * q, QUAD * (q + 1)):
                        chain.add(nc.vector.tensor_scalar(rows[0:TT, 0, col, 0:D], h[0:TT, col, :], mean[0:TT, col:col + 1],
                                                          rstd[0:TT, col:col + 1], ALU.subtract, ALU.mult))
                    chain.settle()
                    dve.sem_inc(s["x_ready"], 1)
                dve.wait_ge(s["loaded"], 48)
                chain.add(nc.vector.tensor_copy(earlier16[:], earlier[:]))
                chain.add(nc.vector.tensor_copy(ones16[:], ones[:]))
                chain.link(nc.vector.memset(prior[0:TT, 0, :], 0.0))

                def places(g):
                    tiles = slice(GT * g, GT * (g + 1))
                    dve.wait_ge(s["score_psum"], GT // QUAD * (g + 1))
                    chain.link(nc.vector.tensor_scalar(
                        score[0:TT, tiles], psum[SCORE_BANKS[g % 2]][0:TT, GT * g * ACTIVE:GT * (g + 1) * ACTIVE].rearrange(
                            "p (t a) -> p t a", a=ACTIVE), BUCKET_SCALE, None, ALU.mult))
                    chain.link(nc.vector.tensor_copy(whole[0:TT, tiles], score[0:TT, tiles]))
                    chain.link(nc.vector.tensor_copy(floor[0:TT, tiles], whole[0:TT, tiles]))
                    chain.link(nc.vector.tensor_tensor(above[0:TT, tiles], floor[0:TT, tiles], score[0:TT, tiles], ALU.is_gt))
                    chain.link(nc.vector.tensor_tensor(floor[0:TT, tiles], floor[0:TT, tiles], above[0:TT, tiles], ALU.subtract))
                    chain.link(nc.vector.tensor_copy(whole[0:TT, tiles], floor[0:TT, tiles]))
                    chain.link(nc.vector.tensor_single_scalar(whole[0:TT, tiles], whole[0:TT, tiles], NEXP - 1, ALU.bitwise_and))
                    chain.link(nc.vector.tensor_copy(expert[0:TT, tiles], whole[0:TT, tiles]))
                    for a in range(ACTIVE):
                        chain.add(nc.vector.tensor_tensor(
                            hot[0:TT, a, tiles], expert[0:TT, tiles, a:a + 1].broadcast_to([TT, GT, NEXP]),
                            buckets[0:TT, :].unsqueeze(1).broadcast_to([TT, GT, NEXP]), ALU.is_equal))
                    chain.settle()
                    chain.link(nc.vector.tensor_tensor(both[0:TT, tiles], hot[0:TT, 0, tiles], hot[0:TT, 1, tiles], ALU.add))
                    for t in range(max(GT * g, 1), GT * (g + 1)):
                        chain.link(nc.vector.tensor_tensor(prior[0:TT, t, :], prior[0:TT, t - 1, :], both[0:TT, t - 1, :], ALU.add))
                    dve.sem_inc(s["prior_ready"], 1)
                    chain.link(nc.vector.tensor_tensor(same[0:TT, tiles], expert[0:TT, tiles, 0], expert[0:TT, tiles, 1], ALU.is_equal))
                    dve.wait_ge(s["rank_psum"], GT // per_bank * (g + 1))
                    for a in range(ACTIVE):
                        for k in range(GT // per_bank):
                            part = slice(GT * g + k * per_bank, GT * g + (k + 1) * per_bank)
                            chain.add(nc.vector.tensor_tensor(
                                product[0:TT, a, k * per_bank:(k + 1) * per_bank, :],
                                psum[3 + 2 * (g % 2) + k][0:TT, :].rearrange("p (t e) -> p t e", e=NEXP),
                                hot[0:TT, a, part, :], ALU.mult))
                    chain.settle()
                    for a in range(ACTIVE):
                        chain.add(nc.vector.tensor_reduce(place[0:TT, a, tiles], product[0:TT, a], AX.X, ALU.add))
                    chain.settle()
                    chain.link(nc.vector.tensor_tensor(place[0:TT, 1, tiles], place[0:TT, 1, tiles], same[0:TT, tiles], ALU.add))
                    chain.link(nc.vector.tensor_scalar(full[0:TT, :, tiles], place[0:TT, :, tiles], float(CAP), None, ALU.is_ge))
                    for a in range(ACTIVE):
                        chain.add(nc.vector.scalar_tensor_tensor(
                            out=slot[0:TT, a, tiles], in0=expert[0:TT, tiles, a], scalar=float(SLOTS),
                            in1=place[0:TT, a, tiles], op0=ALU.mult, op1=ALU.add))
                    chain.settle()
                    chain.link(nc.vector.scalar_tensor_tensor(
                        out=place[0:TT, :, tiles], in0=full[0:TT, :, tiles], scalar=BIG, in1=slot[0:TT, :, tiles],
                        op0=ALU.mult, op1=ALU.add))
                    chain.link(nc.vector.tensor_copy(slot_in[0:TT, :, tiles], place[0:TT, :, tiles]))
                    dve.sem_inc(s["slots_ready"], 1)

                for g in range(NGROUPS):
                    places(g)


def experts(nc, io, weights, slots_dram, pairs_dram, psum, ident):
    U = EXPERTS_AHEAD
    with Memory(nc, "experts") as m:
        w1, w2, b1, b2 = (weights[n] for n in ("w1", "w2", "b1", "b2"))
        got, biases = weights["got"], weights["biases"]
        x = m.sbuf("x", [128, U, 2, ROW])
        xT = m.sbuf("xT", [128, 2, SLOTS])
        inner = m.sbuf("inner", [128, 2, FCH, SLOTS])
        y = m.sbuf("y", [128, U, 2, D])
        empty = m.sbuf("empty", [128, U, 2])
        number = m.sbuf("number", [128, U, 2])
        index = m.sbuf("index", [128, U, 2], I32)
        put = [m.sem(f"put_{u}") for u in range(U)]
        names = "turned_psum xT_ready inner_psum inner_ready y_psum y_ready y_free number_chain gate"
        s = {n: m.sem(n) for n in names.split()}
        ROUNDS = NEXP // U
        later = lambda i, u, n: (i + (u + n) // U, (u + n) % U)
        rows = lambda dram, e: dram[bass.ds(e * SLOTS, SLOTS), :].rearrange("(s p) d -> p s d", p=HP)

        with nc.Block() as block:
            @block.sync
            def _(sp):
                def load_x(e, u):
                    sp.dma_start(x[0:HP, u], rows(slots_dram, e)).then_inc(got[u], 16)

                for u in range(U):
                    load_x(u, u)
                with sp.Fori(0, ROUNDS - 1) as i:
                    for u in range(U):
                        sp.wait_ge(s["y_psum"], U * i + (u + 1) + 2)
                        load_weights(sp, io, weights, U * (i + 1) + u, u)
                        load_x(U * (i + 1) + u, u)

            @block.gpsimd
            def _(pool):
                def stored(i, u):
                    pool.wait_ge(put[u], 32 * i + 32)
                    pool.sem_inc(s["y_free"], 1)

                def body(i, first):
                    for u in range(U):
                        pass_gate(pool, s["y_ready"], U * i + (u + 1) + 2, s["gate"])
                        for k in range(2):
                            nc.gpsimd.indirect_dma_start(
                                pairs_dram, bass.IndirectOffsetOnAxis(index[0:HP, u, k:k + 1], 0), y[0:HP, u, k, :], None,
                                bounds_check=B * L * ACTIVE - 1, oob_is_err=False).then_inc(put[u], 16)
                        if u > 0:
                            stored(i, u - 1)
                        elif not first:
                            stored(i - 1, U - 1)
                body(0, True)
                with pool.Fori(1, ROUNDS) as i:
                    body(i, False)
                stored(ROUNDS - 1, U - 1)

            @block.tensor
            def _(pe):
                def turn(i, u):
                    e = U * i + u
                    pe.wait_ge(got[u], 48 * i + 48)
                    pe.wait_ge(s["xT_ready"], e + 1)
                    for k in range(2):
                        mm = nc.tensor.transpose(psum[4 + u % 2][:, k * HP:(k + 1) * HP], x[0:HP, u, k, 0:D],
                                                 ident[0:HP, 0:HP])
                    mm.then_inc(s["turned_psum"], 1)

                def first(i, u):
                    e = U * i + u
                    pe.wait_ge(s["xT_ready"], e + 1 + 2)
                    for j in range(FCH):
                        pe.wait_ge(s["inner_ready"], FCH * e + (j + 1))
                        nc.tensor.matmul(psum[j][:, 0:SLOTS], w1[:, u, :].rearrange("p (k j) -> p k j", j=FCH)[:, :, j],
                                         xT[:, u % 2, :], start=True, stop=True).then_inc(s["inner_psum"], 1)

                def second(i, u):
                    e = U * i + u
                    pe.wait_ge(s["y_ready"], e + 1)
                    for k in range(2):
                        for j in range(FCH):
                            pe.wait_ge(s["inner_ready"], FCH * e + (j + 1) + FCH)
                            mm = nc.tensor.matmul(psum[6 + u % 2][0:HP, k * D:(k + 1) * D],
                                                  inner[:, u % 2, j, k * HP:(k + 1) * HP], w2[:, u, j, :],
                                                  start=(j == 0), stop=(j == FCH - 1))
                    mm.then_inc(s["y_psum"], 1)

                turn(0, 0)
                first(0, 0)
                turn(0, 1)
                with pe.Fori(0, ROUNDS - 1) as i:
                    for u in range(U):
                        first(*later(i, u, 1))
                        turn(*later(i, u, 2))
                        second(i, u)
                for u in range(U):
                    if u + 1 < U:
                        first(ROUNDS - 1, u + 1)
                    if u + 2 < U:
                        turn(ROUNDS - 1, u + 2)
                    second(ROUNDS - 1, u)

            @block.scalar
            def _(act):
                act.sem_inc(s["inner_ready"], FCH)
                act.wait_ge(biases, 32)
                with act.Fori(0, ROUNDS) as i:
                    for u in range(U):
                        e = U * i + u
                        act.wait_ge(s["y_psum"], e + 1)
                        for j in range(FCH):
                            act.wait_ge(s["inner_psum"], FCH * e + (j + 1) + 2 * FCH)
                            nc.scalar.activation(inner[:, u % 2, j, :], psum[j][:, 0:SLOTS], ACT.Gelu,
                                                 bias=b1[:, bass.ds(e, 1), j:j + 1].rearrange("p o j -> p (o j)")
                                                 ).then_inc(s["inner_ready"], 1)

            @block.vector
            def _(dve):
                dve.sem_inc(s["xT_ready"], 2)
                dve.sem_inc(s["y_ready"], 2)
                dve.sem_inc(s["inner_psum"], 2 * FCH)
                dve.sem_inc(s["y_psum"], 2)
                dve.sem_inc(s["y_free"], U)

                def turned(i, u):
                    e = U * i + u
                    chain = Chain(dve, s["number_chain"], 3 * e)
                    dve.wait_ge(got[u], 48 * i + 48)
                    dve.wait_ge(s["y_free"], e + 1)
                    given = x[0:HP, u, :, D]
                    chain.link(nc.vector.tensor_scalar(empty[0:HP, u, :], given, 0.0, float(2 * B * L * ACTIVE),
                                                       ALU.is_equal, ALU.mult))
                    chain.link(nc.vector.scalar_tensor_tensor(out=number[0:HP, u, :], in0=given, scalar=-1.0,
                                                              in1=empty[0:HP, u, :], op0=ALU.add, op1=ALU.add))
                    chain.link(nc.vector.tensor_copy(index[0:HP, u, :], number[0:HP, u, :]))
                    dve.wait_ge(s["turned_psum"], e + 1)
                    dve.wait_ge(s["inner_psum"], FCH * (e + 1))
                    nc.vector.tensor_copy(xT[:, u % 2, :], psum[4 + u % 2][:, 0:SLOTS]).then_inc(s["xT_ready"], 1)

                def biased(i, u):
                    e = U * i + u
                    if u == 0:
                        dve.wait_ge(biases, 32)
                    dve.wait_ge(s["y_psum"], e + 1 + 2)
                    dve.wait_ge(s["y_free"], e + 1)
                    nc.vector.tensor_tensor(
                        y[0:HP, u], psum[6 + u % 2][0:HP, 0:2 * D].rearrange("p (k d) -> p k d", d=D),
                        b2[0:HP, bass.ds(e, 1), :].broadcast_to([HP, 2, D]), ALU.add).then_inc(s["y_ready"], 1)

                turned(0, 0)
                turned(0, 1)
                with dve.Fori(0, ROUNDS - 1) as i:
                    for u in range(U):
                        turned(*later(i, u, 2))
                        biased(i, u)
                for u in range(U):
                    if u + 2 < U:
                        turned(ROUNDS - 1, u + 2)
                    biased(ROUNDS - 1, u)


def combine(nc, h, pairs_dram, out):
    with Memory(nc, "combine") as m:
        y = m.sbuf("y", [128, B, NT, ACTIVE, D])
        got = [m.sem(f"got_{b}") for b in range(B)]
        done, chain_sem, stored = m.sem("done"), m.sem("chain"), m.sem("stored")
        pairs = pairs_dram.rearrange("(b t p a) d -> b p t (a d)", t=NT, p=TT, a=ACTIVE)
        out_tiles = out.rearrange("b (t p) d -> b p t d", p=TT)
        with nc.Block() as block:
            @block.scalar
            def _(act):
                for b in range(B):
                    act.dma_start(y[0:TT, b].rearrange("p t a d -> p t (a d)"), pairs[b]).then_inc(got[b], 16)

            @block.vector
            def _(dve):
                chain = Chain(dve, chain_sem)
                for b in range(B):
                    dve.wait_ge(got[b], 16)
                    rows = h[0:TT, b * NT:(b + 1) * NT, :]
                    for a in range(ACTIVE):
                        chain.link(nc.vector.scalar_tensor_tensor(
                            out=rows, in0=y[0:TT, b, :, a, :], scalar=1.0 / ACTIVE, in1=rows, op0=ALU.mult, op1=ALU.add))
                    dve.sem_inc(done, 1)

            @block.sync
            def _(sp):
                for b in range(B):
                    sp.wait_ge(done, b + 1)
                    sp.dma_start(out_tiles[b], h[0:TT, b * NT:(b + 1) * NT, :]).then_inc(stored, 16)
                sp.wait_ge(stored, 16 * B)


def tower(nc, io, out):
    pieces_dram = nc.dram_tensor("head_pieces", (B, 2 * PIECES, D, L), BF16).ap()
    k_rows_dram = nc.dram_tensor("key_rows", (B, L, D), FP32).ap()
    coef_dram = nc.dram_tensor("chunk_coefficients", (B, 128, NCH, NCOEF), FP32).ap()
    slots_dram = nc.dram_tensor("slot_rows", (NEXP * SLOTS, ROW), FP32).ap()
    pairs_dram = nc.dram_tensor("result_rows", (B * L * ACTIVE, D), FP32).ap()
    with Memory(nc, "tower") as m:
        h = m.sbuf("h", [128, NTILES, D])
        stats = m.sbuf("stats", [128, NTILES, 6])
        mean = m.sbuf("mean", [128, NTILES])
        rstd = m.sbuf("rstd", [128, NTILES])
        ident = m.sbuf("ident", [128, 128])
        ones = m.sbuf("ones", [128, 128])
        banks = m.stack.enter_context(nc.psum_tensor("tower_banks", [128, 8, 512], FP32))
        psum = [banks[:, i, :] for i in range(8)]
        block_ones = m.sbuf("block_ones", [128, 128])
        block_sum = m.sbuf("block_sum", [128, 128])
        constants = [(ident, io["ident"]), (ones, io["ones"]), (block_ones, io["block_ones"]), (block_sum, io["block_sum"])]

        convolution(nc, io, h, stats, constants, psum, ident)

        layernorm_scalars(nc, "ln1", stats, mean, rstd)
        with Memory(nc, "attention_values") as a:
            n3 = a.sbuf("n3", [128, NTILES, D])
            dmax = a.sbuf("dmax", [128, B])
            head_vectors(nc, io, h, mean, rstd, n3, dmax, pieces_dram, psum, ident, block_ones)
            attention(nc, io, h, stats, n3, dmax, pieces_dram, banks, psum, ident, ones)
        layernorm_scalars(nc, "ln2", stats, mean, rstd)
        expert_of_batch(nc, io, h, stats, mean, rstd, slots_dram, pairs_dram, psum, ident, ones)

        layernorm_scalars(nc, "ln3", stats, mean, rstd)
        with Memory(nc, "delta_values") as a:
            kq_all = a.sbuf("kq_all", [128, NCH, B, 2, C])
            v_all = a.sbuf("v_all", [128, NCH, B, C])
            with Memory(nc, "delta_rates") as r:
                beta = r.sbuf("beta", [128, B, L])
                delta_projections(nc, io, h, mean, rstd, kq_all, v_all, beta, k_rows_dram, psum, ident)
                triangular_coefficients(nc, kq_all, beta, coef_dram, psum, block_sum)
            u_all = a.sbuf("u_all", [128, NCH, B, C])
            o_all = a.sbuf("o_all", [128, NCH, B, C])
            delta_rule(nc, io, kq_all, v_all, u_all, o_all, k_rows_dram, coef_dram, banks, psum)
            within_chunks(nc, kq_all, u_all, o_all, psum, block_sum)
            delta_output(nc, io, h, stats, mean, rstd, o_all, psum, ident, ones)

        layernorm_scalars(nc, "ln4", stats, mean, rstd)
        with Memory(nc, "routing") as a:
            weights = {"w1": a.sbuf("w1", [128, EXPERTS_AHEAD, DFF]), "w2": a.sbuf("w2", [128, EXPERTS_AHEAD, FCH, D]),
                       "b1": a.sbuf("b1", [128, NEXP, FCH]), "b2": a.sbuf("b2", [128, NEXP, D]),
                       "got": [a.sem(f"got_{u}") for u in range(EXPERTS_AHEAD)], "biases": a.sem("biases")}
            route(nc, io, h, mean, rstd, weights, slots_dram, psum, ident, ones)
            experts(nc, io, weights, slots_dram, pairs_dram, psum, ident)
        combine(nc, h, pairs_dram, out)


def kernel(**inputs):
    import concourse.bacc as bacc
    from concourse.bass_utils import run_bass_kernel_spmd

    given = {name: np.asarray(a) for name, a in inputs.items()}
    f32 = np.float32

    def head_rows(w):
        return np.repeat(w.reshape(G, 4, 1, F, D), 2, axis=2).reshape(G, 128, D).transpose(1, 0, 2)

    taps = given["L0_tok_weight"].transpose(1, 2, 0)
    partition = np.arange(128)
    arrays = {
        "x": given["x"], "conv_w_even": taps[:, 0::2], "conv_w_odd": taps[:, 1::2],
        "conv_b": given["L0_tok_bias"].reshape(D, 1),
        "w_qkv_T": given["L0_attn_qkv_w"].T, "w_delta_T": given["L0_attn_delta_w"].T,
        "g12_cols": np.stack([np.tile(given["L0_attn_g1"], H), np.tile(given["L0_attn_g2"], H)], 1),
        "g3_row": np.tile(given["L0_attn_g3"], H),
        "w_qkv_rows": head_rows(given["L0_attn_qkv_w"]), "w_delta_rows": head_rows(given["L0_attn_delta_w"]),
        "moe0_wg": given["L0_ffn_Wg"], "moe0_bg": given["L0_ffn_bg"].reshape(1, -1),
        "moe0_we": given["L0_ffn_We"], "moe0_be": given["L0_ffn_be"],
        "wq": given["L1_attn_Wq"], "wk": given["L1_attn_Wk"], "wv": given["L1_attn_Wv"],
        "wb": given["L1_attn_Wb"], "wo": given["L1_attn_Wo"],
        "ln_cols": np.stack([given["L1_attn_ln_g"], given["L1_attn_ln_b"]], 1),
        "w_hash_T": given["L1_ffn_W_hash"][:ACTIVE].T,
        "moe1_w1": given["L1_ffn_W1"], "moe1_w2": given["L1_ffn_W2"],
        "moe1_b1": given["L1_ffn_b1"].reshape(NEXP, D, FCH).transpose(1, 0, 2), "moe1_b2": given["L1_ffn_b2"],
        "ident": np.eye(128, dtype=f32), "ones": np.ones((128, 128), f32),
        "block_ones": np.kron(np.eye(H), np.full((F, F), 1.0 / F)).astype(f32),
        "block_sum": np.kron(np.eye(H), np.ones((F, F))).astype(f32),
        "head_start": (partition[:, None] == F * np.arange(H)).astype(f32),
        "countdown": (16 - np.arange(16)).astype(f32).reshape(1, 16),
        "pair_masks": -np.stack([partition // F % 2 == 0, partition // F % 2 == 1], 1).astype(f32),
        "numbers": (ACTIVE * (TT * np.arange(NTILES) + np.arange(TT)[:, None])[:, None, :]
                    + np.arange(ACTIVE)[None, :, None] + 1).astype(f32),
        "buckets": np.arange(NEXP).astype(f32),
        "earlier": np.triu(np.ones((128, 128), f32), 1),
    }
    arrays = {name: np.ascontiguousarray(a) for name, a in arrays.items()}
    nc = bacc.Bacc("TRN2", target_bir_lowering=False, num_devices=1)
    io = {name: nc.dram_tensor(name, a.shape, mybir.dt.from_np(a.dtype), kind="ExternalInput").ap()
          for name, a in arrays.items()}
    out = nc.dram_tensor("out", (B, L, D), FP32, kind="ExternalOutput").ap()
    tower(nc, io, out)
    return run_bass_kernel_spmd(nc, [arrays], core_ids=[0]).results[0]["out"]
```
